# Optimizing a Trainium2 kernel written in Bass

```python
import numpy as np
import jax
import jax.numpy as jnp

def _softmax(x, axis=-1):
    return jax.nn.softmax(x, axis=axis)

def _gelu(x):
    return jax.nn.gelu(x, approximate=True)

def _silu(x):
    return jax.nn.silu(x)

def _sigmoid(x):
    return jax.nn.sigmoid(x)

def _layernorm(x, axis=-1, eps=1e-05):
    m = jnp.mean(x, axis=axis, keepdims=True)
    v = jnp.var(x, axis=axis, keepdims=True)
    return (x - m) / jnp.sqrt(v + eps)

def _scatter_add(tgt, idx, src, axis=0):
    return tgt.at[idx].add(src)

def _segment_sum(src, seg, n):
    return jax.ops.segment_sum(src, seg, n)
kernel_name = 'mk_vit_tower_cls_d1_tok_img768_r4_6757f8'

def setup_inputs(seed: int=0):
    np.random.seed(seed)
    _w = jnp.asarray

    def _rec_inputs():
        import jax
        import jax.numpy as jnp
        _rk = jax.random.key(seed)
        x = -0.000348323 + 0.999952 * jax.random.normal(jax.random.fold_in(_rk, 1), (64, 3, 96, 96), jnp.float32)
        cls_tok = 0.02 * jax.random.normal(jax.random.fold_in(_rk, 5), (1, 1, 192), jnp.float32)
        return (x, cls_tok)
    x, cls_tok = _rec_inputs()

    def _L0_tok_setup():
        import jax, jax.numpy as jnp
        import numpy as np
        PATCH = 16
        EMBED = 192
        IMG = 96
        CH = 3
        NP_ = (IMG // PATCH) ** 2
        key = jax.random.key(seed)
        k1, k2, k3 = jax.random.split(key, 3)
        x = jax.random.normal(k1, (32, CH, IMG, IMG), dtype=jnp.float32)
        in_feat = PATCH * PATCH * CH
        lim = 1.0 / np.sqrt(in_feat)
        W = jax.random.uniform(k2, (EMBED, in_feat), dtype=jnp.float32, minval=-lim, maxval=lim)
        b = jax.random.uniform(k3, (EMBED,), dtype=jnp.float32, minval=-lim, maxval=lim)
        pos = jnp.zeros((1, NP_, EMBED), dtype=jnp.float32)
        return {'x': x, 'W': W, 'b': b, 'pos': pos}
    _L0_tok_all = _L0_tok_setup()
    _L0_tok_in = {k: v for k, v in _L0_tok_all.items() if k in ('W', 'b', 'pos')}
    del _L0_tok_all

    def _L0_attn_setup():
        import jax, jax.numpy as jnp
        import numpy as np
        B, T, D, H, K = (4, 256, 192, 12, 64)
        DMIX, DDEC = (32, 64)
        key = jax.random.key(seed)
        ks = jax.random.split(key, 24)

        def n(k, shape, s=1.0):
            return jax.random.normal(k, shape, dtype=jnp.float32) * s
        return {'x': n(ks[0], (B, T, D)), 'time_maa_x': n(ks[1], (1, 1, D), 0.1) + 0.5, 'time_maa_w': n(ks[2], (1, 1, D), 0.1) + 0.5, 'time_maa_k': n(ks[3], (1, 1, D), 0.1) + 0.5, 'time_maa_v': n(ks[4], (1, 1, D), 0.1) + 0.5, 'time_maa_r': n(ks[5], (1, 1, D), 0.1) + 0.5, 'time_maa_g': n(ks[6], (1, 1, D), 0.1) + 0.5, 'maa_w1': n(ks[7], (D, 5 * DMIX), 0.01), 'maa_w2': n(ks[8], (5, DMIX, D), 0.01), 'time_decay': jnp.linspace(-6.0, -1.0, D).reshape(1, 1, D).astype(jnp.float32), 'decay_w1': n(ks[9], (D, DDEC), 0.01), 'decay_w2': n(ks[10], (DDEC, D), 0.01), 'lucid_temp': jnp.ones((1, H, 1, 1), jnp.float32), 'Wr': n(ks[11], (D, D), 0.02), 'Wk': n(ks[12], (D, D), 0.02), 'Wv': n(ks[13], (D, D), 0.02), 'Wg': n(ks[14], (D, D), 0.02), 'Wo': n(ks[15], (D, D), 0.02), 'ln_w': jnp.ones((D,), jnp.float32), 'ln_b': jnp.zeros((D,), jnp.float32)}
    _L0_attn_all = _L0_attn_setup()
    _L0_attn_in = {k: v for k, v in _L0_attn_all.items() if k in ('time_maa_x', 'time_maa_w', 'time_maa_k', 'time_maa_v', 'time_maa_r', 'time_maa_g', 'maa_w1', 'maa_w2', 'time_decay', 'decay_w1', 'decay_w2', 'lucid_temp', 'Wr', 'Wk', 'Wv', 'Wg', 'Wo', 'ln_w', 'ln_b')}
    del _L0_attn_all

    def _L0_ffn_setup():
        import math
        import jax, jax.numpy as jnp
        import numpy as np
        EMBED_CHOICES = [96, 144, 192]
        RATIO_CHOICES = [2, 3, 4]
        E_MAX = 192
        H_MAX = 768

        def new_gelu(x):
            c = math.sqrt(2.0 / math.pi)
            return 0.5 * x * (1.0 + jnp.tanh(c * (x + 0.044715 * x * x * x)))

        def _mixed_coeffs(alpha_e, alpha_r):
            h_idx = jnp.arange(H_MAX)
            d_idx = jnp.arange(E_MAX)
            C0 = jnp.zeros((H_MAX, E_MAX), jnp.float32)
            c0b = jnp.zeros((H_MAX,), jnp.float32)
            C1 = jnp.zeros((E_MAX, H_MAX), jnp.float32)
            c1b = jnp.zeros((E_MAX,), jnp.float32)
            for i, e in enumerate(EMBED_CHOICES):
                m_in = (d_idx < e).astype(jnp.float32)
                for j, r in enumerate(RATIO_CHOICES):
                    a = alpha_e[i] * alpha_r[j]
                    m_out = (h_idx < r * e).astype(jnp.float32)
                    C0 = C0 + a * (m_out[:, None] * m_in[None, :])
                    c0b = c0b + a * m_out
                    C1 = C1 + a * (m_in[:, None] * m_out[None, :])
                    c1b = c1b + a * m_in
            return (C0, c0b, C1, c1b)
        key = jax.random.key(seed)
        ks = jax.random.split(key, 6)
        x = jax.random.normal(ks[0], (8, 512, E_MAX), jnp.float32)
        w_fc = jax.random.normal(ks[1], (H_MAX, E_MAX), jnp.float32) * 0.02
        b_fc = jnp.zeros((H_MAX,), jnp.float32)
        w_proj = jax.random.normal(ks[2], (E_MAX, H_MAX), jnp.float32) * 0.02
        b_proj = jnp.zeros((E_MAX,), jnp.float32)
        alpha_e = jax.nn.softmax(jax.random.normal(ks[3], (3,), jnp.float32))
        alpha_r = jax.nn.softmax(jax.random.normal(ks[4], (3,), jnp.float32))
        return {'x': x, 'w_fc': w_fc, 'b_fc': b_fc, 'w_proj': w_proj, 'b_proj': b_proj, 'alpha_e': alpha_e, 'alpha_r': alpha_r}
    _L0_ffn_all = _L0_ffn_setup()
    _L0_ffn_in = {k: v for k, v in _L0_ffn_all.items() if k in ('w_fc', 'b_fc', 'w_proj', 'b_proj', 'alpha_e', 'alpha_r')}
    del _L0_ffn_all
    return {'x': x, 'cls_tok': cls_tok, 'L0_tok_W': _L0_tok_in['W'], 'L0_tok_b': _L0_tok_in['b'], 'L0_tok_pos': _L0_tok_in['pos'], 'L0_attn_time_maa_x': _L0_attn_in['time_maa_x'], 'L0_attn_time_maa_w': _L0_attn_in['time_maa_w'], 'L0_attn_time_maa_k': _L0_attn_in['time_maa_k'], 'L0_attn_time_maa_v': _L0_attn_in['time_maa_v'], 'L0_attn_time_maa_r': _L0_attn_in['time_maa_r'], 'L0_attn_time_maa_g': _L0_attn_in['time_maa_g'], 'L0_attn_maa_w1': _L0_attn_in['maa_w1'], 'L0_attn_maa_w2': _L0_attn_in['maa_w2'], 'L0_attn_time_decay': _L0_attn_in['time_decay'], 'L0_attn_decay_w1': _L0_attn_in['decay_w1'], 'L0_attn_decay_w2': _L0_attn_in['decay_w2'], 'L0_attn_lucid_temp': _L0_attn_in['lucid_temp'], 'L0_attn_Wr': _L0_attn_in['Wr'], 'L0_attn_Wk': _L0_attn_in['Wk'], 'L0_attn_Wv': _L0_attn_in['Wv'], 'L0_attn_Wg': _L0_attn_in['Wg'], 'L0_attn_Wo': _L0_attn_in['Wo'], 'L0_attn_ln_w': _L0_attn_in['ln_w'], 'L0_attn_ln_b': _L0_attn_in['ln_b'], 'L0_ffn_w_fc': _L0_ffn_in['w_fc'], 'L0_ffn_b_fc': _L0_ffn_in['b_fc'], 'L0_ffn_w_proj': _L0_ffn_in['w_proj'], 'L0_ffn_b_proj': _L0_ffn_in['b_proj'], 'L0_ffn_alpha_e': _L0_ffn_in['alpha_e'], 'L0_ffn_alpha_r': _L0_ffn_in['alpha_r']}

def reference(x, cls_tok, L0_tok_W, L0_tok_b, L0_tok_pos, L0_attn_time_maa_x, L0_attn_time_maa_w, L0_attn_time_maa_k, L0_attn_time_maa_v, L0_attn_time_maa_r, L0_attn_time_maa_g, L0_attn_maa_w1, L0_attn_maa_w2, L0_attn_time_decay, L0_attn_decay_w1, L0_attn_decay_w2, L0_attn_lucid_temp, L0_attn_Wr, L0_attn_Wk, L0_attn_Wv, L0_attn_Wg, L0_attn_Wo, L0_attn_ln_w, L0_attn_ln_b, L0_ffn_w_fc, L0_ffn_b_fc, L0_ffn_w_proj, L0_ffn_b_proj, L0_ffn_alpha_e, L0_ffn_alpha_r):
    import jax
    import jax.numpy as jnp

    def _L0_tok_ref(x, W, b, pos):
        import jax, jax.numpy as jnp
        import numpy as np
        PATCH = 16
        EMBED = 192
        IMG = 96
        CH = 3
        NP_ = (IMG // PATCH) ** 2
        B, C, H, Wd = x.shape
        hp, wp = (H // PATCH, Wd // PATCH)
        patches = x.reshape(B, C, hp, PATCH, wp, PATCH)
        patches = patches.transpose(0, 2, 4, 1, 3, 5).reshape(B, hp * wp, C * PATCH * PATCH)
        out = jnp.einsum('bnf,ef->bne', patches, W) + b + pos
        return out

    def _L0_attn_ref(x, time_maa_x, time_maa_w, time_maa_k, time_maa_v, time_maa_r, time_maa_g, maa_w1, maa_w2, time_decay, decay_w1, decay_w2, lucid_temp, Wr, Wk, Wv, Wg, Wo, ln_w, ln_b):
        import jax, jax.numpy as jnp
        import numpy as np
        B, T, D, H, K = (4, 256, 192, 12, 64)
        DMIX, DDEC = (32, 64)
        Bb, Tt, Dd = x.shape
        Hh = lucid_temp.shape[1]
        Kk = Dd // Hh
        left = jnp.pad(x[:, :-1], ((0, 0), (1, 0), (0, 0)))
        right = jnp.pad(x[:, 1:], ((0, 0), (0, 1), (0, 0)))
        dxprev = 0.5 * (left + right) - x
        xxx = x + dxprev * time_maa_x
        m = jnp.tanh(xxx @ maa_w1).reshape(Bb, Tt, 5, DMIX)
        mm = jnp.einsum('btcd,cde->cbte', m, maa_w2)
        mw, mk, mv, mr, mg = (mm[0], mm[1], mm[2], mm[3], mm[4])
        xw = x + dxprev * (time_maa_w + mw)
        xk = x + dxprev * (time_maa_k + mk)
        xv = x + dxprev * (time_maa_v + mv)
        xr = x + dxprev * (time_maa_r + mr)
        xg = x + dxprev * (time_maa_g + mg)
        r = xr @ Wr
        k = xk @ Wk
        v = xv @ Wv
        g = jax.nn.silu(xg @ Wg)
        w = time_decay + jnp.tanh(xw @ decay_w1) @ decay_w2

        def heads(t):
            return t.reshape(Bb, Tt, Hh, Kk).transpose(0, 2, 1, 3)
        r_h, k_h, v_h = (heads(r), heads(k), heads(v))
        w_h = -jnp.exp(heads(w))
        cs = jnp.cumsum(w_h, axis=2)
        cs_b = cs - w_h
        cs_f_s = jnp.clip(cs - cs[:, :, Tt // 2:Tt // 2 + 1, :], -60.0, 60.0)
        cs_b_s = jnp.clip(cs_b - cs_b[:, :, Tt // 2:Tt // 2 + 1, :], -60.0, 60.0)
        A_fwd = jnp.tril(jnp.einsum('bhtk,bhsk->bhts', r_h * jnp.exp(cs_f_s), k_h * jnp.exp(-cs_f_s)))
        A_bwd = jnp.triu(jnp.einsum('bhtk,bhsk->bhts', r_h * jnp.exp(-cs_b_s), k_h * jnp.exp(cs_b_s)), 1)
        A = A_fwd + A_bwd
        kn = k_h / jnp.maximum(jnp.linalg.norm(k_h, axis=-1, keepdims=True), 1e-12)
        gram = jnp.einsum('bhtk,bhsk->bhts', kn, kn)
        temp = jax.nn.softplus(lucid_temp)
        P = jnp.eye(Tt, dtype=jnp.float32) + jnp.exp(jnp.clip(temp * gram, -20.0, 20.0))
        Pv = jnp.linalg.solve(P, v_h)
        y = jnp.einsum('bhts,bhsk->bhtk', A, Pv)
        y = y.transpose(0, 2, 1, 3)
        eps = 1e-05 * 64.0
        mu = y.mean(axis=-1, keepdims=True)
        var = y.var(axis=-1, keepdims=True)
        yn = (y - mu) / jnp.sqrt(var + eps)
        yn = yn.reshape(Bb, Tt, Dd) * ln_w + ln_b
        return yn * g @ Wo

    def _L0_ffn_ref(x, w_fc, b_fc, w_proj, b_proj, alpha_e, alpha_r):
        import math
        import jax, jax.numpy as jnp
        import numpy as np
        EMBED_CHOICES = [96, 144, 192]
        RATIO_CHOICES = [2, 3, 4]
        E_MAX = 192
        H_MAX = 768

        def new_gelu(x):
            c = math.sqrt(2.0 / math.pi)
            return 0.5 * x * (1.0 + jnp.tanh(c * (x + 0.044715 * x * x * x)))

        def _mixed_coeffs(alpha_e, alpha_r):
            h_idx = jnp.arange(H_MAX)
            d_idx = jnp.arange(E_MAX)
            C0 = jnp.zeros((H_MAX, E_MAX), jnp.float32)
            c0b = jnp.zeros((H_MAX,), jnp.float32)
            C1 = jnp.zeros((E_MAX, H_MAX), jnp.float32)
            c1b = jnp.zeros((E_MAX,), jnp.float32)
            for i, e in enumerate(EMBED_CHOICES):
                m_in = (d_idx < e).astype(jnp.float32)
                for j, r in enumerate(RATIO_CHOICES):
                    a = alpha_e[i] * alpha_r[j]
                    m_out = (h_idx < r * e).astype(jnp.float32)
                    C0 = C0 + a * (m_out[:, None] * m_in[None, :])
                    c0b = c0b + a * m_out
                    C1 = C1 + a * (m_in[:, None] * m_out[None, :])
                    c1b = c1b + a * m_in
            return (C0, c0b, C1, c1b)
        C0, c0b, C1, c1b = _mixed_coeffs(alpha_e, alpha_r)
        W0 = w_fc * C0
        b0 = b_fc * c0b
        h = jnp.einsum('bte,he->bth', x, W0) + b0
        h = new_gelu(h)
        W1 = w_proj * C1
        b1 = b_proj * c1b
        out = jnp.einsum('bth,eh->bte', h, W1) + b1
        return out
    h = _L0_tok_ref(x, L0_tok_W, L0_tok_b, L0_tok_pos)
    h = jnp.concatenate([jnp.broadcast_to(cls_tok, (h.shape[0], 1, h.shape[2])), h], axis=1)
    h = h + _L0_attn_ref(_layernorm(h, axis=-1), L0_attn_time_maa_x, L0_attn_time_maa_w, L0_attn_time_maa_k, L0_attn_time_maa_v, L0_attn_time_maa_r, L0_attn_time_maa_g, L0_attn_maa_w1, L0_attn_maa_w2, L0_attn_time_decay, L0_attn_decay_w1, L0_attn_decay_w2, L0_attn_lucid_temp, L0_attn_Wr, L0_attn_Wk, L0_attn_Wv, L0_attn_Wg, L0_attn_Wo, L0_attn_ln_w, L0_attn_ln_b)
    h = h + _L0_ffn_ref(_layernorm(h, axis=-1), L0_ffn_w_fc, L0_ffn_b_fc, L0_ffn_w_proj, L0_ffn_b_proj, L0_ffn_alpha_e, L0_ffn_alpha_r)
    return h

_drawn_inputs = setup_inputs


def setup_inputs(seed=0):
    import zlib

    import numpy as np

    out = dict(_drawn_inputs(seed))
    spreads = {'L0_tok_pos': (0.0, 0.1),
     'L0_attn_lucid_temp': (1.0, 0.6),
     'L0_attn_ln_w': (1.0, 0.6),
     'L0_attn_ln_b': (0.0, 0.8),
     'L0_ffn_b_fc': (0.0, 0.1),
     'L0_ffn_b_proj': (0.0, 0.1)}
    factors = {'cls_tok': 3.682,
     'L0_attn_time_maa_x': 8.0,
     'L0_attn_time_maa_w': 200.0,
     'L0_attn_time_maa_k': 8.0,
     'L0_attn_time_maa_v': 8.0,
     'L0_attn_time_maa_r': 8.0,
     'L0_attn_time_maa_g': 8.0,
     'L0_attn_maa_w1': 8.0,
     'L0_attn_maa_w2': 8.0,
     'L0_attn_time_decay': 200.0,
     'L0_attn_decay_w1': 200.0,
     'L0_attn_decay_w2': 200.0,
     'L0_ffn_alpha_r': 2.76}
    for name, (base, spread) in spreads.items():
        noise = np.random.default_rng([zlib.crc32(name.encode()), seed]).standard_normal(out[name].shape)
        drawn = base * np.exp(spread * noise) if base else spread * noise
        out[name] = jnp.asarray(drawn.astype(out[name].dtype))
    for name, factor in factors.items():
        out[name] = (out[name] * factor).astype(out[name].dtype)
    return out
```

```python
from contextlib import ExitStack

import numpy as np

import concourse.bass as bass
from concourse import mybir
from concourse.alu_op_type import AluOpType as ALU

F32 = mybir.dt.float32
U32 = mybir.dt.uint32
ACT = mybir.ActivationFunctionType

B, CH, IMG, PATCH, D = 64, 3, 96, 16, 192
HP = IMG // PATCH
NPT = HP * HP
T = NPT + 1
MID = T // 2
H, K = 12, 16
HD = D // 2
FK = CH * PATCH * PATCH // 128
NB = 8
NC = B // NB
TC = NB * T
PC = NB * NPT
PP = NB // 2
TP = 64
Q = HD // 32
NMIX, MR = 5, 32
DDEC = 64
HT = H * T
NSYS = 128
NG = B // 2 * H // NSYS
GR = 2 * NSYS
W = T + K
FH = 4 * D
FC = FH // 128
LN_EPS = 1e-5
GN_EPS = 1e-5 * 64.0
EMBEDS, RATIOS = (96, 144, 192), (2, 3, 4)
NA = len(EMBEDS) * len(RATIOS)
MW, MK, MV, MRR, MG = range(5)
MIXES = (MW, MV, MG, MK, MRR)

V_TOKB, V_CLS, V_MAA, V_TD, V_LNW, V_LNB, V_PAR, V_POS = 0, 2, 4, 16, 18, 20, 22, 24
V_N = V_POS + 2 * NPT


def group_chunk(g):
    return -(-(NSYS * (g + 1)) // (H * PP)) - 1


def pieces(first, n):
    a = first % GR
    m = min(n, GR - a)
    return [(a, 0, m)] + ([(0, m, n - m)] if m < n else [])


def bands(m):
    n = 3 if m >= 24 else 2 if m >= 10 else 1
    cuts = [m * j // n for j in range(n + 1)]
    return list(zip(cuts[:-1], cuts[1:]))


class Ring:

    def __init__(self, slots):
        self.slots, self.tasks, self.index = slots, [], {}

    def add(self, key, read):
        self.index[key] = len(self.tasks)
        self.tasks.append(read)

    def slot(self, key):
        return self.index[key] % self.slots

    def made(self, key):
        return self.index[key] + 1

    def before(self, key):
        n = self.index[key] - self.slots
        return self.tasks[n] if n >= 0 else None


def vit_tower(nc, patches, chan, wtok, w1, w2a, w2b, dw1, dw2, wkvrg, wo, wfc, bfc, wproj, bproj, alphas,
              lucid, ident, blocks, tri, scanmask, din, hout, out):
    h_dram = nc.dram_tensor("h_spill", (NC, HD, 2 * TC), F32, kind="Internal").ap()
    gate_dram = nc.dram_tensor("gate_spill", (NC, HD, 2 * TC), F32, kind="Internal").ap()
    at_dram = nc.dram_tensor("at_spill", (NC, 2, T, PP * HT), F32, kind="Internal").ap()

    ctx = ExitStack()
    with ctx:
        def sem(name):
            return ctx.enter_context(nc.semaphore(name))

        def sb(name, shape, dt=F32, where=ctx):
            return where.enter_context(nc.sbuf_tensor(name, shape, dt))

        chan_s = sb("chan_s", [HD, V_N])
        wtok_s = sb("wtok_s", [128, FK, D])
        w1_s = sb("w1_s", [HD, 2, NMIX * MR])
        w2a_s = sb("w2a_s", [128, D])
        w2b_s = sb("w2b_s", [MR, D])
        dw1_s = sb("dw1_s", [HD, 2, DDEC])
        dw2_s = sb("dw2_s", [DDEC, D])
        wproj4_s = sb("wproj4_s", [HD, 4, 2, D])
        wo_s = sb("wo_s", [HD, 2, D])
        ident_s = sb("ident_s", [128, 128])
        blocks_s = sb("blocks_s", [HD, 2, HD])
        tri_s = sb("tri_s", [128, T], U32)
        scan_s = sb("scan_s", [HD, TC])
        lucid_s = sb("lucid_s", [NSYS, NG])
        temp = sb("temp", [NSYS, NG])
        tmp3 = sb("tmp3", [NSYS, 2, NG])
        eps_s = sb("eps_s", [128, 2])
        posb = sb("posb", [HD, 2, NPT])
        gram = sb("gram", [128, GR * T])
        vring = sb("vring", [128, GR * K])
        sysm = sb("sysm", [NSYS, 2, 2, T, W])
        nrm = sb("nrm", [NSYS, 2, T])
        rdiag = sb("rdiag", [NSYS, 2, 2, T])
        outer = sb("outer", [NSYS, 2880])
        outer_b = sb("outer_b", [NSYS, 2 * (T - 1) * K])

        gram_v = gram[:, :].rearrange("p (s t) -> p s t", t=T)
        v_v = vring[:, :].rearrange("p (s k) -> p s k", k=K)

        actx = ExitStack()

        def sa(name, shape, dt=F32):
            return sb(name, shape, dt, actx)
        pat = sa("pat", [128, FK, PC])
        hbuf = sa("hbuf", [HD, 2, TC])
        xc = sa("xc", [HD, 2, TC])
        rstd = sa("rstd", [HD, TC])
        xpad = sa("xpad", [HD, 2, 2, NB, T + 2])
        dx = sa("dx", [HD, 2, 2, TC])
        xxx = sa("xxx", [HD, 2, TC])
        sq = xxx
        m_a = sa("m_a", [128, TC])
        m_b = sa("m_b", [MR, TC])
        prod = sa("prod", [HD, 2, 2, TC])
        xs = sa("xs", [HD, 2, 2, TC])
        xv = sa("xv", [HD, 2, NB, TP])
        dect = sa("dect", [DDEC, TC])
        ew = sa("ew", [HD, 2, TC])
        cs = sa("cs", [HD, 2, TC])
        cb = sa("cb", [HD, 2, TC])
        ex = sa("ex", [HD, 2, 2, TC])
        kp = sa("kp", [HD, 2, TC + TP - T])
        kpar = sa("kpar", [HD, 2, 2, TC])
        rpar = sa("rpar", [HD, 2, 2, TC])
        ke = sa("ke", [HD, 2, 2, TC + TP - T])
        re = sa("re", [HD, 2, 2, 2, TC])
        th = sa("th", [HD, 2, TC])
        gate = th
        at = sa("at", [128, PP, HT])
        actx.close()

        cctx = ExitStack()

        def sc(name, shape, dt=F32):
            return sb(name, shape, dt, cctx)
        wfc_s = sc("wfc_s", [HD, 2, FH])
        wpr_s = sc("wpr_s", [128, FC, D])
        bfc_s = sc("bfc_s", [128, FC])
        bpr_s = sc("bpr_s", [1, D])
        alph_s = sc("alph_s", [NA, 2])
        aij = sc("aij", [NA, 1])
        din_s = sc("din_s", [NA, D])
        hout_s = sc("hout_s", [NA, FH])
        adin = sc("adin", [NA, D])
        ones_s = sc("ones_s", [1, 128])
        xpose = sc("xpose", [NSYS, K, 2, TP])
        pv = sc("pv", [128, NG, NSYS, K])
        atc = sc("atc", [128, PP, HT + TP - T])
        ysb = sc("ysb", [128, PP, D])
        yT = sc("yT", [HD, 2, TC])
        yc = sc("yc", [HD, 2, TC])
        sqc = sc("sqc", [HD, 2, TC])
        rsc = sc("rsc", [HD, 2, TC])
        gin = sc("gin", [HD, 2, TC])
        z = sc("z", [HD, 2, 2, TC])
        hin = sc("hin", [HD, 2, TC])
        h1 = sc("h1", [HD, 2, TC])
        hc = sc("hc", [HD, 2, TC])
        sq2 = sc("sq2", [HD, 2, TC])
        rs2 = sc("rs2", [HD, TC])
        hn = sc("hn", [HD, 2, TC])
        hact = gram[:, 0:FC * TC].rearrange("p (f t) -> p f t", f=FC)
        osb = gram[:, FC * TC:FC * TC + 3 * D].rearrange("p (n d) -> p n d", n=3)
        cctx.close()

        bank = [ctx.enter_context(nc.psum_tensor(f"bank{i}", [128, 1024], F32)) for i in range(4)]
        def pair_of(i):
            return bank[i][:, :].rearrange("p (h c) -> p h c", h=2)

        chan_loaded, wtok_loaded, w_loaded = sem("chan_loaded"), sem("wtok_loaded"), sem("w_loaded")
        memset_done, prep_done, temp_act, temp_ready = sem("memset_done"), sem("prep_done"), sem("temp_act"), sem("temp_ready")
        pat_loaded, h_ready, h_spilled = sem("pat_loaded"), sem("h_ready"), sem("h_spilled")
        xc_ready, sq_ready, rstd_log, rstd_ready = sem("xc_ready"), sem("sq_ready"), sem("rstd_log"), sem("rstd_ready")
        xn_ready, nbr_ready, dx_ready, xxx_ready = sem("xn_ready"), sem("nbr_ready"), sem("dx_ready"), sem("xxx_ready")
        m_ready, prod_ready, xs_ready = sem("m_ready"), sem("prod_ready"), sem("xs_ready")
        dect_ready, ew_ready, cs_ready = sem("dect_ready"), sem("ew_ready"), sem("cs_ready")
        cdiff_ready, clip_ready, e_ready = sem("cdiff_ready"), sem("clip_ready"), sem("e_ready")
        k_ready, r_ready, v_ready = sem("k_ready"), sem("r_ready"), sem("v_ready")
        th_ready, gate_ready, gate_spilled = sem("th_ready"), sem("gate_ready"), sem("gate_spilled")
        decayed_ready, f_ready = sem("decayed_ready"), sem("f_ready")
        at_ready, at_spilled = sem("at_ready"), sem("at_spilled")
        ring1_made, ring2_made, aux_made = sem("ring1_made"), sem("ring2_made"), sem("aux_made")
        sys_filled = sem("sys_filled")
        prep_dve, prep_act = sem("prep_dve"), sem("prep_act")
        elim_step = sem("elim_step")
        back_step = sem("back_step")
        xpose_ready, pv_ready = sem("xpose_ready"), sem("pv_ready")
        ffnw_loaded, c_memset, ffn_made, ffn_prep = sem("ffnw_loaded"), sem("c_memset"), sem("ffn_made"), sem("ffn_prep")
        at_loaded, gate_loaded, hin_loaded = sem("at_loaded"), sem("gate_loaded"), sem("hin_loaded")
        c1_made, c2_made = sem("c1_made"), sem("c2_made")
        y_ready, yT_ready, yc_ready, sqc_ready, rsc_log, rsc_ready = (sem("y_ready"), sem("yT_ready"), sem("yc_ready"),
                                                                      sem("sqc_ready"), sem("rsc_log"), sem("rsc_ready"))
        yn_ready, affine_ready, z_ready = sem("yn_ready"), sem("affine_ready"), sem("z_ready")
        h1_ready, hc_ready, sq2_ready, rs2_log, rs2_ready = (sem("h1_ready"), sem("hc_ready"), sem("sq2_ready"),
                                                             sem("rs2_log"), sem("rs2_ready"))
        hn_ready, hact_ready, osb_ready, out_stored = sem("hn_ready"), sem("hact_ready"), sem("osb_ready"), sem("out_stored")

        NTG, NTV = -(-T // 4), K // 4
        NFILL = NTG + NTV

        SOLVE_AT = {0: (5, 12), 1: (8, 8)}

        def iteration(i):
            return (i if i < NC else None, i - 1 if 0 <= i - 1 < NC else None, i - 2 if 0 <= i - 2 < NC else None)

        def completed(c3):
            return next((g for g in range(NG) if group_chunk(g) == c3), None)

        def mix_count(c, n):
            return NMIX * c + n + 1

        def heads_count(c, p, q):
            return Q * (PP * c + p) + q + 1

        ring1, ring2, aux = Ring(1), Ring(2), Ring(2)
        for i in range(NC + 2):
            c1, c2, c3 = iteration(i)
            if c1 is not None:
                ring1.add(("embed", c1), (h_ready, 2 * c1 + 2))
                ring1.add(("mean", c1), (xc_ready, c1 + 1))
                ring1.add(("var", c1), (rstd_log, c1 + 1))
                ring1.add(("w1", c1), (m_ready, c1 + 1))
            if c2 is not None:
                reads = {"dec1": (dect_ready, c2 + 1), "dec2": (ew_ready, c2 + 1), "v": (v_ready, c2 + 1),
                         "g": (gate_ready, c2 + 1), "k": (k_ready, c2 + 1), "r": (r_ready, c2 + 1)}
                for what in ((0, 1, "dec1", 2, "v", 3, "dec2", "g", 4, "k", "r")):
                    if isinstance(what, int):
                        ring2.add(("mix", c2, what), (prod_ready, mix_count(c2, what)))
                    else:
                        ring2.add((what, c2), reads[what])
            if c3 is not None:
                for p in range(PP):
                    for q in range(Q):
                        aux.add(("heads", c3, p, q), (at_ready, heads_count(c3, p, q)))
                g = completed(c3)
                if g is not None:
                    if g == 2:
                        for j in range(NTV):
                            aux.add(("solution", 0, j), (pv_ready, j + 1))
                    for j in range(NFILL):
                        aux.add(("fill", g, j), (sys_filled, NFILL * g + j + 1))
        for g in (1, 2):
            for j in range(NTV):
                aux.add(("solution", g, j), (pv_ready, NTV * g + j + 1))
        ringc1, ringc2 = Ring(1), Ring(2)
        for c in range(NC):
            ringc1.add(("y", c), (y_ready, c + 1))
            ringc1.add(("yT", c), (yT_ready, c + 1))
            ringc1.add(("gmean", c), (yc_ready, c + 1))
            ringc1.add(("gvar", c), (rsc_log, c + 1))
            ringc2.add(("wo", c), (h1_ready, c + 1))
            ringc2.add(("lmean", c), (hc_ready, c + 1))
            ringc2.add(("lvar", c), (rs2_log, c + 1))
            for j in range(FC // 2):
                ringc2.add(("fc", c, j), (hact_ready, FC // 2 * c + j + 1))
            ringc2.add(("proj", c), (osb_ready, c + 1))

        elim_at = {}
        count = 0
        for g in range(NG):
            for k in range(T):
                elim_at[g, k, "start"] = count
                count += 2 + 2 * len(bands(T - 1 - k)) if k < T - 1 else 1
            count += 1
            elim_at[g, "scaled"] = count
            if g == NG - 1:
                count += 2 * (T - 1)
                elim_at[g, "solved"] = count
        back_at = {g: 2 * (T - 1) * (g + 1) for g in range(NG - 1)}

        def wait_free(eng, ring, key):
            read = ring.before(key)
            if read is not None:
                eng.wait_ge(*read)

        def wait_solved(eng, g):
            if g < NG - 1:
                eng.wait_ge(back_step, back_at[g])
            else:
                eng.wait_ge(elim_step, elim_at[g, "solved"])

        def phase_a_over(eng):
            eng.wait_ge(ring1_made, len(ring1.tasks))
            eng.wait_ge(ring2_made, len(ring2.tasks))
            eng.wait_ge(aux_made, aux.made(("heads", NC - 1, PP - 1, Q - 1)))
            eng.wait_ge(decayed_ready, 4 * NC)
            eng.wait_ge(at_ready, Q * PP * NC)
            eng.wait_ge(r_ready, NC)
            eng.wait_ge(e_ready, 4 * NC)
            eng.wait_ge(clip_ready, 2 * NC)
            eng.wait_ge(gate_ready, NC)
            eng.wait_ge(h_spilled, 16 * NC)
            eng.wait_ge(gate_spilled, 16 * NC)
            eng.wait_ge(at_spilled, 32 * NC)

        def need(c):
            return next(g for g in range(NG) if NSYS * (g + 1) >= H * PP * (c + 1))

        def c_iterations():
            for j in range(NC + 1):
                yield (j if j < NC else None, j - 1 if j > 0 else None)

        def tokens(c):
            return [(n, 128 * n, min(128, TC - 128 * n)) for n in range(-(-TC // 128))]

        block = ctx.enter_context(nc.Block())

        @block.sync
        def _(sp):
            sp.dma_start(chan_s[:, :], chan).then_inc(chan_loaded, 16)
            sp.dma_start(pat[:, :, :], patches[0]).then_inc(pat_loaded, 16)
            sp.dma_start(wtok_s[:, :, :], wtok).then_inc(wtok_loaded, 16)
            for dst, src in ((blocks_s[:, :, :], blocks), (w1_s[:, :, :], w1), (w2a_s[:, :], w2a), (w2b_s[:, :], w2b),
                             (dw1_s[:, :, :], dw1), (dw2_s[:, :], dw2), (wproj4_s[:, :, :, :], wkvrg),
                             (scan_s[:, :], scanmask), (tri_s[:, :], tri), (ident_s[:, :], ident),
                             (lucid_s[:, :], lucid), (wo_s[:, :, :], wo)):
                sp.dma_start(dst, src).then_inc(w_loaded, 16)
            for i in range(NC + 2):
                c1, c2, c3 = iteration(i)
                if c1 is not None:
                    if c1 + 1 < NC:
                        sp.wait_ge(ring1_made, ring1.made(("embed", c1)))
                        sp.dma_start(pat[:, :, :], patches[c1 + 1]).then_inc(pat_loaded, 16)
                    sp.wait_ge(h_ready, 2 * c1 + 2)
                    sp.dma_start(h_dram[c1], hbuf[:, :, :].rearrange("p a t -> p (a t)")).then_inc(h_spilled, 16)
                if c2 is not None:
                    sp.wait_ge(gate_ready, c2 + 1)
                    sp.dma_start(gate_dram[c2], gate[:, :, :].rearrange("p a t -> p (a t)")).then_inc(gate_spilled, 16)
                if c3 is not None:
                    sp.wait_ge(at_ready, Q * PP * (c3 + 1))
                    for b2 in range(2):
                        sp.dma_start(at_dram[c3, b2], at[TP * b2:TP * b2 + T, :, :].rearrange("p a t -> p (a t)")
                                     ).then_inc(at_spilled, 16)
            phase_a_over(sp)
            for dst, src in ((wfc_s[:, :, :], wfc), (wpr_s[:, :, :], wproj), (bfc_s[:, :], bfc), (bpr_s[:, :], bproj),
                             (alph_s[:, :], alphas), (din_s[:, :], din), (hout_s[:, :], hout)):
                sp.dma_start(dst, src).then_inc(ffnw_loaded, 16)
            sp.wait_ge(c_memset, 1)
            for j1, j2 in c_iterations():
                if j1 is not None:
                    if j1 > 0:
                        sp.wait_ge(c1_made, ringc1.made(("y", j1 - 1)))
                    for b2 in range(2):
                        sp.dma_start(atc[TP * b2:TP * b2 + T, :, 0:HT],
                                     at_dram[j1, b2].rearrange("p (a t) -> p a t", a=PP)).then_inc(at_loaded, 16)
                    if j1 > 0:
                        sp.wait_ge(z_ready, j1)
                    sp.dma_start(gin[:, :, :].rearrange("p a t -> p (a t)"), gate_dram[j1]).then_inc(gate_loaded, 16)
                    if j1 > 0:
                        sp.wait_ge(h1_ready, j1)
                    sp.dma_start(hin[:, :, :].rearrange("p a t -> p (a t)"), h_dram[j1]).then_inc(hin_loaded, 16)
                if j2 is not None:
                    sp.wait_ge(osb_ready, j2 + 1)
                    for n, t0, nt in tokens(j2):
                        sp.dma_start(out[TC * j2 + t0:TC * j2 + t0 + nt, :], osb[0:nt, n, :]).then_inc(out_stored, 16)
            sp.wait_ge(out_stored, 16 * NC * len(tokens(0)))

        @block.tensor
        def _(pe):
            def mm(o, l, r, start=True, stop=True, at_tile=None):
                if at_tile is None:
                    return nc.tensor.matmul(o, l, r, start=start, stop=stop)
                return nc.tensor.matmul(o, l, r, start=start, stop=stop, tile_position=at_tile)

            r1 = pair_of(0)

            def two_halves(o, w, x):
                mm(o, w[:, 0], x[:, 0], True, False)
                return mm(o, w[:, 1], x[:, 1], False, True)

            def embed(c):
                pe.wait_ge(pat_loaded, 16 * (c + 1))
                wait_free(pe, ring1, ("embed", c))
                for half in range(2):
                    for f in range(FK):
                        last = mm(r1[0:HD, half, 0:PC], wtok_s[:, f, HD * half:HD * (half + 1)], pat[:, f, :],
                                  f == 0, f == FK - 1)
                last.then_inc(ring1_made, 1)

            def mean(c):
                pe.wait_ge(h_ready, 2 * c + 2)
                wait_free(pe, ring1, ("mean", c))
                mm(r1[0:HD, 0, 0:TC], blocks_s[:, 0, :], hbuf[:, 0, :], True, False)
                mm(r1[0:HD, 0, 0:TC], blocks_s[:, 0, :], hbuf[:, 1, :], False, True).then_inc(ring1_made, 1)

            def var(c):
                pe.wait_ge(sq_ready, c + 1)
                wait_free(pe, ring1, ("var", c))
                mm(r1[0:HD, 0, 0:TC], blocks_s[:, 0, :], sq[:, 0, :], True, False)
                mm(r1[0:HD, 0, 0:TC], blocks_s[:, 0, :], sq[:, 1, :], False, True).then_inc(ring1_made, 1)

            def lora_in(c):
                pe.wait_ge(xxx_ready, c + 1)
                wait_free(pe, ring1, ("w1", c))
                two_halves(r1[:, 0, 0:TC], w1_s[:, :, 0:128], xxx)
                two_halves(r1[0:MR, 1, 0:TC], w1_s[:, :, 128:128 + MR], xxx).then_inc(ring1_made, 1)

            def slot2(key):
                return pair_of(1 + ring2.slot(key))

            def mix(c, n):
                key, m = ("mix", c, n), MIXES[n]
                if n == 0:
                    pe.wait_ge(m_ready, c + 1)
                wait_free(pe, ring2, key)
                w2, mt, row = (w2a_s, m_a, MR * m) if m < 4 else (w2b_s, m_b, 0)
                for half in range(2):
                    last = mm(slot2(key)[0:HD, half, 0:TC], w2[row:row + MR, HD * half:HD * (half + 1)],
                              mt[row:row + MR, :], at_tile=(row, 0))
                last.then_inc(ring2_made, 1)

            def decay_in(c):
                pe.wait_ge(xs_ready, mix_count(c, 0))
                wait_free(pe, ring2, ("dec1", c))
                two_halves(slot2(("dec1", c))[0:DDEC, 0, 0:TC], dw1_s, xs[:, 0]).then_inc(ring2_made, 1)

            def decay_out(c):
                pe.wait_ge(dect_ready, c + 1)
                wait_free(pe, ring2, ("dec2", c))
                for half in range(2):
                    last = mm(slot2(("dec2", c))[0:HD, half, 0:TC], dw2_s[:, HD * half:HD * (half + 1)], dect[:, :])
                last.then_inc(ring2_made, 1)

            def project(c, what):
                n, w, x = {"k": (3, 0, 0), "r": (4, 2, 1), "g": (2, 3, 1)}[what]
                pe.wait_ge(xs_ready, mix_count(c, n))
                wait_free(pe, ring2, (what, c))
                for half in range(2):
                    last = two_halves(slot2((what, c))[0:HD, half, 0:TC],
                                      wproj4_s[:, w, :, HD * half:HD * (half + 1)], xs[:, x])
                last.then_inc(ring2_made, 1)

            def project_v(c):
                pe.wait_ge(xs_ready, mix_count(c, 1))
                wait_free(pe, ring2, ("v", c))
                for p in range(PP):
                    o = slot2(("v", c))[:, p // 2, D * (p % 2):D * (p % 2 + 1)]
                    for half in range(2):
                        last = mm(o, xv[:, half, 2 * p:2 * p + 2, :].rearrange("p b t -> p (b t)"),
                                  wproj4_s[:, 1, half, :], half == 0, half == 1)
                last.then_inc(ring2_made, 1)

            def aux_bank(key):
                s = aux.slot(key)
                return bank[3][:, 512 * s:512 * (s + 1)]

            def head_matrices(c, p):
                for q in range(Q):
                    key, row = ("heads", c, p, q), 32 * q
                    if p == 0 and q == 0:
                        pe.wait_ge(k_ready, c + 1)
                        pe.wait_ge(decayed_ready, 4 * c + 4)
                    wait_free(pe, aux, key)
                    o = aux_bank(key)
                    for n, (left, right) in enumerate(((kp, kpar), (ke[:, 0], re[:, 0]), (ke[:, 1], re[:, 1]))):
                        for b2 in range(2):
                            t0 = T * (2 * p + b2)
                            for half in range(2):
                                col = 2 * T * (2 * n + half)
                                last = mm(o[TP * b2:TP * (b2 + 1), col:col + 2 * T], left[row:row + 32, half, t0:t0 + TP],
                                          right[row:row + 32, :, half, t0:t0 + T], at_tile=(row, TP * b2))
                    last.then_inc(aux_made, 1)

            def fill(g):
                base = NSYS * (g % 2)
                for j in range(NFILL):
                    key = ("fill", g, j)
                    wait_free(pe, aux, key)
                    if j == 0:
                        pe.wait_ge(f_ready, Q * PP * (group_chunk(g) + 1))
                    if j == NTG:
                        pe.wait_ge(v_ready, group_chunk(g) + 1)
                    for n in range(4):
                        if j < NTG and 4 * j + n < T:
                            src = gram_v[:, base:base + NSYS, 4 * j + n]
                        elif j >= NTG:
                            src = v_v[:, base:base + NSYS, 4 * (j - NTG) + n]
                        else:
                            break
                        last = nc.tensor.transpose(aux_bank(key)[:, 128 * n:128 * (n + 1)], src, ident_s[:, :])
                    last.then_inc(aux_made, 1)

            def solution(g):
                for j in range(NTV):
                    key = ("solution", g, j)
                    wait_free(pe, aux, key)
                    if j == 0:
                        pe.wait_ge(xpose_ready, g + 1)
                    for n in range(4):
                        last = nc.tensor.transpose(aux_bank(key)[:, 128 * n:128 * (n + 1)],
                                                   xpose[:, 4 * j + n, :, :].rearrange("p b t -> p (b t)"), ident_s[:, :])
                    last.then_inc(aux_made, 1)

            pe.wait_ge(wtok_loaded, 16)
            for i in range(NC + 2):
                c1, c2, c3 = iteration(i)
                if c1 is not None:
                    embed(c1)
                    if c1 == 0:
                        pe.wait_ge(w_loaded, 16 * 12)
                if c2 is not None:
                    mix(c2, 0)
                    mix(c2, 1)
                if c3 is not None:
                    head_matrices(c3, 0)
                if c1 is not None:
                    mean(c1)
                if c2 is not None:
                    decay_in(c2)
                    mix(c2, 2)
                if c3 is not None:
                    head_matrices(c3, 1)
                if c1 is not None:
                    var(c1)
                if c2 is not None:
                    project_v(c2)
                    mix(c2, 3)
                    decay_out(c2)
                if c3 is not None:
                    head_matrices(c3, 2)
                if c2 is not None:
                    project(c2, "g")
                    mix(c2, 4)
                if c3 is not None:
                    head_matrices(c3, 3)
                if c1 is not None:
                    lora_in(c1)
                if c2 is not None:
                    project(c2, "k")
                    project(c2, "r")
                g = None if c3 is None else completed(c3)
                if g == 2:
                    solution(0)
                if g is not None:
                    fill(g)

            c1p, c2p = pair_of(1), (pair_of(0), pair_of(2))
            pe.wait_ge(ffn_prep, 1)
            pe.wait_ge(ffnw_loaded, 16 * 7)
            phase_a_over(pe)
            for half in range(2):
                o = c2p[half]
                for n in range(2):
                    last = mm(o[0:HD, n, 0:FH // 2], adin[:, HD * half:HD * (half + 1)],
                              hout_s[:, FH // 2 * n:FH // 2 * (n + 1)])
            for n in range(2):
                last = mm(c1p[:, n, 0:D], hout_s[:, 128 * n:128 * (n + 1)], adin[:, :])
            last.then_inc(ffn_made, 1)
            pe.wait_ge(ffn_prep, 2)
            for n in range(2, FC):
                j = n - 2
                last = mm(c2p[j // 2][:, j % 2, 0:D], hout_s[:, 128 * n:128 * (n + 1)], adin[:, :])
            for n in range(FC):
                mm(c1p[:, 0, n:n + 1], hout_s[:, 128 * n:128 * (n + 1)], aij[:, :])
            mm(c1p[0:1, 1, 0:D], aij[:, :], din_s[:, :]).then_inc(ffn_made, 1)
            pe.wait_ge(ffn_prep, 3)

            def c1slot(key):
                wait_free(pe, ringc1, key)
                return c1p

            def c2slot(key):
                wait_free(pe, ringc2, key)
                return c2p[ringc2.slot(key)]

            def apply_a(c):
                o = c1slot(("y", c))
                pe.wait_ge(at_loaded, 32 * (c + 1))
                pe.wait_ge(pv_ready, NTV * (need(c) + 1))
                for p in range(PP):
                    for b2 in range(2):
                        rows = slice(TP * b2, TP * b2 + T)
                        for h in range(H):
                            s = H * (PP * c + p) + h
                            last = mm(o[TP * b2:TP * (b2 + 1), p // 2, D * (p % 2) + K * h:D * (p % 2) + K * (h + 1)],
                                      atc[rows, p, T * h:T * h + TP], pv[rows, s // NSYS, s % NSYS, :],
                                      at_tile=(TP * b2, TP * b2))
                last.then_inc(c1_made, 1)

            def turn_y(c):
                pe.wait_ge(y_ready, c + 1)
                o = c1slot(("yT", c))
                for half in range(2):
                    for p in range(PP):
                        last = nc.tensor.transpose(o[0:HD, half, 128 * p:128 * (p + 1)],
                                                   ysb[:, p, HD * half:HD * (half + 1)], ident_s[:, :])
                last.then_inc(c1_made, 1)

            def per_head(c, key, ready, x):
                pe.wait_ge(ready, c + 1)
                o = c1slot((key, c))
                for half in range(2):
                    last = mm(o[0:HD, half, 0:TC], blocks_s[:, 1, :], x[:, half, :])
                last.then_inc(c1_made, 1)

            def attention_out(c):
                pe.wait_ge(z_ready, c + 1)
                o = c2slot(("wo", c))
                for half in range(2):
                    last = two_halves(o[0:HD, half, 0:TC], wo_s[:, :, HD * half:HD * (half + 1)], z[:, c % 2])
                last.then_inc(c2_made, 1)

            def per_token(c, key, ready, x):
                pe.wait_ge(ready, c + 1)
                o = c2slot((key, c))
                mm(o[0:HD, 0, 0:TC], blocks_s[:, 0, :], x[:, 0, :], True, False)
                mm(o[0:HD, 0, 0:TC], blocks_s[:, 0, :], x[:, 1, :], False, True).then_inc(c2_made, 1)

            def ffn_in(c, j):
                if j == 0:
                    pe.wait_ge(hn_ready, c + 1)
                o = c2slot(("fc", c, j))
                for n in range(2):
                    f = 2 * j + n
                    last = two_halves(o[:, n, 0:TC], wfc_s[:, :, 128 * f:128 * (f + 1)], hn)
                last.then_inc(c2_made, 1)

            def ffn_out(c):
                o = c2slot(("proj", c))
                pe.wait_ge(hact_ready, FC // 2 * (c + 1))
                for n, t0, nt in tokens(c):
                    dst = o[0:nt, n // 2, D * (n % 2):D * (n % 2 + 1)]
                    for f in range(FC):
                        mm(dst, hact[:, f, t0:t0 + nt], wpr_s[:, f, :], f == 0, False)
                    for half in range(2):
                        mm(dst[:, HD * half:HD * (half + 1)], h1[:, half, t0:t0 + nt], ident_s[0:HD, 0:HD], False, False)
                    last = mm(dst, ones_s[:, 0:nt], bpr_s[:, :], False, True)
                last.then_inc(c2_made, 1)

            for j1, j2 in c_iterations():
                if j1 is not None:
                    if j1 > 0 and need(j1) > need(j1 - 1):
                        solution(need(j1))
                    apply_a(j1)
                if j2 is not None:
                    attention_out(j2)
                if j1 is not None:
                    turn_y(j1)
                if j2 is not None:
                    per_token(j2, "lmean", h1_ready, h1)
                if j1 is not None:
                    per_head(j1, "gmean", yT_ready, yT)
                if j2 is not None:
                    per_token(j2, "lvar", sq2_ready, sq2)
                if j1 is not None:
                    per_head(j1, "gvar", sqc_ready, sqc)
                if j2 is not None:
                    for j in range(FC // 2):
                        ffn_in(j2, j)
                    ffn_out(j2)

        @block.scalar
        def _(act):
            r1, a = pair_of(0), nc.scalar.activation

            def slot2(key):
                return pair_of(1 + ring2.slot(key))

            def aux_bank(key):
                s = aux.slot(key)
                return bank[3][:, 512 * s:512 * (s + 1)]

            act.wait_ge(w_loaded, 16 * 12)
            nc.scalar.preload_act_table_set("natural_log_exp_and_others")
            a(tmp3[:, 0, :], lucid_s[:, :], ACT.Abs).then_inc(temp_act, 1)
            act.wait_ge(temp_act, 1)
            a(tmp3[:, 1, :], tmp3[:, 0, :], ACT.Exp, scale=-1.0).then_inc(temp_act, 1)
            act.wait_ge(temp_act, 2)
            act.wait_ge(memset_done, 1)
            a(tmp3[:, 0, :], tmp3[:, 1, :], ACT.Ln, bias=1.0).then_inc(temp_act, 1)

            def square(c):
                act.wait_ge(xc_ready, c + 1)
                if c > 0:
                    act.wait_ge(ring1_made, ring1.made(("w1", c - 1)))
                a(sq[:, :, :], xc[:, :, :], ACT.Square).then_inc(sq_ready, 1)

            def inverse_std(c):
                nc.scalar.preload_act_table_set("natural_log_exp_and_others")
                act.wait_ge(ring1_made, ring1.made(("var", c)))
                if c > 0:
                    act.wait_ge(xn_ready, c)
                a(rstd[:, :], r1[0:HD, 0, 0:TC], ACT.Ln, bias=eps_s[0:HD, 0:1]).then_inc(rstd_log, 1)
                act.wait_ge(rstd_log, c + 1)
                a(rstd[:, :], rstd[:, :], ACT.Exp, scale=-0.5).then_inc(rstd_ready, 1)

            def lora_tanh(c):
                act.wait_ge(ring1_made, ring1.made(("w1", c)))
                if c > 0:
                    act.wait_ge(ring2_made, ring2.made(("mix", c - 1, 4)))
                a(m_a[:, :], r1[:, 0, 0:TC], ACT.Tanh)
                a(m_b[:, :], r1[0:MR, 1, 0:TC], ACT.Tanh).then_inc(m_ready, 1)

            def decay_tanh(c):
                act.wait_ge(ring2_made, ring2.made(("dec1", c)))
                if c > 0:
                    act.wait_ge(ring2_made, ring2.made(("dec2", c - 1)))
                a(dect[:, :], slot2(("dec1", c))[0:DDEC, 0, 0:TC], ACT.Tanh).then_inc(dect_ready, 1)

            def decay_exp(c):
                act.wait_ge(ring2_made, ring2.made(("dec2", c)))
                if c > 0:
                    act.wait_ge(e_ready, 4 * c)
                for half in range(2):
                    last = a(ew[:, half, :], slot2(("dec2", c))[0:HD, half, 0:TC], ACT.Exp,
                             bias=chan_s[:, V_TD + half:V_TD + half + 1])
                last.then_inc(ew_ready, 1)

            def copy_v(c):
                act.wait_ge(ring2_made, ring2.made(("v", c)))
                if H * PP * (c + 1) > GR:
                    act.wait_ge(aux_made, aux.made(("fill", 0, NFILL - 1)))
                for n in range(2):
                    for ro, so, m in pieces(H * (PP * c + 2 * n), 2 * H):
                        last = nc.scalar.copy(vring[:, K * ro:K * (ro + m)],
                                              slot2(("v", c))[:, n, K * so:K * (so + m)])
                last.then_inc(v_ready, 1)

            def gate_tanh(c):
                act.wait_ge(ring2_made, ring2.made(("g", c)))
                if c > 0:
                    act.wait_ge(gate_spilled, 16 * c)
                a(th[:, :, :], slot2(("g", c))[0:HD, :, 0:TC], ACT.Tanh, scale=0.5).then_inc(th_ready, 1)

            def decay_factors(c, e):
                act.wait_ge(clip_ready, 2 * c + 1 + e // 2)
                n = 4 * c + e
                if n >= 2:
                    act.wait_ge(decayed_ready, n - 1)
                src, scale = ((ew, 1.0), (ew, -1.0), (cs, -1.0), (cs, 1.0))[e]
                a(ex[:, e % 2], src[:, :, :], ACT.Exp, scale=scale).then_inc(e_ready, 1)

            def copy_k(c):
                act.wait_ge(ring2_made, ring2.made(("k", c)))
                if c > 0:
                    act.wait_ge(aux_made, aux.made(("heads", c - 1, PP - 1, Q - 1)))
                    act.wait_ge(decayed_ready, 4 * c)
                src = slot2(("k", c))[0:HD, :, 0:TC]
                nc.scalar.copy(kp[:, :, 0:TC], src)
                for par in range(2):
                    last = nc.scalar.activation(kpar[:, par], src, ACT.Copy, scale=chan_s[:, V_PAR + par:V_PAR + par + 1])
                last.then_inc(k_ready, 1)

            def copy_r(c):
                act.wait_ge(ring2_made, ring2.made(("r", c)))
                if c > 0:
                    act.wait_ge(decayed_ready, 4 * c)
                for par in range(2):
                    last = nc.scalar.activation(rpar[:, par], slot2(("r", c))[0:HD, :, 0:TC], ACT.Copy,
                                                scale=chan_s[:, V_PAR + par:V_PAR + par + 1])
                last.then_inc(r_ready, 1)

            def copy_matrices(c, p):
                first = H * (PP * c + p)
                if first + H > GR:
                    act.wait_ge(aux_made, aux.made(("fill", 0, NFILL - 1)))
                if c > 0 and p == 0:
                    act.wait_ge(at_spilled, 32 * c)
                for q in range(Q):
                    key = ("heads", c, p, q)
                    act.wait_ge(aux_made, aux.made(key))
                    src = aux_bank(key)[:, 0:4 * T].rearrange("p (a n) -> p a n", a=2)
                    s0, s1 = (first + 2 * q) % GR, (first + H // 2 + 2 * q) % GR
                    if s1 > s0:
                        a0 = min(s0, GR - H)
                        nc.scalar.copy(gram[:, T * a0:T * (a0 + H)].rearrange("p (a n) -> p a n", a=2)[
                            :, :, T * (s0 - a0):T * (s0 - a0 + 2)], src)
                    else:
                        nc.scalar.copy(gram[:, T * s0:T * (s0 + 2)], src[:, 0])
                        nc.scalar.copy(gram[:, T * s1:T * (s1 + 2)], src[:, 1])
                    nc.scalar.copy(at[:, p, :].rearrange("p (a n) -> p a n", a=2)[:, :, 2 * T * q:2 * T * (q + 1)],
                                   aux_bank(key)[:, 4 * T:8 * T].rearrange("p (a n) -> p a n", a=2)).then_inc(f_ready, 1)

            def fill(g):
                m = sysm[:, g % 2]
                for j in range(NFILL):
                    key = ("fill", g, j)
                    act.wait_ge(aux_made, aux.made(key))
                    if j == 0 and g == 2:
                        act.wait_ge(xpose_ready, 1)
                    src = aux_bank(key)[:, :].rearrange("p (n b t) -> p n b t", n=4, b=2)
                    if j < NTG:
                        n = min(4, T - 4 * j)
                        dst = m[:, :, 4 * j:4 * j + n, 0:T].rearrange("p b n t -> p n b t")
                    else:
                        n = 4
                        k0 = T + 4 * (j - NTG)
                        dst = m[:, :, :, k0:k0 + 4].rearrange("p b t n -> p n b t")
                    nc.scalar.copy(dst, src[:, 0:n, :, 0:T]).then_inc(sys_filled, 1)

            def prepare(g):
                act.wait_ge(prep_dve, 6 * g + 1)
                a(nrm[:, :, :], nrm[:, :, :], ACT.Sqrt).then_inc(prep_act, 1)
                act.wait_ge(prep_dve, 6 * g + 4)
                act.wait_ge(temp_ready, 1)
                a(sysm[:, g % 2, :, :, 0:T], sysm[:, g % 2, :, :, 0:T], ACT.Exp, scale=temp[:, g:g + 1]).then_inc(prep_act, 1)

            def solution_out(g):
                wait_solved(act, g)
                if g > 0:
                    act.wait_ge(aux_made, aux.made(("solution", g - 1, NTV - 1)))
                else:
                    act.wait_ge(c_memset, 1)
                for b2 in range(2):
                    last = nc.scalar.copy(xpose[:, :, b2, 0:T], sysm[:, g % 2, b2, :, T:W].rearrange("p t k -> p k t"))
                last.then_inc(xpose_ready, 1)

            def solution_in(g):
                for j in range(NTV):
                    act.wait_ge(aux_made, aux.made(("solution", g, j)))
                    nc.scalar.copy(pv[:, g, :, 4 * j:4 * j + 4].rearrange("p s k -> p k s"),
                                   aux_bank(("solution", g, j))[:, :].rearrange("p (k s) -> p k s", k=4)
                                   ).then_inc(pv_ready, 1)

            for i in range(NC + 2):
                c1, c2, c3 = iteration(i)
                if c3 is not None:
                    copy_matrices(c3, 0)
                if c1 is not None:
                    square(c1)
                for g in range(NG - 1):
                    if i == SOLVE_AT[g][0]:
                        prepare(g)
                if c2 is not None:
                    decay_tanh(c2)
                if c3 is not None:
                    copy_matrices(c3, 1)
                if c1 is not None:
                    inverse_std(c1)
                if c2 is not None:
                    copy_v(c2)
                    decay_exp(c2)
                if c3 is not None:
                    copy_matrices(c3, 2)
                if c2 is not None:
                    gate_tanh(c2)
                if c3 is not None:
                    copy_matrices(c3, 3)
                if c1 is not None:
                    lora_tanh(c1)
                if c2 is not None:
                    decay_factors(c2, 0)
                    copy_k(c2)
                    copy_r(c2)
                    for e in range(1, 4):
                        decay_factors(c2, e)
                g = None if c3 is None else completed(c3)
                if g is not None and g < 2:
                    fill(g)
            phase_a_over(act)
            solution_out(0)
            solution_in(0)
            fill(2)
            prepare(2)

            c1p, c2p = pair_of(1), (pair_of(0), pair_of(2))

            def copy_y(c):
                act.wait_ge(c1_made, ringc1.made(("y", c)))
                if c > 0:
                    act.wait_ge(c1_made, ringc1.made(("yT", c - 1)))
                nc.scalar.copy(ysb[:, :, :].rearrange("p (n m) d -> p n (m d)", n=2), c1p[:, :, 0:2 * D]
                               ).then_inc(y_ready, 1)

            def copy_yT(c):
                act.wait_ge(c1_made, ringc1.made(("yT", c)))
                if c > 0:
                    act.wait_ge(yc_ready, c)
                for half in range(2):
                    last = nc.scalar.copy(yT[:, half, :].rearrange("p (b t) -> p b t", b=NB),
                                          c1p[0:HD, half, :].rearrange("p (b t) -> p b t", b=NB)[:, :, 0:T])
                last.then_inc(yT_ready, 1)

            def square_y(c):
                act.wait_ge(yc_ready, c + 1)
                if c > 0:
                    act.wait_ge(c1_made, ringc1.made(("gvar", c - 1)))
                a(sqc[:, :, :], yc[:, :, :], ACT.Square).then_inc(sqc_ready, 1)

            def inverse_std_y(c):
                nc.scalar.preload_act_table_set("natural_log_exp_and_others")
                act.wait_ge(c1_made, ringc1.made(("gvar", c)))
                if c > 0:
                    act.wait_ge(yn_ready, c)
                a(rsc[:, :, :], c1p[0:HD, :, 0:TC], ACT.Ln, bias=eps_s[0:HD, 1:2]).then_inc(rsc_log, 1)
                act.wait_ge(rsc_log, c + 1)
                a(rsc[:, :, :], rsc[:, :, :], ACT.Exp, scale=-0.5).then_inc(rsc_ready, 1)

            def affine(c):
                act.wait_ge(yn_ready, c + 1)
                for half in range(2):
                    last = a(yc[:, half, :], yc[:, half, :], ACT.Identity, scale=chan_s[:, V_LNW + half:V_LNW + half + 1],
                             bias=chan_s[:, V_LNB + half:V_LNB + half + 1])
                last.then_inc(affine_ready, 1)

            def square_h(c):
                act.wait_ge(hc_ready, c + 1)
                if c > 0:
                    act.wait_ge(c2_made, ringc2.made(("lvar", c - 1)))
                a(sq2[:, :, :], hc[:, :, :], ACT.Square).then_inc(sq2_ready, 1)

            def inverse_std_h(c):
                nc.scalar.preload_act_table_set("natural_log_exp_and_others")
                act.wait_ge(c2_made, ringc2.made(("lvar", c)))
                if c > 0:
                    act.wait_ge(hn_ready, c)
                a(rs2[:, :], c2p[ringc2.slot(("lvar", c))][0:HD, 0, 0:TC], ACT.Ln, bias=eps_s[0:HD, 0:1]
                  ).then_inc(rs2_log, 1)
                act.wait_ge(rs2_log, c + 1)
                a(rs2[:, :], rs2[:, :], ACT.Exp, scale=-0.5).then_inc(rs2_ready, 1)

            def gelu(c, j):
                act.wait_ge(c2_made, ringc2.made(("fc", c, j)))
                if c > 0 and j == 0:
                    act.wait_ge(c2_made, ringc2.made(("proj", c - 1)))
                if c == 0:
                    act.wait_ge(ffn_prep, 3)
                for n in range(2):
                    f = 2 * j + n
                    last = a(hact[:, f, :], c2p[ringc2.slot(("fc", c, j))][:, n, 0:TC], ACT.Gelu_apprx_tanh,
                             bias=bfc_s[:, f:f + 1])
                last.then_inc(hact_ready, 1)

            for j1, j2 in c_iterations():
                if j1 is not None:
                    if j1 > 0 and need(j1) > need(j1 - 1):
                        solution_out(need(j1))
                        solution_in(need(j1))
                    copy_y(j1)
                    copy_yT(j1)
                if j2 is not None:
                    square_h(j2)
                if j1 is not None:
                    square_y(j1)
                if j2 is not None:
                    inverse_std_h(j2)
                if j1 is not None:
                    inverse_std_y(j1)
                    affine(j1)
                if j2 is not None:
                    for j in range(FC // 2):
                        gelu(j2, j)

        @block.gpsimd
        def _(pool):
            tt = nc.gpsimd.tensor_tensor
            nc.gpsimd.memset(eps_s[:, 0:1], LN_EPS)
            nc.gpsimd.memset(eps_s[:, 1:2], GN_EPS)
            nc.gpsimd.memset(xpad[:, :, :, :, :], 0.0)
            nc.gpsimd.memset(xv[:, :, :, :], 0.0)
            nc.gpsimd.memset(kp[:, :, TC:TC + TP - T], 0.0)
            nc.gpsimd.memset(ke[:, :, :, TC:TC + TP - T], 0.0).then_inc(memset_done, 1)

            def token_view(x):
                return x.rearrange("p a (b t) -> p (a b) t", t=T)

            def neighbours(c):
                pool.wait_ge(xn_ready, c + 1)
                x = xpad[:, c % 2].rearrange("p a b t -> p (a b) t")
                tt(token_view(dx[:, c % 2]), x[:, :, 0:T], x[:, :, 2:T + 2], ALU.add).then_inc(nbr_ready, 1)

            def mixed(c, n):
                pool.wait_ge(prod_ready, mix_count(c, n))
                slot = (NMIX * c + n) % 2
                x = xpad[:, c % 2].rearrange("p a b t -> p (a b) t")[:, :, 1:T + 1]
                if n == 1:
                    if c > 0:
                        pool.wait_ge(ring2_made, ring2.made(("v", c - 1)))
                    dst = xv[:, :, :, :].rearrange("p a b t -> p (a b) t")[:, :, 0:T]
                else:
                    which = {0: 0, 2: 1, 3: 0, 4: 1}[n]
                    if n == 0 and c > 0:
                        pool.wait_ge(ring2_made, ring2.made(("k", c - 1)))
                    if n == 2 and c > 0:
                        pool.wait_ge(ring2_made, ring2.made(("r", c - 1)))
                    if n == 3:
                        pool.wait_ge(ring2_made, ring2.made(("dec1", c)))
                    if n == 4:
                        pool.wait_ge(ring2_made, ring2.made(("g", c)))
                    dst = token_view(xs[:, which])
                tt(dst, token_view(prod[:, slot]), x, ALU.add).then_inc(xs_ready, 1)

            def decay_sums(c):
                pool.wait_ge(cs_ready, c + 1)
                if c > 0:
                    pool.wait_ge(cdiff_ready, 3 * c)
                tt(cb[:, :, :], cs[:, :, :], ew[:, :, :], ALU.add).then_inc(cdiff_ready, 1)
                pool.wait_ge(cdiff_ready, 3 * c + 1)

                def centred(dst, src):
                    s = token_view(src)
                    mid = s[:, :, MID:MID + 1].broadcast_to([HD, 2 * NB, T])
                    return tt(token_view(dst), s, mid, ALU.subtract)
                centred(ew, cs).then_inc(cdiff_ready, 1)
                pool.wait_ge(cdiff_ready, 3 * c + 2)
                centred(cs, cb).then_inc(cdiff_ready, 1)

            def decayed(c, e):
                pool.wait_ge(e_ready, 4 * c + e + 1)
                if e == 0:
                    pool.wait_ge(k_ready, c + 1)
                    pool.wait_ge(r_ready, c + 1)
                    if c > 0:
                        pool.wait_ge(aux_made, aux.made(("heads", c - 1, PP - 1, Q - 1)))
                f = ex[:, e % 2]
                if e % 2 == 0:
                    f2 = f.unsqueeze(1).broadcast_to([HD, 2, 2, TC])
                    last = tt(re[:, e // 2], rpar[:, :, :, :], f2, ALU.mult)
                else:
                    last = tt(ke[:, e // 2, :, 0:TC], kp[:, :, 0:TC], f, ALU.mult)
                last.then_inc(decayed_ready, 1)

            def back_substitute(g, k_from, k_to):
                m = sysm[:, g % 2]
                step = 2 * (T - 1) * g + 2 * (T - 1 - k_from)
                if k_from == T - 1:
                    pool.wait_ge(elim_step, elim_at[g, "scaled"])
                for k in range(k_from, k_to, -1):
                    if step > 0:
                        pool.wait_ge(back_step, step)
                    o = outer_b[:, 0:2 * k * K].rearrange("p (b i c) -> p b i c", b=2, c=K)
                    u = m[:, :, k, 0:k].unsqueeze(3).broadcast_to([NSYS, 2, k, K])
                    x = m[:, :, k, T:W].unsqueeze(2).broadcast_to([NSYS, 2, k, K])
                    tt(o, u, x, ALU.mult).then_inc(back_step, 1)
                    pool.wait_ge(back_step, step + 1)
                    v = m[:, :, 0:k, T:W]
                    tt(v, v, o, ALU.subtract).then_inc(back_step, 1)
                    step += 2

            for i in range(NC + 2):
                c1, c2, c3 = iteration(i)
                if c2 is not None:
                    mixed(c2, 0)
                    mixed(c2, 1)
                    mixed(c2, 2)
                if c1 is not None:
                    neighbours(c1)
                if c2 is not None:
                    mixed(c2, 3)
                    decay_sums(c2)
                    mixed(c2, 4)
                    for e in range(4):
                        decayed(c2, e)
                if i == 8:
                    back_substitute(0, T - 1, 0)
            phase_a_over(pool)
            nc.gpsimd.memset(xpose[:, :, :, :], 0.0)
            nc.gpsimd.memset(atc[:, :, :], 0.0)
            nc.gpsimd.memset(ones_s[:, :], 1.0).then_inc(c_memset, 1)
            back_substitute(1, T - 1, 0)
            for c in range(NC):
                pool.wait_ge(affine_ready, c + 1)
                pool.wait_ge(gate_loaded, 16 * (c + 1))
                if c > 1:
                    pool.wait_ge(c2_made, ringc2.made(("wo", c - 2)))
                tt(z[:, c % 2], yc[:, :, :], gin[:, :, :], ALU.mult).then_inc(z_ready, 1)

        @block.vector
        def _(dve):
            tt, ts, stt = nc.vector.tensor_tensor, nc.vector.tensor_scalar, nc.vector.scalar_tensor_tensor
            r1 = pair_of(0)

            def slot2(key):
                return pair_of(1 + ring2.slot(key))

            def token_view(x):
                return x.rearrange("p a (b t) -> p (a b) t", t=T)

            dve.wait_ge(chan_loaded, 16)
            for half in range(2):
                ts(posb[:, half, :], chan_s[:, V_POS + NPT * half:V_POS + NPT * (half + 1)],
                   chan_s[:, V_TOKB + half:V_TOKB + half + 1], None, ALU.add).then_inc(prep_done, 1)
            dve.wait_ge(prep_done, 2)

            def embedded(c):
                if c > 0:
                    dve.wait_ge(h_spilled, 16 * c)
                    dve.wait_ge(ring1_made, ring1.made(("mean", c - 1)))
                h4 = hbuf[:, :, :].rearrange("p a (b t) -> p a b t", b=NB)
                nc.vector.tensor_copy(h4[:, :, :, 0], chan_s[:, V_CLS:V_CLS + 2].unsqueeze(2).broadcast_to([HD, 2, NB])
                                      ).then_inc(h_ready, 1)
                dve.wait_ge(ring1_made, ring1.made(("embed", c)))
                for half in range(2):
                    src = r1[0:HD, half, 0:PC].rearrange("p (b t) -> p b t", b=NB)
                    last = tt(h4[:, half, :, 1:T], src, posb[:, half, :].unsqueeze(1).broadcast_to([HD, NB, NPT]), ALU.add)
                last.then_inc(h_ready, 1)

            def centre(c):
                dve.wait_ge(ring1_made, ring1.made(("mean", c)))
                dve.wait_ge(h_ready, 2 * c + 2)
                if c > 0:
                    dve.wait_ge(sq_ready, c)
                    dve.wait_ge(xn_ready, c)
                tt(xc[:, :, :], hbuf[:, :, :], r1[0:HD, 0:1, 0:TC].broadcast_to([HD, 2, TC]), ALU.subtract
                   ).then_inc(xc_ready, 1)

            def normalised(c):
                dve.wait_ge(rstd_ready, c + 1)
                dve.wait_ge(memset_done, 1)
                if c > 1:
                    dve.wait_ge(xs_ready, mix_count(c - 2, 4))
                dst = xpad[:, c % 2].rearrange("p a b t -> p (a b) t")[:, :, 1:T + 1]
                for half in range(2):
                    last = tt(dst[:, NB * half:NB * (half + 1)], xc[:, half, :].rearrange("p (b t) -> p b t", t=T),
                              rstd[:, :].rearrange("p (b t) -> p b t", t=T), ALU.mult)
                last.then_inc(xn_ready, 1)

            def difference(c):
                dve.wait_ge(nbr_ready, c + 1)
                x = xpad[:, c % 2].rearrange("p a b t -> p (a b) t")[:, :, 1:T + 1]
                d = token_view(dx[:, c % 2])
                stt(out=d, in0=d, scalar=0.5, in1=x, op0=ALU.mult, op1=ALU.subtract).then_inc(dx_ready, 1)
                dve.wait_ge(dx_ready, c + 1)
                if c > 0:
                    dve.wait_ge(ring1_made, ring1.made(("w1", c - 1)))
                for half in range(2):
                    b = slice(NB * half, NB * (half + 1))
                    last = stt(out=xxx[:, half, :].rearrange("p (b t) -> p b t", t=T), in0=d[:, b],
                               scalar=chan_s[:, V_MAA + half:V_MAA + half + 1], in1=x[:, b], op0=ALU.mult, op1=ALU.add)
                last.then_inc(xxx_ready, 1)

            def product(c, n):
                key, m = ("mix", c, n), MIXES[n]
                dve.wait_ge(ring2_made, ring2.made(key))
                count = mix_count(c, n)
                if count > 2:
                    dve.wait_ge(xs_ready, count - 2)
                for half in range(2):
                    col = V_MAA + 2 * (m + 1) + half
                    last = stt(out=prod[:, (count - 1) % 2, half, :], in0=slot2(key)[0:HD, half, 0:TC],
                               scalar=chan_s[:, col:col + 1], in1=dx[:, c % 2, half, :], op0=ALU.add, op1=ALU.mult)
                last.then_inc(prod_ready, 1)

            def scan(c):
                dve.wait_ge(ew_ready, c + 1)
                if c > 0:
                    dve.wait_ge(e_ready, 4 * c)
                for half in range(2):
                    last = nc.vector.tensor_tensor_scan(cs[:, half, :], scan_s[:, :], ew[:, half, :], 0.0, ALU.mult,
                                                        ALU.subtract)
                last.then_inc(cs_ready, 1)

            def clip(c):
                for n, x in enumerate((ew, cs)):
                    dve.wait_ge(cdiff_ready, 3 * c + 2 + n)
                    ts(x[:, :, :], x[:, :, :], -60.0, 60.0, ALU.max, ALU.min).then_inc(clip_ready, 1)

            def gated(c):
                dve.wait_ge(th_ready, c + 1)
                stt(out=gate[:, :, :], in0=th[:, :, :], scalar=1.0, in1=slot2(("g", c))[0:HD, :, 0:TC], op0=ALU.add,
                    op1=ALU.mult).then_inc(gate_ready, 1)

            def backward_half(c, p):
                for q in range(Q):
                    key = ("heads", c, p, q)
                    dve.wait_ge(f_ready, heads_count(c, p, q))
                    s = aux.slot(key)
                    nc.vector.copy_predicated(
                        at[:, p, :].rearrange("p (a h t) -> p a h t", a=2, t=T)[:, :, 2 * q:2 * q + 2, :],
                        tri_s[:, :].unsqueeze(1).unsqueeze(1).broadcast_to([128, 2, 2, T]),
                        bank[3][:, 512 * s + 8 * T:512 * s + 12 * T].rearrange("p (a h t) -> p a h t", a=2, t=T)
                        ).then_inc(at_ready, 1)

            def diagonal(g):
                flat = sysm[:, g % 2].rearrange("p b i j -> p b (i j)")
                return flat[:, :, 0:(T - 1) * (W + 1) + 1:W + 1]

            def prepare(g):
                m = sysm[:, g % 2, :, :, 0:T]
                n0 = 6 * g
                dve.wait_ge(sys_filled, NFILL * (g + 1))
                ts(nrm[:, :, :], diagonal(g), 1e-24, None, ALU.max).then_inc(prep_dve, 1)
                dve.wait_ge(prep_act, 2 * g + 1)
                nc.vector.reciprocal(nrm[:, :, :], nrm[:, :, :]).then_inc(prep_dve, 1)
                dve.wait_ge(prep_dve, n0 + 2)
                rows = nrm[:, :, :].unsqueeze(3).broadcast_to([NSYS, 2, T, T])
                cols = nrm[:, :, :].unsqueeze(2).broadcast_to([NSYS, 2, T, T])
                tt(m, m, rows, ALU.mult).then_inc(prep_dve, 1)
                dve.wait_ge(prep_dve, n0 + 3)
                tt(m, m, cols, ALU.mult).then_inc(prep_dve, 1)
                dve.wait_ge(prep_act, 2 * g + 2)
                ts(m, m, float(np.exp(-20.0)), float(np.exp(20.0)), ALU.max, ALU.min).then_inc(prep_dve, 1)
                dve.wait_ge(prep_dve, n0 + 5)
                ts(diagonal(g), diagonal(g), 1.0, None, ALU.add).then_inc(prep_dve, 1)
                dve.wait_ge(prep_dve, n0 + 6)

            def eliminate(g, k_from, k_to):
                m, rd = sysm[:, g % 2], rdiag[:, g % 2]
                for k in range(k_from, k_to):
                    n = elim_at[g, k, "start"]
                    if n > 0:
                        dve.wait_ge(elim_step, n)
                    nc.vector.reciprocal(rd[:, :, k:k + 1], m[:, :, k, k:k + 1]).then_inc(elim_step, 1)
                    n += 1
                    if k == T - 1:
                        continue
                    rest = T - 1 - k
                    dve.wait_ge(elim_step, n)
                    mult = m[:, :, k + 1:T, k]
                    tt(mult, m[:, :, k, k + 1:T], rd[:, :, k:k + 1].broadcast_to([NSYS, 2, rest]), ALU.mult
                       ).then_inc(elim_step, 1)
                    n += 1
                    dve.wait_ge(elim_step, n)
                    parts, used = [], 0
                    for r0, r1_ in bands(rest):
                        rows, cols = r1_ - r0, W - (k + 1 + r0)
                        o = outer[:, used:used + 2 * rows * cols].rearrange("p (b i j) -> p b i j", b=2, j=cols)
                        used += 2 * rows * cols
                        tt(o, m[:, :, k + 1 + r0:k + 1 + r1_, k].unsqueeze(3).broadcast_to([NSYS, 2, rows, cols]),
                           m[:, :, k, k + 1 + r0:W].unsqueeze(2).broadcast_to([NSYS, 2, rows, cols]), ALU.mult
                           ).then_inc(elim_step, 1)
                        parts.append((o, m[:, :, k + 1 + r0:k + 1 + r1_, k + 1 + r0:W]))
                    for o, a_ in parts:
                        n += 1
                        dve.wait_ge(elim_step, n)
                        tt(a_, a_, o, ALU.subtract).then_inc(elim_step, 1)

            def scale_rows(g):
                v = sysm[:, g % 2, :, :, T:W]
                dve.wait_ge(elim_step, elim_at[g, "scaled"] - 1)
                tt(v, v, rdiag[:, g % 2].unsqueeze(3).broadcast_to([NSYS, 2, T, K]), ALU.mult).then_inc(elim_step, 1)

            def back_substitute(g):
                m = sysm[:, g % 2]
                n = elim_at[g, "scaled"]
                for k in range(T - 1, 0, -1):
                    dve.wait_ge(elim_step, n)
                    o = outer[:, 0:2 * k * K].rearrange("p (b i c) -> p b i c", b=2, c=K)
                    u = m[:, :, k, 0:k].unsqueeze(3).broadcast_to([NSYS, 2, k, K])
                    x = m[:, :, k, T:W].unsqueeze(2).broadcast_to([NSYS, 2, k, K])
                    tt(o, u, x, ALU.mult).then_inc(elim_step, 1)
                    dve.wait_ge(elim_step, n + 1)
                    v = m[:, :, 0:k, T:W]
                    tt(v, v, o, ALU.subtract).then_inc(elim_step, 1)
                    n += 2

            def solve_part(i, part):
                for g, (i0, n_parts) in SOLVE_AT.items():
                    at_part = 4 * (i - i0) + part
                    if 0 <= at_part < n_parts:
                        total = n_parts if g == 0 else 12
                        if at_part == 0:
                            prepare(g)
                        eliminate(g, T * at_part // total, T * (at_part + 1) // total)
                        if at_part == total - 1:
                            scale_rows(g)

            for i in range(NC + 2):
                c1, c2, c3 = iteration(i)
                if c1 is not None:
                    embedded(c1)
                    if c1 == 0:
                        dve.wait_ge(w_loaded, 16 * 12)
                        ts(wo_s[:, :, :], wo_s[:, :, :], 0.5, None, ALU.mult).then_inc(prep_done, 1)
                        dve.wait_ge(temp_act, 3)
                        ts(lucid_s[:, :], lucid_s[:, :], 0.0, None, ALU.max).then_inc(prep_done, 1)
                        dve.wait_ge(prep_done, 4)
                        tt(temp[:, :], lucid_s[:, :], tmp3[:, 0, :], ALU.add).then_inc(temp_ready, 1)
                if c2 is not None:
                    product(c2, 0)
                    product(c2, 1)
                if c3 is not None:
                    backward_half(c3, 0)
                if c1 is not None:
                    centre(c1)
                solve_part(i, 0)
                if c2 is not None:
                    product(c2, 2)
                if c3 is not None:
                    backward_half(c3, 1)
                if c1 is not None:
                    normalised(c1)
                solve_part(i, 1)
                if c2 is not None:
                    product(c2, 3)
                if c1 is not None:
                    difference(c1)
                if c2 is not None:
                    scan(c2)
                if c3 is not None:
                    backward_half(c3, 2)
                solve_part(i, 2)
                if c2 is not None:
                    gated(c2)
                    product(c2, 4)
                    clip(c2)
                if c3 is not None:
                    backward_half(c3, 3)
                solve_part(i, 3)

            eliminate(1, T * 8 // 12, T)
            scale_rows(1)

            c1p, c2p = pair_of(1), (pair_of(0), pair_of(2))
            phase_a_over(dve)
            dve.wait_ge(ffnw_loaded, 16 * 7)
            tt(aij[:, :], alph_s[:, 0:1], alph_s[:, 1:2], ALU.mult).then_inc(prep_done, 1)
            dve.wait_ge(prep_done, 5)
            ts(adin[:, :], din_s[:, :], aij[:, 0:1], None, ALU.mult).then_inc(ffn_prep, 1)
            dve.wait_ge(ffn_made, 1)
            for half in range(2):
                w = wfc_s[:, half, :].rearrange("p (n f) -> p n f", n=2)
                tt(w, w, c2p[half][0:HD, :, 0:FH // 2], ALU.mult)
            tt(wpr_s[:, 0:2, :], wpr_s[:, 0:2, :], c1p[:, :, 0:D], ALU.mult).then_inc(ffn_prep, 1)
            dve.wait_ge(ffn_made, 2)
            for j in range(2):
                w = wpr_s[:, 2 + 2 * j:4 + 2 * j, :]
                tt(w, w, c2p[j][:, :, 0:D], ALU.mult)
            tt(bfc_s[:, :], bfc_s[:, :], c1p[:, 0, 0:FC], ALU.mult)
            tt(bpr_s[:, :], bpr_s[:, :], c1p[0:1, 1, 0:D], ALU.mult).then_inc(ffn_prep, 1)

            def centre_y(c):
                dve.wait_ge(c1_made, ringc1.made(("gmean", c)))
                if c > 0:
                    dve.wait_ge(z_ready, c)
                dve.wait_ge(yT_ready, c + 1)
                tt(yc[:, :, :], yT[:, :, :], c1p[0:HD, :, 0:TC], ALU.subtract).then_inc(yc_ready, 1)

            def normalise_y(c):
                dve.wait_ge(rsc_ready, c + 1)
                tt(yc[:, :, :], yc[:, :, :], rsc[:, :, :], ALU.mult).then_inc(yn_ready, 1)

            def residual(c):
                dve.wait_ge(c2_made, ringc2.made(("wo", c)))
                dve.wait_ge(hin_loaded, 16 * (c + 1))
                if c > 0:
                    dve.wait_ge(c2_made, ringc2.made(("proj", c - 1)))
                tt(h1[:, :, :], hin[:, :, :], c2p[ringc2.slot(("wo", c))][0:HD, :, 0:TC], ALU.add).then_inc(h1_ready, 1)

            def centre_h(c):
                dve.wait_ge(c2_made, ringc2.made(("lmean", c)))
                if c > 0:
                    dve.wait_ge(sq2_ready, c)
                tt(hc[:, :, :], h1[:, :, :], c2p[ringc2.slot(("lmean", c))][0:HD, 0:1, 0:TC].broadcast_to([HD, 2, TC]),
                   ALU.subtract).then_inc(hc_ready, 1)

            def normalise_h(c):
                dve.wait_ge(rs2_ready, c + 1)
                if c > 0:
                    dve.wait_ge(c2_made, ringc2.made(("fc", c - 1, FC // 2 - 1)))
                tt(hn[:, :, :], hc[:, :, :], rs2[:, :].unsqueeze(1).broadcast_to([HD, 2, TC]), ALU.mult
                   ).then_inc(hn_ready, 1)

            def copy_out(c):
                dve.wait_ge(c2_made, ringc2.made(("proj", c)))
                if c > 0:
                    dve.wait_ge(out_stored, 16 * 3 * c)
                src = c2p[ringc2.slot(("proj", c))]
                for n, _, nt in tokens(c):
                    last = nc.vector.tensor_copy(osb[0:nt, n, :], src[0:nt, n // 2, D * (n % 2):D * (n % 2 + 1)])
                last.then_inc(osb_ready, 1)

            first_late = next(c for c in range(NC) if need(c) == NG - 1)
            prepare(NG - 1)
            parts = 2 * first_late

            def last_group_part(n):
                eliminate(NG - 1, T * n // parts, T * (n + 1) // parts)
                if n == parts - 1:
                    scale_rows(NG - 1)
                    back_substitute(NG - 1)

            for j1, j2 in c_iterations():
                if j1 is not None:
                    if j1 < first_late:
                        last_group_part(2 * j1)
                if j2 is not None:
                    residual(j2)
                    centre_h(j2)
                if j1 is not None:
                    centre_y(j1)
                if j2 is not None:
                    normalise_h(j2)
                if j1 is not None:
                    normalise_y(j1)
                    if j1 < first_late:
                        last_group_part(2 * j1 + 1)
                if j2 is not None:
                    copy_out(j2)


def kernel(**inputs):
    import concourse.bacc as bacc
    from concourse.bass_utils import run_bass_kernel_spmd as run

    a = {k: np.asarray(v) for k, v in inputs.items()}

    def halves(v):
        v = v.reshape(v.shape[:-1] + (2, HD))
        return np.moveaxis(v, -1, 0)

    def rows(w):
        return w.reshape(2, HD, -1).transpose(1, 0, 2)

    x = a["x"].reshape(B, CH, HP, PATCH, HP, PATCH).transpose(0, 2, 4, 1, 3, 5)
    maa = np.stack([a["L0_attn_time_maa_" + n].reshape(D) for n in "xwkvrg"])
    par = (np.arange(HD)[:, None] // K % 2 == np.arange(2)[None, :]).astype(np.float32)
    chan = np.concatenate([
        halves(a["L0_tok_b"]), halves(a["cls_tok"].reshape(D)), halves(maa).reshape(HD, 12),
        halves(a["L0_attn_time_decay"].reshape(D)), halves(a["L0_attn_ln_w"]), halves(a["L0_attn_ln_b"]), par,
        halves(a["L0_tok_pos"].reshape(NPT, D)).transpose(0, 2, 1).reshape(HD, 2 * NPT)], axis=1)
    heads = np.arange(HD) // K
    p = np.arange(128)
    w2 = a["L0_attn_maa_w2"]
    token = np.arange(TC) % T
    arrays = {
        "patches": x.reshape(NC, PC, FK, 128).transpose(0, 3, 2, 1),
        "chan": chan,
        "wtok": a["L0_tok_W"].T.reshape(FK, 128, D).transpose(1, 0, 2),
        "w1": rows(a["L0_attn_maa_w1"]),
        "w2a": w2[0:4].reshape(128, D), "w2b": w2[4],
        "dw1": rows(a["L0_attn_decay_w1"]), "dw2": a["L0_attn_decay_w2"],
        "wkvrg": np.stack([rows(a["L0_attn_W" + n]) for n in "kvrg"], axis=1),
        "wo": rows(a["L0_attn_Wo"]),
        "wfc": rows(a["L0_ffn_w_fc"].T), "bfc": a["L0_ffn_b_fc"].reshape(FC, 128).T,
        "wproj": a["L0_ffn_w_proj"].T.reshape(FC, 128, D).transpose(1, 0, 2), "bproj": a["L0_ffn_b_proj"].reshape(1, D),
        "alphas": np.stack([np.repeat(a["L0_ffn_alpha_e"], len(RATIOS)), np.tile(a["L0_ffn_alpha_r"], len(EMBEDS))], axis=1),
        "lucid": np.tile(a["L0_attn_lucid_temp"].reshape(H), B // 2).reshape(NG, NSYS).T,
        "ident": np.eye(128, dtype=np.float32),
        "blocks": np.stack([np.full((HD, HD), 1.0 / D), (heads[:, None] == heads[None, :]) / K], axis=1).astype(np.float32),
        "tri": (np.arange(T)[None, :] < p[:, None] % TP).astype(np.uint32),
        "scanmask": np.broadcast_to((token > 0).astype(np.float32), (HD, TC)),
        "din": np.array([[d < e for d in range(D)] for e in EMBEDS for _ in RATIOS], np.float32),
        "hout": np.array([[f < r * e for f in range(FH)] for e in EMBEDS for r in RATIOS], np.float32),
    }
    arrays = {k: np.ascontiguousarray(v) for k, v in arrays.items()}
    nc = bacc.Bacc("TRN2", target_bir_lowering=False, num_devices=1)
    aps = {k: nc.dram_tensor(f"in_{k}", v.shape, mybir.dt.from_np(v.dtype), kind="ExternalInput").ap()
           for k, v in arrays.items()}
    o = nc.dram_tensor("out_0", (B, T, D), F32, kind="ExternalOutput").ap()
    vit_tower(nc, **aps, out=o.rearrange("b t d -> (b t) d"))
    r = run(nc, [{f"in_{k}": v for k, v in arrays.items()}], core_ids=[0])
    return r.results[0]["out_0"]
```

```python
from contextlib import ExitStack

import numpy as np

import concourse.bass as bass
from concourse import mybir
from concourse.alu_op_type import AluOpType as ALU

F32 = mybir.dt.float32
U32 = mybir.dt.uint32
ACT = mybir.ActivationFunctionType

B, CH, IMG, PATCH, D = 64, 3, 96, 16, 192
HP = IMG // PATCH
NPT = HP * HP
T = NPT + 1
MID = T // 2
H, K = 12, 16
HD = D // 2
FK = CH * PATCH * PATCH // 128
NB = 8
NC = B // NB
TC = NB * T
PC = NB * NPT
PP = NB // 2
TP = 64
Q = HD // 32
NMIX, MR = 5, 32
DDEC = 64
HT = H * T
NSYS = 128
NG = B // 2 * H // NSYS
GR = 2 * NSYS
W = T + K
FH = 4 * D
FC = FH // 128
LN_EPS = 1e-5
GN_EPS = 1e-5 * 64.0
EMBEDS, RATIOS = (96, 144, 192), (2, 3, 4)
NA = len(EMBEDS) * len(RATIOS)
MW, MK, MV, MRR, MG = range(5)
MIXES = (MW, MV, MG, MK, MRR)

V_TOKB, V_CLS, V_MAA, V_TD, V_LNW, V_LNB, V_PAR, V_POS = 0, 2, 4, 16, 18, 20, 22, 24
V_N = V_POS + 2 * NPT


def group_chunk(g):
    return -(-(NSYS * (g + 1)) // (H * PP)) - 1


def pieces(first, n):
    a = first % GR
    m = min(n, GR - a)
    return [(a, 0, m)] + ([(0, m, n - m)] if m < n else [])


def bands(m):
    n = 3 if m >= 24 else 2 if m >= 10 else 1
    cuts = [m * j // n for j in range(n + 1)]
    return list(zip(cuts[:-1], cuts[1:]))


def cuts(n, work):
    total, done, out = sum(work), 0, [0]
    for i, w in enumerate(work):
        done += w
        while len(out) <= n and done * n >= total * len(out):
            out.append(i + 1)
    return out


def pivot_steps():
    out = [(0, "recip", 0), (0, "scale", 0)]
    for k in range(T - 1):
        n = len(bands(T - 1 - k))
        out += [(k, "outer", b) for b in range(n)] + [(k, "subtract", b) for b in range(min(n, 2))]
        out += [(k + 1, "recip", 0)] + [(k, "subtract", b) for b in range(2, n)]
        if k + 1 < T - 1:
            out += [(k + 1, "scale", 0)]
    return out


STEPS = pivot_steps()
STEP_AT = {step: n for n, step in enumerate(STEPS)}


def step_work(k, kind, band):
    if kind in ("recip", "scale"):
        return 100
    r0, r1 = bands(T - 1 - k)[band]
    return 70 + 2 * (r1 - r0) * (W - k - 1 - r0)


STEP_WORK = [step_work(*step) for step in STEPS]
BACK_WORK = [k for k in range(T - 1, 0, -1)]


class Ring:

    def __init__(self, slots):
        self.slots, self.tasks, self.index = slots, [], {}

    def add(self, key, read):
        self.index[key] = len(self.tasks)
        self.tasks.append(read)

    def slot(self, key):
        return self.index[key] % self.slots

    def made(self, key):
        return self.index[key] + 1

    def before(self, key):
        n = self.index[key] - self.slots
        return self.tasks[n] if n >= 0 else None


def vit_tower(nc, patches, chan, wtok, w1, w2a, w2b, dw1, dw2, wkvrg, wo, wfc, bfc, wproj, bproj, alphas,
              lucid, ident, blocks, tri, scanmask, din, hout, out):
    h_dram = nc.dram_tensor("h_spill", (NC, HD, 2 * TC), F32, kind="Internal").ap()
    gate_dram = nc.dram_tensor("gate_spill", (NC, HD, 2 * TC), F32, kind="Internal").ap()
    at_dram = nc.dram_tensor("at_spill", (NC, 2, T, PP * HT), F32, kind="Internal").ap()

    ctx = ExitStack()
    with ctx:
        def sem(name):
            return ctx.enter_context(nc.semaphore(name))

        def sb(name, shape, dt=F32, where=ctx):
            return where.enter_context(nc.sbuf_tensor(name, shape, dt))

        chan_s = sb("chan_s", [HD, V_N])
        wtok_s = sb("wtok_s", [128, FK, D])
        w1_s = sb("w1_s", [HD, 2, NMIX * MR])
        w2a_s = sb("w2a_s", [128, D])
        w2b_s = sb("w2b_s", [MR, D])
        dw1_s = sb("dw1_s", [HD, 2, DDEC])
        dw2_s = sb("dw2_s", [DDEC, D])
        wproj4_s = sb("wproj4_s", [HD, 4, 2, D])
        wo_s = sb("wo_s", [HD, 2, D])
        ident_s = sb("ident_s", [128, 128])
        blocks_s = sb("blocks_s", [HD, 2, HD])
        tri_s = sb("tri_s", [128, T], U32)
        scan_s = sb("scan_s", [HD, TC])
        lucid_s = sb("lucid_s", [NSYS, NG])
        temp = sb("temp", [NSYS, NG])
        tmp3 = sb("tmp3", [NSYS, 2, NG])
        eps_s = sb("eps_s", [128, 2])
        posb = sb("posb", [HD, 2, NPT])
        gram = sb("gram", [128, GR * T])
        vring = sb("vring", [128, GR * K])
        sysm = sb("sysm", [NSYS, 2, 2, T, W])
        nrm = sb("nrm", [NSYS, 2, T])
        rdiag = sb("rdiag", [NSYS, 2, 2, T])
        outer = sb("outer", [NSYS, 2880])
        outer_b = sb("outer_b", [NSYS, 2 * (T - 1) * K])

        gram_v = gram[:, :].rearrange("p (s t) -> p s t", t=T)
        v_v = vring[:, :].rearrange("p (s k) -> p s k", k=K)

        actx = ExitStack()

        def sa(name, shape, dt=F32):
            return sb(name, shape, dt, actx)
        pat = sa("pat", [128, FK, PC])
        hbuf = sa("hbuf", [HD, 2, TC])
        xc = sa("xc", [HD, 2, TC])
        rstd = sa("rstd", [HD, TC])
        xpad = sa("xpad", [HD, 2, 2, NB, T + 2])
        dx = sa("dx", [HD, 2, 2, TC])
        xxx = sa("xxx", [HD, 2, TC])
        sq = xxx
        m_a = sa("m_a", [128, TC])
        m_b = sa("m_b", [MR, TC])
        prod = sa("prod", [HD, 2, 2, TC])
        xs = sa("xs", [HD, 2, 2, TC])
        xv = sa("xv", [HD, 2, NB, TP])
        dect = sa("dect", [DDEC, TC])
        ew = sa("ew", [HD, 2, TC])
        cs = sa("cs", [HD, 2, TC])
        cb = sa("cb", [HD, 2, TC])
        ex = sa("ex", [HD, 2, 2, TC])
        kp = sa("kp", [HD, 2, TC + TP - T])
        kpar = sa("kpar", [HD, 2, 2, TC])
        rpar = sa("rpar", [HD, 2, 2, TC])
        ke = sa("ke", [HD, 2, 2, TC + TP - T])
        re = sa("re", [HD, 2, 2, 2, TC])
        th = sa("th", [HD, 2, TC])
        gate = th
        at = sa("at", [128, PP, HT])
        actx.close()

        cctx = ExitStack()

        def sc(name, shape, dt=F32):
            return sb(name, shape, dt, cctx)
        wfc_s = sc("wfc_s", [HD, 2, FH])
        wpr_s = sc("wpr_s", [128, FC, D])
        bfc_s = sc("bfc_s", [128, FC])
        bpr_s = sc("bpr_s", [1, D])
        alph_s = sc("alph_s", [NA, 2])
        aij = sc("aij", [NA, 1])
        din_s = sc("din_s", [NA, D])
        hout_s = sc("hout_s", [NA, FH])
        adin = sc("adin", [NA, D])
        ones_s = sc("ones_s", [1, 128])
        xpose = sc("xpose", [NSYS, K, 2, TP])
        pv = sc("pv", [128, NG, NSYS, K])
        atc = sc("atc", [128, PP, HT + TP - T])
        ysb = sc("ysb", [128, PP, D])
        yT = sc("yT", [HD, 2, TC])
        yc = sc("yc", [HD, 2, TC])
        sqc = sc("sqc", [HD, 2, TC])
        rsc = sc("rsc", [HD, 2, TC])
        gin = sc("gin", [HD, 2, TC])
        z = sc("z", [HD, 2, 2, TC])
        hin = sc("hin", [HD, 2, TC])
        hc = sc("hc", [HD, 2, TC])
        sq2 = sc("sq2", [HD, 2, TC])
        rs2 = sc("rs2", [HD, TC])
        hact = gram[:, 0:FC * TC].rearrange("p (f t) -> p f t", f=FC)
        at_ = FC * TC
        osb = gram[:, at_:at_ + 3 * D].rearrange("p (n d) -> p n d", n=3)
        at_ += 3 * D
        h1 = gram[0:HD, at_:at_ + 4 * TC].rearrange("p (n a t) -> p n a t", n=2, a=2)
        at_ += 4 * TC
        hn = gram[0:HD, at_:at_ + 4 * TC].rearrange("p (n a t) -> p n a t", n=2, a=2)
        cctx.close()

        bank = [ctx.enter_context(nc.psum_tensor(f"bank{i}", [128, 1024], F32)) for i in range(4)]
        def pair_of(i):
            return bank[i][:, :].rearrange("p (h c) -> p h c", h=2)

        chan_loaded, wtok_loaded, w_loaded = sem("chan_loaded"), sem("wtok_loaded"), sem("w_loaded")
        memset_done, prep_done, temp_act, temp_ready = sem("memset_done"), sem("prep_done"), sem("temp_act"), sem("temp_ready")
        pat_loaded, h_ready, h_spilled = sem("pat_loaded"), sem("h_ready"), sem("h_spilled")
        xc_ready, sq_ready, rstd_log, rstd_ready = sem("xc_ready"), sem("sq_ready"), sem("rstd_log"), sem("rstd_ready")
        xn_ready, nbr_ready, dx_ready, xxx_ready = sem("xn_ready"), sem("nbr_ready"), sem("dx_ready"), sem("xxx_ready")
        m_ready, prod_ready, xs_ready = sem("m_ready"), sem("prod_ready"), sem("xs_ready")
        dect_ready, ew_ready, cs_ready = sem("dect_ready"), sem("ew_ready"), sem("cs_ready")
        cdiff_ready, clip_ready, e_ready = sem("cdiff_ready"), sem("clip_ready"), sem("e_ready")
        k_ready, r_ready, v_ready = sem("k_ready"), sem("r_ready"), sem("v_ready")
        th_ready, gate_ready, gate_spilled = sem("th_ready"), sem("gate_ready"), sem("gate_spilled")
        decayed_ready, f_ready = sem("decayed_ready"), sem("f_ready")
        at_ready, at_spilled = sem("at_ready"), sem("at_spilled")
        ring1_made, ring2_made, aux_made = sem("ring1_made"), sem("ring2_made"), sem("aux_made")
        sys_filled = sem("sys_filled")
        prep_dve, prep_act = sem("prep_dve"), sem("prep_act")
        elim_step = sem("elim_step")
        back_step = sem("back_step")
        xpose_ready, pv_ready = sem("xpose_ready"), sem("pv_ready")
        ffnw_loaded, c_memset, ffn_made, ffn_prep = sem("ffnw_loaded"), sem("c_memset"), sem("ffn_made"), sem("ffn_prep")
        at_loaded, gate_loaded, hin_loaded = sem("at_loaded"), sem("gate_loaded"), sem("hin_loaded")
        c1_made, c2_made = sem("c1_made"), sem("c2_made")
        y_ready, yT_ready, yc_ready, sqc_ready, rsc_log, rsc_ready = (sem("y_ready"), sem("yT_ready"), sem("yc_ready"),
                                                                      sem("sqc_ready"), sem("rsc_log"), sem("rsc_ready"))
        yn_ready, affine_ready, z_ready = sem("yn_ready"), sem("affine_ready"), sem("z_ready")
        h1_ready, hc_ready, sq2_ready, rs2_log, rs2_ready = (sem("h1_ready"), sem("hc_ready"), sem("sq2_ready"),
                                                             sem("rs2_log"), sem("rs2_ready"))
        hn_ready, hact_ready, osb_ready, out_stored = sem("hn_ready"), sem("hact_ready"), sem("osb_ready"), sem("out_stored")

        NTG, NTV = -(-T // 4), K // 4
        NFILL = NTG + NTV

        SLOTS = 12
        SOLVE_AT = {0: (5, 3 * SLOTS, 3 * SLOTS), 1: (8, 2 * SLOTS, 5 * SLOTS // 2)}
        SEGMENTS = ((0, 2), (2, 5), (5, 8))

        def c_iterations(segment):
            first, end = SEGMENTS[segment]
            for j in range(first, end + 2):
                yield tuple(j - d if first <= j - d < end else None for d in range(3))

        def iteration(i):
            return (i if i < NC else None, i - 1 if 0 <= i - 1 < NC else None, i - 2 if 0 <= i - 2 < NC else None)

        def completed(c3):
            return next((g for g in range(NG) if group_chunk(g) == c3), None)

        def mix_count(c, n):
            return NMIX * c + n + 1

        def heads_count(c, p, q):
            return Q * (PP * c + p) + q + 1

        ring1, ring2, aux = Ring(1), Ring(2), Ring(2)
        for i in range(NC + 2):
            c1, c2, c3 = iteration(i)
            if c1 is not None:
                ring1.add(("embed", c1), (h_ready, 2 * c1 + 2))
                ring1.add(("mean", c1), (xc_ready, c1 + 1))
                ring1.add(("var", c1), (rstd_log, c1 + 1))
                ring1.add(("w1", c1), (m_ready, c1 + 1))
            if c2 is not None:
                reads = {"dec1": (dect_ready, c2 + 1), "dec2": (ew_ready, c2 + 1), "v": (v_ready, c2 + 1),
                         "g": (gate_ready, c2 + 1), "k": (k_ready, c2 + 1), "r": (r_ready, c2 + 1)}
                for what in ((0, 1, "dec1", 2, "v", 3, "dec2", "g", 4, "k", "r")):
                    if isinstance(what, int):
                        ring2.add(("mix", c2, what), (prod_ready, mix_count(c2, what)))
                    else:
                        ring2.add((what, c2), reads[what])
            if c3 is not None:
                for p in range(PP):
                    for q in range(Q):
                        aux.add(("heads", c3, p, q), (at_ready, heads_count(c3, p, q)))
                g = completed(c3)
                if g is not None:
                    for j in range(NFILL):
                        aux.add(("fill", g, j), (sys_filled, NFILL * g + j + 1))
        ringc1, ringc2 = Ring(1), Ring(3)
        for seg in range(len(SEGMENTS)):
            for j in range(NTV // 2):
                ringc1.add(("solution", seg, j), (pv_ready, NTV // 2 * seg + j + 1))
            for d1, d2, d3 in c_iterations(seg):
                if d1 is not None:
                    ringc1.add(("y", d1), (y_ready, d1 + 1))
                if d2 is not None:
                    ringc2.add(("wo", d2), (h1_ready, d2 + 1))
                if d3 is not None:
                    ringc2.add(("fc", d3, 0), (hact_ready, FC // 2 * d3 + 1))
                if d1 is not None:
                    ringc1.add(("yT", d1), (yT_ready, d1 + 1))
                if d2 is not None:
                    ringc2.add(("lmean", d2), (hc_ready, d2 + 1))
                if d3 is not None:
                    ringc2.add(("fc", d3, 1), (hact_ready, FC // 2 * d3 + 2))
                if d1 is not None:
                    ringc1.add(("gmean", d1), (yc_ready, d1 + 1))
                if d2 is not None:
                    ringc2.add(("lvar", d2), (rs2_log, d2 + 1))
                if d3 is not None:
                    ringc2.add(("fc", d3, 2), (hact_ready, FC // 2 * d3 + 3))
                if d1 is not None:
                    ringc1.add(("gvar", d1), (rsc_log, d1 + 1))
                if d3 is not None:
                    ringc2.add(("proj", d3), (osb_ready, d3 + 1))

        elim_at = {}
        count = 0
        for g in range(NG):
            elim_at[g, "start"] = count
            count += len(STEPS) + 1
            elim_at[g, "scaled"] = count
            if g == NG - 1:
                count += 2 * (T - 1)
                elim_at[g, "solved"] = count
        back_at = {g: 2 * (T - 1) * (g + 1) for g in range(NG - 1)}

        def wait_free(eng, ring, key):
            read = ring.before(key)
            if read is not None:
                eng.wait_ge(*read)

        def wait_solved(eng, g):
            if g < NG - 1:
                eng.wait_ge(back_step, back_at[g])
            else:
                eng.wait_ge(elim_step, elim_at[g, "solved"])

        def phase_a_over(eng):
            eng.wait_ge(ring1_made, len(ring1.tasks))
            eng.wait_ge(ring2_made, len(ring2.tasks))
            eng.wait_ge(aux_made, aux.made(("heads", NC - 1, PP - 1, Q - 1)))
            eng.wait_ge(decayed_ready, 4 * NC)
            eng.wait_ge(at_ready, Q * PP * NC)
            eng.wait_ge(r_ready, NC)
            eng.wait_ge(e_ready, 4 * NC)
            eng.wait_ge(clip_ready, 2 * NC)
            eng.wait_ge(gate_ready, NC)
            eng.wait_ge(h_spilled, 16 * NC)
            eng.wait_ge(gate_spilled, 16 * NC)
            eng.wait_ge(at_spilled, 32 * NC)

        def need(c):
            return next(g for g in range(NG) if NSYS * (g + 1) >= H * PP * (c + 1))

        def tokens(c):
            return [(n, 128 * n, min(128, TC - 128 * n)) for n in range(-(-TC // 128))]

        block = ctx.enter_context(nc.Block())

        @block.sync
        def _(sp):
            sp.dma_start(chan_s[:, :], chan).then_inc(chan_loaded, 16)
            sp.dma_start(pat[:, :, :], patches[0]).then_inc(pat_loaded, 16)
            sp.dma_start(wtok_s[:, :, :], wtok).then_inc(wtok_loaded, 16)
            for dst, src in ((blocks_s[:, :, :], blocks), (w1_s[:, :, :], w1), (w2a_s[:, :], w2a), (w2b_s[:, :], w2b),
                             (dw1_s[:, :, :], dw1), (dw2_s[:, :], dw2), (wproj4_s[:, :, :, :], wkvrg),
                             (scan_s[:, :], scanmask), (tri_s[:, :], tri), (ident_s[:, :], ident),
                             (lucid_s[:, :], lucid), (wo_s[:, :, :], wo)):
                sp.dma_start(dst, src).then_inc(w_loaded, 16)
            for i in range(NC + 2):
                c1, c2, c3 = iteration(i)
                if c1 is not None:
                    if c1 + 1 < NC:
                        sp.wait_ge(ring1_made, ring1.made(("embed", c1)))
                        sp.dma_start(pat[:, :, :], patches[c1 + 1]).then_inc(pat_loaded, 16)
                    sp.wait_ge(h_ready, 2 * c1 + 2)
                    sp.dma_start(h_dram[c1], hbuf[:, :, :].rearrange("p a t -> p (a t)")).then_inc(h_spilled, 16)
                if c2 is not None:
                    sp.wait_ge(gate_ready, c2 + 1)
                    sp.dma_start(gate_dram[c2], gate[:, :, :].rearrange("p a t -> p (a t)")).then_inc(gate_spilled, 16)
                if c3 is not None:
                    sp.wait_ge(at_ready, Q * PP * (c3 + 1))
                    for b2 in range(2):
                        sp.dma_start(at_dram[c3, b2], at[TP * b2:TP * b2 + T, :, :].rearrange("p a t -> p (a t)")
                                     ).then_inc(at_spilled, 16)
            phase_a_over(sp)
            for dst, src in ((wfc_s[:, :, :], wfc), (wpr_s[:, :, :], wproj), (bfc_s[:, :], bfc), (bpr_s[:, :], bproj),
                             (alph_s[:, :], alphas), (din_s[:, :], din), (hout_s[:, :], hout)):
                sp.dma_start(dst, src).then_inc(ffnw_loaded, 16)
            sp.wait_ge(c_memset, 1)
            for seg in range(len(SEGMENTS)):
                for d1, d2, d3 in c_iterations(seg):
                    if d1 is not None:
                        if d1 > 0:
                            sp.wait_ge(c1_made, ringc1.made(("y", d1 - 1)))
                        for b2 in range(2):
                            sp.dma_start(atc[TP * b2:TP * b2 + T, :, 0:HT],
                                         at_dram[d1, b2].rearrange("p (a t) -> p a t", a=PP)).then_inc(at_loaded, 16)
                        if d1 > 0:
                            sp.wait_ge(z_ready, d1)
                        sp.dma_start(gin[:, :, :].rearrange("p a t -> p (a t)"), gate_dram[d1]).then_inc(gate_loaded, 16)
                        if d1 > 0:
                            sp.wait_ge(h1_ready, d1)
                        sp.dma_start(hin[:, :, :].rearrange("p a t -> p (a t)"), h_dram[d1]).then_inc(hin_loaded, 16)
                    if d3 is not None:
                        sp.wait_ge(osb_ready, d3 + 1)
                        for n, t0, nt in tokens(d3):
                            sp.dma_start(out[TC * d3 + t0:TC * d3 + t0 + nt, :], osb[0:nt, n, :]).then_inc(out_stored, 16)
            sp.wait_ge(out_stored, 16 * NC * len(tokens(0)))

        @block.tensor
        def _(pe):
            def mm(o, l, r, start=True, stop=True, at_tile=None):
                if at_tile is None:
                    return nc.tensor.matmul(o, l, r, start=start, stop=stop)
                return nc.tensor.matmul(o, l, r, start=start, stop=stop, tile_position=at_tile)

            r1 = pair_of(0)

            def two_halves(o, w, x):
                mm(o, w[:, 0], x[:, 0], True, False)
                return mm(o, w[:, 1], x[:, 1], False, True)

            def embed(c):
                pe.wait_ge(pat_loaded, 16 * (c + 1))
                wait_free(pe, ring1, ("embed", c))
                for half in range(2):
                    for f in range(FK):
                        last = mm(r1[0:HD, half, 0:PC], wtok_s[:, f, HD * half:HD * (half + 1)], pat[:, f, :],
                                  f == 0, f == FK - 1)
                last.then_inc(ring1_made, 1)

            def mean(c):
                pe.wait_ge(h_ready, 2 * c + 2)
                wait_free(pe, ring1, ("mean", c))
                mm(r1[0:HD, 0, 0:TC], blocks_s[:, 0, :], hbuf[:, 0, :], True, False)
                mm(r1[0:HD, 0, 0:TC], blocks_s[:, 0, :], hbuf[:, 1, :], False, True).then_inc(ring1_made, 1)

            def var(c):
                pe.wait_ge(sq_ready, c + 1)
                wait_free(pe, ring1, ("var", c))
                mm(r1[0:HD, 0, 0:TC], blocks_s[:, 0, :], sq[:, 0, :], True, False)
                mm(r1[0:HD, 0, 0:TC], blocks_s[:, 0, :], sq[:, 1, :], False, True).then_inc(ring1_made, 1)

            def lora_in(c):
                pe.wait_ge(xxx_ready, c + 1)
                wait_free(pe, ring1, ("w1", c))
                two_halves(r1[:, 0, 0:TC], w1_s[:, :, 0:128], xxx)
                two_halves(r1[0:MR, 1, 0:TC], w1_s[:, :, 128:128 + MR], xxx).then_inc(ring1_made, 1)

            def slot2(key):
                return pair_of(1 + ring2.slot(key))

            def mix(c, n):
                key, m = ("mix", c, n), MIXES[n]
                if n == 0:
                    pe.wait_ge(m_ready, c + 1)
                wait_free(pe, ring2, key)
                w2, mt, row = (w2a_s, m_a, MR * m) if m < 4 else (w2b_s, m_b, 0)
                for half in range(2):
                    last = mm(slot2(key)[0:HD, half, 0:TC], w2[row:row + MR, HD * half:HD * (half + 1)],
                              mt[row:row + MR, :], at_tile=(row, 0))
                last.then_inc(ring2_made, 1)

            def decay_in(c):
                pe.wait_ge(xs_ready, mix_count(c, 0))
                wait_free(pe, ring2, ("dec1", c))
                two_halves(slot2(("dec1", c))[0:DDEC, 0, 0:TC], dw1_s, xs[:, 0]).then_inc(ring2_made, 1)

            def decay_out(c):
                pe.wait_ge(dect_ready, c + 1)
                wait_free(pe, ring2, ("dec2", c))
                for half in range(2):
                    last = mm(slot2(("dec2", c))[0:HD, half, 0:TC], dw2_s[:, HD * half:HD * (half + 1)], dect[:, :])
                last.then_inc(ring2_made, 1)

            def project(c, what):
                n, w, x = {"k": (3, 0, 0), "r": (4, 2, 1), "g": (2, 3, 1)}[what]
                pe.wait_ge(xs_ready, mix_count(c, n))
                wait_free(pe, ring2, (what, c))
                for half in range(2):
                    last = two_halves(slot2((what, c))[0:HD, half, 0:TC],
                                      wproj4_s[:, w, :, HD * half:HD * (half + 1)], xs[:, x])
                last.then_inc(ring2_made, 1)

            def project_v(c):
                pe.wait_ge(xs_ready, mix_count(c, 1))
                wait_free(pe, ring2, ("v", c))
                for p in range(PP):
                    o = slot2(("v", c))[:, p // 2, D * (p % 2):D * (p % 2 + 1)]
                    for half in range(2):
                        last = mm(o, xv[:, half, 2 * p:2 * p + 2, :].rearrange("p b t -> p (b t)"),
                                  wproj4_s[:, 1, half, :], half == 0, half == 1)
                last.then_inc(ring2_made, 1)

            def aux_bank(key):
                s = aux.slot(key)
                return bank[3][:, 512 * s:512 * (s + 1)]

            def head_matrices(c, p):
                for q in range(Q):
                    key, row = ("heads", c, p, q), 32 * q
                    if p == 0 and q == 0:
                        pe.wait_ge(k_ready, c + 1)
                        pe.wait_ge(decayed_ready, 4 * c + 4)
                    wait_free(pe, aux, key)
                    o = aux_bank(key)
                    for n, (left, right) in enumerate(((kp, kpar), (ke[:, 0], re[:, 0]), (ke[:, 1], re[:, 1]))):
                        for b2 in range(2):
                            t0 = T * (2 * p + b2)
                            for half in range(2):
                                col = 2 * T * (2 * n + half)
                                last = mm(o[TP * b2:TP * (b2 + 1), col:col + 2 * T], left[row:row + 32, half, t0:t0 + TP],
                                          right[row:row + 32, :, half, t0:t0 + T], at_tile=(row, TP * b2))
                    last.then_inc(aux_made, 1)

            def fill(g):
                base = NSYS * (g % 2)
                for j in range(NFILL):
                    key = ("fill", g, j)
                    wait_free(pe, aux, key)
                    if j == 0:
                        pe.wait_ge(f_ready, Q * PP * (group_chunk(g) + 1))
                    if j == NTG:
                        pe.wait_ge(v_ready, group_chunk(g) + 1)
                    for n in range(4):
                        if j < NTG and 4 * j + n < T:
                            src = gram_v[:, base:base + NSYS, 4 * j + n]
                        elif j >= NTG:
                            src = v_v[:, base:base + NSYS, 4 * (j - NTG) + n]
                        else:
                            break
                        last = nc.tensor.transpose(aux_bank(key)[:, 128 * n:128 * (n + 1)], src, ident_s[:, :])
                    last.then_inc(aux_made, 1)

            pe.wait_ge(wtok_loaded, 16)
            for i in range(NC + 2):
                c1, c2, c3 = iteration(i)
                if c1 is not None:
                    embed(c1)
                    if c1 == 0:
                        pe.wait_ge(w_loaded, 16 * 12)
                if c2 is not None:
                    mix(c2, 0)
                    mix(c2, 1)
                if c3 is not None:
                    head_matrices(c3, 0)
                if c1 is not None:
                    mean(c1)
                if c2 is not None:
                    decay_in(c2)
                    mix(c2, 2)
                if c3 is not None:
                    head_matrices(c3, 1)
                if c1 is not None:
                    var(c1)
                if c2 is not None:
                    project_v(c2)
                    mix(c2, 3)
                    decay_out(c2)
                if c3 is not None:
                    head_matrices(c3, 2)
                if c2 is not None:
                    project(c2, "g")
                    mix(c2, 4)
                if c3 is not None:
                    head_matrices(c3, 3)
                if c1 is not None:
                    lora_in(c1)
                if c2 is not None:
                    project(c2, "k")
                    project(c2, "r")
                g = None if c3 is None else completed(c3)
                if g is not None:
                    fill(g)

            c1p, c2p = pair_of(1), (pair_of(0), pair_of(2), pair_of(3))
            pe.wait_ge(ffn_prep, 1)
            pe.wait_ge(ffnw_loaded, 16 * 7)
            phase_a_over(pe)
            for half in range(2):
                o = c2p[half]
                for n in range(2):
                    last = mm(o[0:HD, n, 0:FH // 2], adin[:, HD * half:HD * (half + 1)],
                              hout_s[:, FH // 2 * n:FH // 2 * (n + 1)])
            for n in range(2):
                last = mm(c1p[:, n, 0:D], hout_s[:, 128 * n:128 * (n + 1)], adin[:, :])
            last.then_inc(ffn_made, 1)
            pe.wait_ge(ffn_prep, 2)
            for n in range(2, FC):
                j = n - 2
                last = mm(c2p[j // 2][:, j % 2, 0:D], hout_s[:, 128 * n:128 * (n + 1)], adin[:, :])
            for n in range(FC):
                mm(c1p[:, 0, n:n + 1], hout_s[:, 128 * n:128 * (n + 1)], aij[:, :])
            mm(c1p[0:1, 1, 0:D], aij[:, :], din_s[:, :]).then_inc(ffn_made, 1)
            pe.wait_ge(ffn_prep, 3)

            def c1slot(key):
                wait_free(pe, ringc1, key)
                return c1p

            def c2slot(key):
                wait_free(pe, ringc2, key)
                return c2p[ringc2.slot(key)]

            def solution(g):
                for j in range(NTV // 2):
                    o = c1slot(("solution", g, j))
                    if j == 0:
                        pe.wait_ge(xpose_ready, g + 1)
                    for n in range(8):
                        last = nc.tensor.transpose(o[:, n // 4, 128 * (n % 4):128 * (n % 4 + 1)],
                                                   xpose[:, 8 * j + n, :, :].rearrange("p b t -> p (b t)"), ident_s[:, :])
                    last.then_inc(c1_made, 1)

            def apply_a(c):
                o = c1slot(("y", c))
                pe.wait_ge(at_loaded, 32 * (c + 1))
                pe.wait_ge(pv_ready, NTV // 2 * (need(c) + 1))
                for p in range(PP):
                    for b2 in range(2):
                        rows = slice(TP * b2, TP * b2 + T)
                        for h in range(H):
                            s = H * (PP * c + p) + h
                            last = mm(o[TP * b2:TP * (b2 + 1), p // 2, D * (p % 2) + K * h:D * (p % 2) + K * (h + 1)],
                                      atc[rows, p, T * h:T * h + TP], pv[rows, s // NSYS, s % NSYS, :],
                                      at_tile=(TP * b2, TP * b2))
                last.then_inc(c1_made, 1)

            def turn_y(c):
                pe.wait_ge(y_ready, c + 1)
                o = c1slot(("yT", c))
                for half in range(2):
                    for p in range(PP):
                        last = nc.tensor.transpose(o[0:HD, half, 128 * p:128 * (p + 1)],
                                                   ysb[:, p, HD * half:HD * (half + 1)], ident_s[:, :])
                last.then_inc(c1_made, 1)

            def per_head(c, key, ready, x):
                pe.wait_ge(ready, c + 1)
                o = c1slot((key, c))
                for half in range(2):
                    last = mm(o[0:HD, half, 0:TC], blocks_s[:, 1, :], x[:, half, :])
                last.then_inc(c1_made, 1)

            def attention_out(c):
                pe.wait_ge(z_ready, c + 1)
                o = c2slot(("wo", c))
                for half in range(2):
                    last = two_halves(o[0:HD, half, 0:TC], wo_s[:, :, HD * half:HD * (half + 1)], z[:, c % 2])
                last.then_inc(c2_made, 1)

            def per_token(c, key, ready, x):
                pe.wait_ge(ready, c + 1)
                o = c2slot((key, c))
                mm(o[0:HD, 0, 0:TC], blocks_s[:, 0, :], x[:, 0, :], True, False)
                mm(o[0:HD, 0, 0:TC], blocks_s[:, 0, :], x[:, 1, :], False, True).then_inc(c2_made, 1)

            def ffn_in(c, j):
                if j == 0:
                    pe.wait_ge(hn_ready, c + 1)
                o = c2slot(("fc", c, j))
                for n in range(2):
                    f = 2 * j + n
                    last = two_halves(o[:, n, 0:TC], wfc_s[:, :, 128 * f:128 * (f + 1)], hn[:, c % 2])
                last.then_inc(c2_made, 1)

            def ffn_out(c):
                o = c2slot(("proj", c))
                pe.wait_ge(hact_ready, FC // 2 * (c + 1))
                for n, t0, nt in tokens(c):
                    dst = o[0:nt, n // 2, D * (n % 2):D * (n % 2 + 1)]
                    for f in range(FC):
                        mm(dst, hact[:, f, t0:t0 + nt], wpr_s[:, f, :], f == 0, False)
                    for half in range(2):
                        mm(dst[:, HD * half:HD * (half + 1)], h1[:, c % 2, half, t0:t0 + nt], ident_s[0:HD, 0:HD], False, False)
                    last = mm(dst, ones_s[:, 0:nt], bpr_s[:, :], False, True)
                last.then_inc(c2_made, 1)

            for seg in range(len(SEGMENTS)):
                solution(seg)
                for d1, d2, d3 in c_iterations(seg):
                    if d1 is not None:
                        apply_a(d1)
                    if d2 is not None:
                        attention_out(d2)
                    if d3 is not None:
                        ffn_in(d3, 0)
                    if d1 is not None:
                        turn_y(d1)
                    if d2 is not None:
                        per_token(d2, "lmean", h1_ready, h1[:, d2 % 2])
                    if d3 is not None:
                        ffn_in(d3, 1)
                    if d1 is not None:
                        per_head(d1, "gmean", yT_ready, yT)
                    if d2 is not None:
                        per_token(d2, "lvar", sq2_ready, sq2)
                    if d3 is not None:
                        ffn_in(d3, 2)
                    if d1 is not None:
                        per_head(d1, "gvar", sqc_ready, sqc)
                    if d3 is not None:
                        ffn_out(d3)

        @block.scalar
        def _(act):
            r1, a = pair_of(0), nc.scalar.activation

            def slot2(key):
                return pair_of(1 + ring2.slot(key))

            def aux_bank(key):
                s = aux.slot(key)
                return bank[3][:, 512 * s:512 * (s + 1)]

            act.wait_ge(w_loaded, 16 * 12)
            nc.scalar.preload_act_table_set("natural_log_exp_and_others")
            a(tmp3[:, 0, :], lucid_s[:, :], ACT.Abs).then_inc(temp_act, 1)
            act.wait_ge(temp_act, 1)
            a(tmp3[:, 1, :], tmp3[:, 0, :], ACT.Exp, scale=-1.0).then_inc(temp_act, 1)
            act.wait_ge(temp_act, 2)
            act.wait_ge(memset_done, 1)
            a(tmp3[:, 0, :], tmp3[:, 1, :], ACT.Ln, bias=1.0).then_inc(temp_act, 1)

            def square(c):
                act.wait_ge(xc_ready, c + 1)
                if c > 0:
                    act.wait_ge(ring1_made, ring1.made(("w1", c - 1)))
                a(sq[:, :, :], xc[:, :, :], ACT.Square).then_inc(sq_ready, 1)

            def inverse_std(c):
                nc.scalar.preload_act_table_set("natural_log_exp_and_others")
                act.wait_ge(ring1_made, ring1.made(("var", c)))
                if c > 0:
                    act.wait_ge(xn_ready, c)
                a(rstd[:, :], r1[0:HD, 0, 0:TC], ACT.Ln, bias=eps_s[0:HD, 0:1]).then_inc(rstd_log, 1)
                act.wait_ge(rstd_log, c + 1)
                a(rstd[:, :], rstd[:, :], ACT.Exp, scale=-0.5).then_inc(rstd_ready, 1)

            def lora_tanh(c):
                act.wait_ge(ring1_made, ring1.made(("w1", c)))
                if c > 0:
                    act.wait_ge(ring2_made, ring2.made(("mix", c - 1, 4)))
                a(m_a[:, :], r1[:, 0, 0:TC], ACT.Tanh)
                a(m_b[:, :], r1[0:MR, 1, 0:TC], ACT.Tanh).then_inc(m_ready, 1)

            def decay_tanh(c):
                act.wait_ge(ring2_made, ring2.made(("dec1", c)))
                if c > 0:
                    act.wait_ge(ring2_made, ring2.made(("dec2", c - 1)))
                a(dect[:, :], slot2(("dec1", c))[0:DDEC, 0, 0:TC], ACT.Tanh).then_inc(dect_ready, 1)

            def decay_exp(c):
                act.wait_ge(ring2_made, ring2.made(("dec2", c)))
                if c > 0:
                    act.wait_ge(e_ready, 4 * c)
                for half in range(2):
                    last = a(ew[:, half, :], slot2(("dec2", c))[0:HD, half, 0:TC], ACT.Exp,
                             bias=chan_s[:, V_TD + half:V_TD + half + 1])
                last.then_inc(ew_ready, 1)

            def copy_v(c):
                act.wait_ge(ring2_made, ring2.made(("v", c)))
                if H * PP * (c + 1) > GR:
                    act.wait_ge(aux_made, aux.made(("fill", 0, NFILL - 1)))
                for n in range(2):
                    for ro, so, m in pieces(H * (PP * c + 2 * n), 2 * H):
                        last = nc.scalar.copy(vring[:, K * ro:K * (ro + m)],
                                              slot2(("v", c))[:, n, K * so:K * (so + m)])
                last.then_inc(v_ready, 1)

            def gate_tanh(c):
                act.wait_ge(ring2_made, ring2.made(("g", c)))
                if c > 0:
                    act.wait_ge(gate_spilled, 16 * c)
                a(th[:, :, :], slot2(("g", c))[0:HD, :, 0:TC], ACT.Tanh, scale=0.5).then_inc(th_ready, 1)

            def decay_factors(c, e):
                act.wait_ge(clip_ready, 2 * c + 1 + e // 2)
                n = 4 * c + e
                if n >= 2:
                    act.wait_ge(decayed_ready, n - 1)
                src, scale = ((ew, 1.0), (ew, -1.0), (cs, -1.0), (cs, 1.0))[e]
                a(ex[:, e % 2], src[:, :, :], ACT.Exp, scale=scale).then_inc(e_ready, 1)

            def copy_k(c):
                act.wait_ge(ring2_made, ring2.made(("k", c)))
                if c > 0:
                    act.wait_ge(aux_made, aux.made(("heads", c - 1, PP - 1, Q - 1)))
                    act.wait_ge(decayed_ready, 4 * c)
                src = slot2(("k", c))[0:HD, :, 0:TC]
                nc.scalar.copy(kp[:, :, 0:TC], src)
                for par in range(2):
                    last = nc.scalar.activation(kpar[:, par], src, ACT.Copy, scale=chan_s[:, V_PAR + par:V_PAR + par + 1])
                last.then_inc(k_ready, 1)

            def copy_r(c):
                act.wait_ge(ring2_made, ring2.made(("r", c)))
                if c > 0:
                    act.wait_ge(decayed_ready, 4 * c)
                for par in range(2):
                    last = nc.scalar.activation(rpar[:, par], slot2(("r", c))[0:HD, :, 0:TC], ACT.Copy,
                                                scale=chan_s[:, V_PAR + par:V_PAR + par + 1])
                last.then_inc(r_ready, 1)

            def copy_matrices(c, p):
                first = H * (PP * c + p)
                if first + H > GR:
                    act.wait_ge(aux_made, aux.made(("fill", 0, NFILL - 1)))
                if c > 0 and p == 0:
                    act.wait_ge(at_spilled, 32 * c)
                for q in range(Q):
                    key = ("heads", c, p, q)
                    act.wait_ge(aux_made, aux.made(key))
                    src = aux_bank(key)[:, 0:4 * T].rearrange("p (a n) -> p a n", a=2)
                    s0, s1 = (first + 2 * q) % GR, (first + H // 2 + 2 * q) % GR
                    if s1 > s0:
                        a0 = min(s0, GR - H)
                        nc.scalar.copy(gram[:, T * a0:T * (a0 + H)].rearrange("p (a n) -> p a n", a=2)[
                            :, :, T * (s0 - a0):T * (s0 - a0 + 2)], src)
                    else:
                        nc.scalar.copy(gram[:, T * s0:T * (s0 + 2)], src[:, 0])
                        nc.scalar.copy(gram[:, T * s1:T * (s1 + 2)], src[:, 1])
                    nc.scalar.copy(at[:, p, :].rearrange("p (a n) -> p a n", a=2)[:, :, 2 * T * q:2 * T * (q + 1)],
                                   aux_bank(key)[:, 4 * T:8 * T].rearrange("p (a n) -> p a n", a=2)).then_inc(f_ready, 1)

            def fill(g):
                m = sysm[:, g % 2]
                for j in range(NFILL):
                    key = ("fill", g, j)
                    act.wait_ge(aux_made, aux.made(key))
                    if j == 0 and g == 2:
                        act.wait_ge(xpose_ready, 1)
                    src = aux_bank(key)[:, :].rearrange("p (n b t) -> p n b t", n=4, b=2)
                    if j < NTG:
                        n = min(4, T - 4 * j)
                        dst = m[:, :, 4 * j:4 * j + n, 0:T].rearrange("p b n t -> p n b t")
                    else:
                        n = 4
                        k0 = T + 4 * (j - NTG)
                        dst = m[:, :, :, k0:k0 + 4].rearrange("p b t n -> p n b t")
                    nc.scalar.copy(dst, src[:, 0:n, :, 0:T]).then_inc(sys_filled, 1)

            def prepare(g):
                act.wait_ge(prep_dve, 6 * g + 1)
                a(nrm[:, :, :], nrm[:, :, :], ACT.Sqrt).then_inc(prep_act, 1)
                act.wait_ge(prep_dve, 6 * g + 4)
                act.wait_ge(temp_ready, 1)
                a(sysm[:, g % 2, :, :, 0:T], sysm[:, g % 2, :, :, 0:T], ACT.Exp, scale=temp[:, g:g + 1]).then_inc(prep_act, 1)

            def solution_out(g):
                wait_solved(act, g)
                if g > 0:
                    act.wait_ge(c1_made, ringc1.made(("solution", g - 1, NTV // 2 - 1)))
                else:
                    act.wait_ge(c_memset, 1)
                for b2 in range(2):
                    last = nc.scalar.copy(xpose[:, :, b2, 0:T], sysm[:, g % 2, b2, :, T:W].rearrange("p t k -> p k t"))
                last.then_inc(xpose_ready, 1)

            def solution_in(g):
                for j in range(NTV // 2):
                    act.wait_ge(c1_made, ringc1.made(("solution", g, j)))
                    for n in range(2):
                        k0 = 8 * j + 4 * n
                        last = nc.scalar.copy(pv[:, g, :, k0:k0 + 4].rearrange("p s k -> p k s"),
                                              pair_of(1)[:, n, :].rearrange("p (k s) -> p k s", k=4))
                    last.then_inc(pv_ready, 1)

            for i in range(NC + 2):
                c1, c2, c3 = iteration(i)
                if c3 is not None:
                    copy_matrices(c3, 0)
                if c1 is not None:
                    square(c1)
                for g in range(NG - 1):
                    if i == SOLVE_AT[g][0]:
                        prepare(g)
                if c2 is not None:
                    decay_tanh(c2)
                if c3 is not None:
                    copy_matrices(c3, 1)
                if c1 is not None:
                    inverse_std(c1)
                if c2 is not None:
                    copy_v(c2)
                    decay_exp(c2)
                if c3 is not None:
                    copy_matrices(c3, 2)
                if c2 is not None:
                    gate_tanh(c2)
                if c3 is not None:
                    copy_matrices(c3, 3)
                if c1 is not None:
                    lora_tanh(c1)
                if c2 is not None:
                    decay_factors(c2, 0)
                    copy_k(c2)
                    copy_r(c2)
                    for e in range(1, 4):
                        decay_factors(c2, e)
                g = None if c3 is None else completed(c3)
                if g is not None and g < 2:
                    fill(g)
            phase_a_over(act)
            solution_out(0)
            fill(2)
            prepare(2)

            c1p, c2p = pair_of(1), (pair_of(0), pair_of(2), pair_of(3))

            def copy_y(c):
                act.wait_ge(c1_made, ringc1.made(("y", c)))
                if c > 0:
                    act.wait_ge(c1_made, ringc1.made(("yT", c - 1)))
                nc.scalar.copy(ysb[:, :, :].rearrange("p (n m) d -> p n (m d)", n=2), c1p[:, :, 0:2 * D]
                               ).then_inc(y_ready, 1)

            def copy_yT(c):
                act.wait_ge(c1_made, ringc1.made(("yT", c)))
                if c > 0:
                    act.wait_ge(yc_ready, c)
                for half in range(2):
                    last = nc.scalar.copy(yT[:, half, :].rearrange("p (b t) -> p b t", b=NB),
                                          c1p[0:HD, half, :].rearrange("p (b t) -> p b t", b=NB)[:, :, 0:T])
                last.then_inc(yT_ready, 1)

            def square_y(c):
                act.wait_ge(yc_ready, c + 1)
                if c > 0:
                    act.wait_ge(c1_made, ringc1.made(("gvar", c - 1)))
                a(sqc[:, :, :], yc[:, :, :], ACT.Square).then_inc(sqc_ready, 1)

            def inverse_std_y(c):
                nc.scalar.preload_act_table_set("natural_log_exp_and_others")
                act.wait_ge(c1_made, ringc1.made(("gvar", c)))
                if c > 0:
                    act.wait_ge(yn_ready, c)
                a(rsc[:, :, :], c1p[0:HD, :, 0:TC], ACT.Ln, bias=eps_s[0:HD, 1:2]).then_inc(rsc_log, 1)
                act.wait_ge(rsc_log, c + 1)
                a(rsc[:, :, :], rsc[:, :, :], ACT.Exp, scale=-0.5).then_inc(rsc_ready, 1)

            def affine(c):
                act.wait_ge(yn_ready, c + 1)
                for half in range(2):
                    last = a(yc[:, half, :], yc[:, half, :], ACT.Identity, scale=chan_s[:, V_LNW + half:V_LNW + half + 1],
                             bias=chan_s[:, V_LNB + half:V_LNB + half + 1])
                last.then_inc(affine_ready, 1)

            def square_h(c):
                act.wait_ge(hc_ready, c + 1)
                if c > 0:
                    act.wait_ge(c2_made, ringc2.made(("lvar", c - 1)))
                a(sq2[:, :, :], hc[:, :, :], ACT.Square).then_inc(sq2_ready, 1)

            def inverse_std_h(c):
                nc.scalar.preload_act_table_set("natural_log_exp_and_others")
                act.wait_ge(c2_made, ringc2.made(("lvar", c)))
                if c > 0:
                    act.wait_ge(hn_ready, c)
                a(rs2[:, :], c2p[ringc2.slot(("lvar", c))][0:HD, 0, 0:TC], ACT.Ln, bias=eps_s[0:HD, 0:1]
                  ).then_inc(rs2_log, 1)
                act.wait_ge(rs2_log, c + 1)
                a(rs2[:, :], rs2[:, :], ACT.Exp, scale=-0.5).then_inc(rs2_ready, 1)

            def gelu(c, j):
                act.wait_ge(c2_made, ringc2.made(("fc", c, j)))
                if c > 0 and j == 0:
                    act.wait_ge(c2_made, ringc2.made(("proj", c - 1)))
                if c == 0:
                    act.wait_ge(ffn_prep, 3)
                for n in range(2):
                    f = 2 * j + n
                    last = a(hact[:, f, :], c2p[ringc2.slot(("fc", c, j))][:, n, 0:TC], ACT.Gelu_apprx_tanh,
                             bias=bfc_s[:, f:f + 1])
                last.then_inc(hact_ready, 1)

            for seg in range(len(SEGMENTS)):
                if seg > 0:
                    solution_out(seg)
                solution_in(seg)
                for d1, d2, d3 in c_iterations(seg):
                    if d1 is not None:
                        copy_y(d1)
                    if d3 is not None:
                        gelu(d3, 0)
                    if d1 is not None:
                        copy_yT(d1)
                    if d2 is not None:
                        square_h(d2)
                    if d3 is not None:
                        gelu(d3, 1)
                    if d1 is not None:
                        square_y(d1)
                    if d3 is not None:
                        gelu(d3, 2)
                    if d2 is not None:
                        inverse_std_h(d2)
                    if d1 is not None:
                        inverse_std_y(d1)
                        affine(d1)

        @block.gpsimd
        def _(pool):
            tt = nc.gpsimd.tensor_tensor
            nc.gpsimd.memset(eps_s[:, 0:1], LN_EPS)
            nc.gpsimd.memset(eps_s[:, 1:2], GN_EPS)
            nc.gpsimd.memset(xpad[:, :, :, :, :], 0.0)
            nc.gpsimd.memset(xv[:, :, :, :], 0.0)
            nc.gpsimd.memset(kp[:, :, TC:TC + TP - T], 0.0)
            nc.gpsimd.memset(ke[:, :, :, TC:TC + TP - T], 0.0).then_inc(memset_done, 1)

            def token_view(x):
                return x.rearrange("p a (b t) -> p (a b) t", t=T)

            def neighbours(c):
                pool.wait_ge(xn_ready, c + 1)
                x = xpad[:, c % 2].rearrange("p a b t -> p (a b) t")
                tt(token_view(dx[:, c % 2]), x[:, :, 0:T], x[:, :, 2:T + 2], ALU.add).then_inc(nbr_ready, 1)

            def mixed(c, n):
                pool.wait_ge(prod_ready, mix_count(c, n))
                slot = (NMIX * c + n) % 2
                x = xpad[:, c % 2].rearrange("p a b t -> p (a b) t")[:, :, 1:T + 1]
                if n == 1:
                    if c > 0:
                        pool.wait_ge(ring2_made, ring2.made(("v", c - 1)))
                    dst = xv[:, :, :, :].rearrange("p a b t -> p (a b) t")[:, :, 0:T]
                else:
                    which = {0: 0, 2: 1, 3: 0, 4: 1}[n]
                    if n == 0 and c > 0:
                        pool.wait_ge(ring2_made, ring2.made(("k", c - 1)))
                    if n == 2 and c > 0:
                        pool.wait_ge(ring2_made, ring2.made(("r", c - 1)))
                    if n == 3:
                        pool.wait_ge(ring2_made, ring2.made(("dec1", c)))
                    if n == 4:
                        pool.wait_ge(ring2_made, ring2.made(("g", c)))
                    dst = token_view(xs[:, which])
                tt(dst, token_view(prod[:, slot]), x, ALU.add).then_inc(xs_ready, 1)

            def decay_sums(c):
                pool.wait_ge(cs_ready, c + 1)
                if c > 0:
                    pool.wait_ge(cdiff_ready, 3 * c)
                tt(cb[:, :, :], cs[:, :, :], ew[:, :, :], ALU.add).then_inc(cdiff_ready, 1)
                pool.wait_ge(cdiff_ready, 3 * c + 1)

                def centred(dst, src):
                    s = token_view(src)
                    mid = s[:, :, MID:MID + 1].broadcast_to([HD, 2 * NB, T])
                    return tt(token_view(dst), s, mid, ALU.subtract)
                centred(ew, cs).then_inc(cdiff_ready, 1)
                pool.wait_ge(cdiff_ready, 3 * c + 2)
                centred(cs, cb).then_inc(cdiff_ready, 1)

            def decayed(c, e):
                pool.wait_ge(e_ready, 4 * c + e + 1)
                if e == 0:
                    pool.wait_ge(k_ready, c + 1)
                    pool.wait_ge(r_ready, c + 1)
                    if c > 0:
                        pool.wait_ge(aux_made, aux.made(("heads", c - 1, PP - 1, Q - 1)))
                f = ex[:, e % 2]
                if e % 2 == 0:
                    f2 = f.unsqueeze(1).broadcast_to([HD, 2, 2, TC])
                    last = tt(re[:, e // 2], rpar[:, :, :, :], f2, ALU.mult)
                else:
                    last = tt(ke[:, e // 2, :, 0:TC], kp[:, :, 0:TC], f, ALU.mult)
                last.then_inc(decayed_ready, 1)

            def back_substitute(g, k_from, k_to):
                m = sysm[:, g % 2]
                step = 2 * (T - 1) * g + 2 * (T - 1 - k_from)
                if k_from == T - 1:
                    pool.wait_ge(elim_step, elim_at[g, "scaled"])
                for k in range(k_from, k_to, -1):
                    if step > 0:
                        pool.wait_ge(back_step, step)
                    o = outer_b[:, 0:2 * k * K].rearrange("p (b i c) -> p b i c", b=2, c=K)
                    u = m[:, :, k, 0:k].unsqueeze(3).broadcast_to([NSYS, 2, k, K])
                    x = m[:, :, k, T:W].unsqueeze(2).broadcast_to([NSYS, 2, k, K])
                    tt(o, u, x, ALU.mult).then_inc(back_step, 1)
                    pool.wait_ge(back_step, step + 1)
                    v = m[:, :, 0:k, T:W]
                    tt(v, v, o, ALU.subtract).then_inc(back_step, 1)
                    step += 2

            def back_part(g, part, n):
                b = cuts(n, BACK_WORK)
                back_substitute(g, T - 1 - b[part], T - 1 - b[part + 1])

            def back_0(i, slot):
                if i == 8:
                    back_part(0, slot, 12)

            for i in range(NC + 2):
                c1, c2, c3 = iteration(i)
                if c2 is not None:
                    mixed(c2, 0)
                    mixed(c2, 1)
                    back_0(i, 0)
                    mixed(c2, 2)
                    back_0(i, 1)
                if c1 is not None:
                    neighbours(c1)
                if c2 is not None:
                    mixed(c2, 3)
                    back_0(i, 2)
                    decay_sums(c2)
                    mixed(c2, 4)
                    back_0(i, 3)
                    for e in range(4):
                        decayed(c2, e)
            for part in range(4, 12):
                back_part(0, part, 12)
            phase_a_over(pool)
            nc.gpsimd.memset(xpose[:, :, :, :], 0.0)
            nc.gpsimd.memset(atc[:, :, :], 0.0)
            nc.gpsimd.memset(ones_s[:, :], 1.0).then_inc(c_memset, 1)

            def gated(c):
                pool.wait_ge(affine_ready, c + 1)
                pool.wait_ge(gate_loaded, 16 * (c + 1))
                if c > 1:
                    pool.wait_ge(c2_made, ringc2.made(("wo", c - 2)))
                tt(z[:, c % 2], yc[:, :, :], gin[:, :, :], ALU.mult).then_inc(z_ready, 1)

            for seg in range(len(SEGMENTS)):
                for n, (d1, _, _) in enumerate(c_iterations(seg)):
                    if seg == 0:
                        back_part(1, n, 4)
                    if d1 is not None:
                        gated(d1)

        @block.vector
        def _(dve):
            tt, ts, stt = nc.vector.tensor_tensor, nc.vector.tensor_scalar, nc.vector.scalar_tensor_tensor
            r1 = pair_of(0)

            def slot2(key):
                return pair_of(1 + ring2.slot(key))

            def token_view(x):
                return x.rearrange("p a (b t) -> p (a b) t", t=T)

            dve.wait_ge(chan_loaded, 16)
            for half in range(2):
                ts(posb[:, half, :], chan_s[:, V_POS + NPT * half:V_POS + NPT * (half + 1)],
                   chan_s[:, V_TOKB + half:V_TOKB + half + 1], None, ALU.add).then_inc(prep_done, 1)
            dve.wait_ge(prep_done, 2)

            def embedded(c):
                if c > 0:
                    dve.wait_ge(h_spilled, 16 * c)
                    dve.wait_ge(ring1_made, ring1.made(("mean", c - 1)))
                h4 = hbuf[:, :, :].rearrange("p a (b t) -> p a b t", b=NB)
                nc.vector.tensor_copy(h4[:, :, :, 0], chan_s[:, V_CLS:V_CLS + 2].unsqueeze(2).broadcast_to([HD, 2, NB])
                                      ).then_inc(h_ready, 1)
                dve.wait_ge(ring1_made, ring1.made(("embed", c)))
                for half in range(2):
                    src = r1[0:HD, half, 0:PC].rearrange("p (b t) -> p b t", b=NB)
                    last = tt(h4[:, half, :, 1:T], src, posb[:, half, :].unsqueeze(1).broadcast_to([HD, NB, NPT]), ALU.add)
                last.then_inc(h_ready, 1)

            def centre(c):
                dve.wait_ge(ring1_made, ring1.made(("mean", c)))
                dve.wait_ge(h_ready, 2 * c + 2)
                if c > 0:
                    dve.wait_ge(sq_ready, c)
                    dve.wait_ge(xn_ready, c)
                tt(xc[:, :, :], hbuf[:, :, :], r1[0:HD, 0:1, 0:TC].broadcast_to([HD, 2, TC]), ALU.subtract
                   ).then_inc(xc_ready, 1)

            def normalised(c):
                dve.wait_ge(rstd_ready, c + 1)
                dve.wait_ge(memset_done, 1)
                if c > 1:
                    dve.wait_ge(xs_ready, mix_count(c - 2, 4))
                dst = xpad[:, c % 2].rearrange("p a b t -> p (a b) t")[:, :, 1:T + 1]
                for half in range(2):
                    last = tt(dst[:, NB * half:NB * (half + 1)], xc[:, half, :].rearrange("p (b t) -> p b t", t=T),
                              rstd[:, :].rearrange("p (b t) -> p b t", t=T), ALU.mult)
                last.then_inc(xn_ready, 1)

            def difference(c):
                dve.wait_ge(nbr_ready, c + 1)
                x = xpad[:, c % 2].rearrange("p a b t -> p (a b) t")[:, :, 1:T + 1]
                d = token_view(dx[:, c % 2])
                stt(out=d, in0=d, scalar=0.5, in1=x, op0=ALU.mult, op1=ALU.subtract).then_inc(dx_ready, 1)
                dve.wait_ge(dx_ready, c + 1)
                if c > 0:
                    dve.wait_ge(ring1_made, ring1.made(("w1", c - 1)))
                for half in range(2):
                    b = slice(NB * half, NB * (half + 1))
                    last = stt(out=xxx[:, half, :].rearrange("p (b t) -> p b t", t=T), in0=d[:, b],
                               scalar=chan_s[:, V_MAA + half:V_MAA + half + 1], in1=x[:, b], op0=ALU.mult, op1=ALU.add)
                last.then_inc(xxx_ready, 1)

            def product(c, n):
                key, m = ("mix", c, n), MIXES[n]
                dve.wait_ge(ring2_made, ring2.made(key))
                count = mix_count(c, n)
                if count > 2:
                    dve.wait_ge(xs_ready, count - 2)
                for half in range(2):
                    col = V_MAA + 2 * (m + 1) + half
                    last = stt(out=prod[:, (count - 1) % 2, half, :], in0=slot2(key)[0:HD, half, 0:TC],
                               scalar=chan_s[:, col:col + 1], in1=dx[:, c % 2, half, :], op0=ALU.add, op1=ALU.mult)
                last.then_inc(prod_ready, 1)

            def scan(c):
                dve.wait_ge(ew_ready, c + 1)
                if c > 0:
                    dve.wait_ge(e_ready, 4 * c)
                for half in range(2):
                    last = nc.vector.tensor_tensor_scan(cs[:, half, :], scan_s[:, :], ew[:, half, :], 0.0, ALU.mult,
                                                        ALU.subtract)
                last.then_inc(cs_ready, 1)

            def clip(c):
                for n, x in enumerate((ew, cs)):
                    dve.wait_ge(cdiff_ready, 3 * c + 2 + n)
                    ts(x[:, :, :], x[:, :, :], -60.0, 60.0, ALU.max, ALU.min).then_inc(clip_ready, 1)

            def gated(c):
                dve.wait_ge(th_ready, c + 1)
                stt(out=gate[:, :, :], in0=th[:, :, :], scalar=1.0, in1=slot2(("g", c))[0:HD, :, 0:TC], op0=ALU.add,
                    op1=ALU.mult).then_inc(gate_ready, 1)

            def backward_half(c, p):
                for q in range(Q):
                    key = ("heads", c, p, q)
                    dve.wait_ge(f_ready, heads_count(c, p, q))
                    s = aux.slot(key)
                    nc.vector.copy_predicated(
                        at[:, p, :].rearrange("p (a h t) -> p a h t", a=2, t=T)[:, :, 2 * q:2 * q + 2, :],
                        tri_s[:, :].unsqueeze(1).unsqueeze(1).broadcast_to([128, 2, 2, T]),
                        bank[3][:, 512 * s + 8 * T:512 * s + 12 * T].rearrange("p (a h t) -> p a h t", a=2, t=T)
                        ).then_inc(at_ready, 1)

            def diagonal(g):
                flat = sysm[:, g % 2].rearrange("p b i j -> p b (i j)")
                return flat[:, :, 0:(T - 1) * (W + 1) + 1:W + 1]

            def prepare(g):
                m = sysm[:, g % 2, :, :, 0:T]
                n0 = 6 * g
                dve.wait_ge(sys_filled, NFILL * (g + 1))
                ts(nrm[:, :, :], diagonal(g), 1e-24, None, ALU.max).then_inc(prep_dve, 1)
                dve.wait_ge(prep_act, 2 * g + 1)
                nc.vector.reciprocal(nrm[:, :, :], nrm[:, :, :]).then_inc(prep_dve, 1)
                dve.wait_ge(prep_dve, n0 + 2)
                rows = nrm[:, :, :].unsqueeze(3).broadcast_to([NSYS, 2, T, T])
                cols = nrm[:, :, :].unsqueeze(2).broadcast_to([NSYS, 2, T, T])
                tt(m, m, rows, ALU.mult).then_inc(prep_dve, 1)
                dve.wait_ge(prep_dve, n0 + 3)
                tt(m, m, cols, ALU.mult).then_inc(prep_dve, 1)
                dve.wait_ge(prep_act, 2 * g + 2)
                ts(m, m, float(np.exp(-20.0)), float(np.exp(20.0)), ALU.max, ALU.min).then_inc(prep_dve, 1)
                dve.wait_ge(prep_dve, n0 + 5)
                ts(diagonal(g), diagonal(g), 1.0, None, ALU.add).then_inc(prep_dve, 1)
                dve.wait_ge(prep_dve, n0 + 6)

            def eliminate(g, first, end):
                m, rd, n0 = sysm[:, g % 2], rdiag[:, g % 2], elim_at[g, "start"]
                for k, kind, band in STEPS[first:end]:
                    rest = T - 1 - k
                    if kind == "recip":
                        if k > 0:
                            dve.wait_ge(elim_step, n0 + STEP_AT[k - 1, "subtract", 0] + 1)
                        nc.vector.reciprocal(rd[:, :, k:k + 1], m[:, :, k, k:k + 1]).then_inc(elim_step, 1)
                        continue
                    if kind == "scale":
                        dve.wait_ge(elim_step, n0 + STEP_AT[k, "recip", 0] + 1)
                        tt(m[:, :, k + 1:T, k], m[:, :, k, k + 1:T], rd[:, :, k:k + 1].broadcast_to([NSYS, 2, rest]),
                           ALU.mult).then_inc(elim_step, 1)
                        continue
                    used = sum(2 * (b1 - b0) * (W - k - 1 - b0) for b0, b1 in bands(rest)[:band])
                    r0, r1_ = bands(rest)[band]
                    rows, cols = r1_ - r0, W - (k + 1 + r0)
                    o = outer[:, used:used + 2 * rows * cols].rearrange("p (b i j) -> p b i j", b=2, j=cols)
                    if kind == "outer":
                        dve.wait_ge(elim_step, n0 + STEP_AT[k, "scale", 0] + 1)
                        tt(o, m[:, :, k + 1 + r0:k + 1 + r1_, k].unsqueeze(3).broadcast_to([NSYS, 2, rows, cols]),
                           m[:, :, k, k + 1 + r0:W].unsqueeze(2).broadcast_to([NSYS, 2, rows, cols]), ALU.mult
                           ).then_inc(elim_step, 1)
                    else:
                        dve.wait_ge(elim_step, n0 + STEP_AT[k, "outer", band] + 1)
                        a_ = m[:, :, k + 1 + r0:k + 1 + r1_, k + 1 + r0:W]
                        tt(a_, a_, o, ALU.subtract).then_inc(elim_step, 1)

            def scale_rows(g):
                v = sysm[:, g % 2, :, :, T:W]
                dve.wait_ge(elim_step, elim_at[g, "scaled"] - 1)
                tt(v, v, rdiag[:, g % 2].unsqueeze(3).broadcast_to([NSYS, 2, T, K]), ALU.mult).then_inc(elim_step, 1)

            def back_substitute(g, k_from, k_to):
                m = sysm[:, g % 2]
                n = elim_at[g, "scaled"] + 2 * (T - 1 - k_from)
                for k in range(k_from, k_to, -1):
                    dve.wait_ge(elim_step, n)
                    o = outer[:, 0:2 * k * K].rearrange("p (b i c) -> p b i c", b=2, c=K)
                    u = m[:, :, k, 0:k].unsqueeze(3).broadcast_to([NSYS, 2, k, K])
                    x = m[:, :, k, T:W].unsqueeze(2).broadcast_to([NSYS, 2, k, K])
                    tt(o, u, x, ALU.mult).then_inc(elim_step, 1)
                    dve.wait_ge(elim_step, n + 1)
                    v = m[:, :, 0:k, T:W]
                    tt(v, v, o, ALU.subtract).then_inc(elim_step, 1)
                    n += 2

            def solve(i, slot):
                for g, (i0, n_parts, total) in SOLVE_AT.items():
                    part = SLOTS * (i - i0) + slot
                    if 0 <= part < n_parts:
                        if part == 0:
                            prepare(g)
                        b = cuts(total, STEP_WORK)
                        eliminate(g, b[part], b[part + 1])
                        if part == total - 1:
                            scale_rows(g)

            for i in range(NC + 2):
                c1, c2, c3 = iteration(i)
                if c1 is not None:
                    embedded(c1)
                    if c1 == 0:
                        dve.wait_ge(w_loaded, 16 * 12)
                        ts(wo_s[:, :, :], wo_s[:, :, :], 0.5, None, ALU.mult).then_inc(prep_done, 1)
                        dve.wait_ge(temp_act, 3)
                        ts(lucid_s[:, :], lucid_s[:, :], 0.0, None, ALU.max).then_inc(prep_done, 1)
                        dve.wait_ge(prep_done, 4)
                        tt(temp[:, :], lucid_s[:, :], tmp3[:, 0, :], ALU.add).then_inc(temp_ready, 1)
                if c2 is not None:
                    product(c2, 0)
                    product(c2, 1)
                if c3 is not None:
                    backward_half(c3, 0)
                if c1 is not None:
                    centre(c1)
                solve(i, 0)
                if c2 is not None:
                    product(c2, 2)
                solve(i, 1)
                if c3 is not None:
                    backward_half(c3, 1)
                solve(i, 2)
                if c1 is not None:
                    normalised(c1)
                solve(i, 3)
                if c2 is not None:
                    product(c2, 3)
                solve(i, 4)
                if c1 is not None:
                    difference(c1)
                solve(i, 5)
                if c2 is not None:
                    scan(c2)
                solve(i, 6)
                if c3 is not None:
                    backward_half(c3, 2)
                solve(i, 7)
                if c2 is not None:
                    gated(c2)
                    product(c2, 4)
                solve(i, 8)
                if c2 is not None:
                    clip(c2)
                solve(i, 9)
                if c3 is not None:
                    backward_half(c3, 3)
                solve(i, 10)
                solve(i, 11)

            rest = cuts(SOLVE_AT[1][2], STEP_WORK)[SOLVE_AT[1][1]]
            eliminate(1, rest, len(STEPS))
            scale_rows(1)

            c1p, c2p = pair_of(1), (pair_of(0), pair_of(2), pair_of(3))
            phase_a_over(dve)
            dve.wait_ge(ffnw_loaded, 16 * 7)
            tt(aij[:, :], alph_s[:, 0:1], alph_s[:, 1:2], ALU.mult).then_inc(prep_done, 1)
            dve.wait_ge(prep_done, 5)
            ts(adin[:, :], din_s[:, :], aij[:, 0:1], None, ALU.mult).then_inc(ffn_prep, 1)
            dve.wait_ge(ffn_made, 1)
            for half in range(2):
                w = wfc_s[:, half, :].rearrange("p (n f) -> p n f", n=2)
                tt(w, w, c2p[half][0:HD, :, 0:FH // 2], ALU.mult)
            tt(wpr_s[:, 0:2, :], wpr_s[:, 0:2, :], c1p[:, :, 0:D], ALU.mult).then_inc(ffn_prep, 1)
            dve.wait_ge(ffn_made, 2)
            for j in range(2):
                w = wpr_s[:, 2 + 2 * j:4 + 2 * j, :]
                tt(w, w, c2p[j][:, :, 0:D], ALU.mult)
            tt(bfc_s[:, :], bfc_s[:, :], c1p[:, 0, 0:FC], ALU.mult)
            tt(bpr_s[:, :], bpr_s[:, :], c1p[0:1, 1, 0:D], ALU.mult).then_inc(ffn_prep, 1)

            def centre_y(c):
                dve.wait_ge(c1_made, ringc1.made(("gmean", c)))
                if c > 0:
                    dve.wait_ge(z_ready, c)
                dve.wait_ge(yT_ready, c + 1)
                tt(yc[:, :, :], yT[:, :, :], c1p[0:HD, :, 0:TC], ALU.subtract).then_inc(yc_ready, 1)

            def normalise_y(c):
                dve.wait_ge(rsc_ready, c + 1)
                tt(yc[:, :, :], yc[:, :, :], rsc[:, :, :], ALU.mult).then_inc(yn_ready, 1)

            def residual(c):
                dve.wait_ge(c2_made, ringc2.made(("wo", c)))
                dve.wait_ge(hin_loaded, 16 * (c + 1))
                if c > 1:
                    dve.wait_ge(c2_made, ringc2.made(("proj", c - 2)))
                tt(h1[:, c % 2], hin[:, :, :], c2p[ringc2.slot(("wo", c))][0:HD, :, 0:TC], ALU.add).then_inc(h1_ready, 1)

            def centre_h(c):
                dve.wait_ge(c2_made, ringc2.made(("lmean", c)))
                if c > 0:
                    dve.wait_ge(sq2_ready, c)
                dve.wait_ge(h1_ready, c + 1)
                tt(hc[:, :, :], h1[:, c % 2], c2p[ringc2.slot(("lmean", c))][0:HD, 0:1, 0:TC].broadcast_to([HD, 2, TC]),
                   ALU.subtract).then_inc(hc_ready, 1)

            def normalise_h(c):
                dve.wait_ge(rs2_ready, c + 1)
                if c > 1:
                    dve.wait_ge(c2_made, ringc2.made(("fc", c - 2, FC // 2 - 1)))
                tt(hn[:, c % 2], hc[:, :, :], rs2[:, :].unsqueeze(1).broadcast_to([HD, 2, TC]), ALU.mult
                   ).then_inc(hn_ready, 1)

            def copy_out(c):
                dve.wait_ge(c2_made, ringc2.made(("proj", c)))
                if c > 0:
                    dve.wait_ge(out_stored, 16 * 3 * c)
                src = c2p[ringc2.slot(("proj", c))]
                for n, _, nt in tokens(c):
                    last = nc.vector.tensor_copy(osb[0:nt, n, :], src[0:nt, n // 2, D * (n % 2):D * (n % 2 + 1)])
                last.then_inc(osb_ready, 1)

            prepare(NG - 1)

            def last_group(seg, slot):
                if seg == 0:
                    b = cuts(4 * 6, STEP_WORK)
                    eliminate(NG - 1, b[slot], b[slot + 1])
                    if slot == 4 * 6 - 1:
                        scale_rows(NG - 1)
                elif seg == 1:
                    b = cuts(5 * 6, BACK_WORK)
                    back_substitute(NG - 1, T - 1 - b[slot], T - 1 - b[slot + 1])

            for seg in range(len(SEGMENTS)):
                for n, (d1, d2, d3) in enumerate(c_iterations(seg)):
                    last_group(seg, 6 * n)
                    if d2 is not None:
                        residual(d2)
                    last_group(seg, 6 * n + 1)
                    if d2 is not None:
                        centre_h(d2)
                    last_group(seg, 6 * n + 2)
                    if d1 is not None:
                        centre_y(d1)
                    last_group(seg, 6 * n + 3)
                    if d2 is not None:
                        normalise_h(d2)
                    last_group(seg, 6 * n + 4)
                    if d1 is not None:
                        normalise_y(d1)
                    last_group(seg, 6 * n + 5)
                    if d3 is not None:
                        copy_out(d3)


def kernel(**inputs):
    import concourse.bacc as bacc
    from concourse.bass_utils import run_bass_kernel_spmd as run

    a = {k: np.asarray(v) for k, v in inputs.items()}

    def halves(v):
        v = v.reshape(v.shape[:-1] + (2, HD))
        return np.moveaxis(v, -1, 0)

    def rows(w):
        return w.reshape(2, HD, -1).transpose(1, 0, 2)

    x = a["x"].reshape(B, CH, HP, PATCH, HP, PATCH).transpose(0, 2, 4, 1, 3, 5)
    maa = np.stack([a["L0_attn_time_maa_" + n].reshape(D) for n in "xwkvrg"])
    par = (np.arange(HD)[:, None] // K % 2 == np.arange(2)[None, :]).astype(np.float32)
    chan = np.concatenate([
        halves(a["L0_tok_b"]), halves(a["cls_tok"].reshape(D)), halves(maa).reshape(HD, 12),
        halves(a["L0_attn_time_decay"].reshape(D)), halves(a["L0_attn_ln_w"]), halves(a["L0_attn_ln_b"]), par,
        halves(a["L0_tok_pos"].reshape(NPT, D)).transpose(0, 2, 1).reshape(HD, 2 * NPT)], axis=1)
    heads = np.arange(HD) // K
    p = np.arange(128)
    w2 = a["L0_attn_maa_w2"]
    token = np.arange(TC) % T
    arrays = {
        "patches": x.reshape(NC, PC, FK, 128).transpose(0, 3, 2, 1),
        "chan": chan,
        "wtok": a["L0_tok_W"].T.reshape(FK, 128, D).transpose(1, 0, 2),
        "w1": rows(a["L0_attn_maa_w1"]),
        "w2a": w2[0:4].reshape(128, D), "w2b": w2[4],
        "dw1": rows(a["L0_attn_decay_w1"]), "dw2": a["L0_attn_decay_w2"],
        "wkvrg": np.stack([rows(a["L0_attn_W" + n]) for n in "kvrg"], axis=1),
        "wo": rows(a["L0_attn_Wo"]),
        "wfc": rows(a["L0_ffn_w_fc"].T), "bfc": a["L0_ffn_b_fc"].reshape(FC, 128).T,
        "wproj": a["L0_ffn_w_proj"].T.reshape(FC, 128, D).transpose(1, 0, 2), "bproj": a["L0_ffn_b_proj"].reshape(1, D),
        "alphas": np.stack([np.repeat(a["L0_ffn_alpha_e"], len(RATIOS)), np.tile(a["L0_ffn_alpha_r"], len(EMBEDS))], axis=1),
        "lucid": np.tile(a["L0_attn_lucid_temp"].reshape(H), B // 2).reshape(NG, NSYS).T,
        "ident": np.eye(128, dtype=np.float32),
        "blocks": np.stack([np.full((HD, HD), 1.0 / D), (heads[:, None] == heads[None, :]) / K], axis=1).astype(np.float32),
        "tri": (np.arange(T)[None, :] < p[:, None] % TP).astype(np.uint32),
        "scanmask": np.broadcast_to((token > 0).astype(np.float32), (HD, TC)),
        "din": np.array([[d < e for d in range(D)] for e in EMBEDS for _ in RATIOS], np.float32),
        "hout": np.array([[f < r * e for f in range(FH)] for e in EMBEDS for r in RATIOS], np.float32),
    }
    arrays = {k: np.ascontiguousarray(v) for k, v in arrays.items()}
    nc = bacc.Bacc("TRN2", target_bir_lowering=False, num_devices=1)
    aps = {k: nc.dram_tensor(f"in_{k}", v.shape, mybir.dt.from_np(v.dtype), kind="ExternalInput").ap()
           for k, v in arrays.items()}
    o = nc.dram_tensor("out_0", (B, T, D), F32, kind="ExternalOutput").ap()
    vit_tower(nc, **aps, out=o.rearrange("b t d -> (b t) d"))
    r = run(nc, [{f"in_{k}": v for k, v in arrays.items()}], core_ids=[0])
    return r.results[0]["out_0"]
```

```python
from contextlib import ExitStack

import numpy as np

import concourse.bass as bass
from concourse import mybir
from concourse.alu_op_type import AluOpType as ALU

F32 = mybir.dt.float32
U32 = mybir.dt.uint32
ACT = mybir.ActivationFunctionType

B, CH, IMG, PATCH, D = 64, 3, 96, 16, 192
HP = IMG // PATCH
NPT = HP * HP
T = NPT + 1
MID = T // 2
H, K = 12, 16
HD = D // 2
FK = CH * PATCH * PATCH // 128
NB = 8
NC = B // NB
TC = NB * T
PC = NB * NPT
PP = NB // 2
TP = 64
Q = HD // 32
NMIX, MR = 5, 32
DDEC = 64
HT = H * T
NSYS = 128
NG = B // 2 * H // NSYS
GR = 2 * NSYS
W = T + K
FH = 4 * D
FC = FH // 128
LN_EPS = 1e-5
GN_EPS = 1e-5 * 64.0
EMBEDS, RATIOS = (96, 144, 192), (2, 3, 4)
NA = len(EMBEDS) * len(RATIOS)
MW, MK, MV, MRR, MG = range(5)
MIXES = (MW, MV, MG, MK, MRR)

V_TOKB, V_CLS, V_MAA, V_TD, V_LNW, V_LNB, V_PAR, V_POS = 0, 2, 4, 16, 18, 20, 22, 24
V_N = V_POS + 2 * NPT


def group_chunk(g):
    return -(-(NSYS * (g + 1)) // (H * PP)) - 1


def pieces(first, n):
    a = first % GR
    m = min(n, GR - a)
    return [(a, 0, m)] + ([(0, m, n - m)] if m < n else [])


def bands(m):
    n = 3 if m >= 24 else 2 if m >= 10 else 1
    cuts = [m * j // n for j in range(n + 1)]
    return list(zip(cuts[:-1], cuts[1:]))


def cuts(shares, work):
    total, done, share, out = sum(work), 0, 0, [0]
    ends = [sum(shares[:n + 1]) * total / sum(shares) for n in range(len(shares))]
    for i, w in enumerate(work):
        done += w
        while len(out) <= len(shares) and done >= ends[len(out) - 1] - w / 2:
            out.append(i + 1)
    out[-1:] = [len(work)] if len(out) == len(shares) + 1 else [out[-1]] + [len(work)] * (len(shares) + 1 - len(out))
    return out


def pivot_steps():
    out = [(0, "recip", 0), (0, "scale", 0)]
    for k in range(T - 1):
        n = len(bands(T - 1 - k))
        out += [(k, "outer", b) for b in range(n)] + [(k, "subtract", b) for b in range(min(n, 2))]
        out += [(k + 1, "recip", 0)] + [(k, "subtract", b) for b in range(2, n)]
        if k + 1 < T - 1:
            out += [(k + 1, "scale", 0)]
    return out


DVE_COLS = (8, 10, 12)


def back_steps():
    return [(T, "rows", 0)] + [(k, kind, 0) for k in range(T - 1, 0, -1) for kind in ("back_outer", "back_subtract")]


def dve_work(g, k, kind, band):
    c = DVE_COLS[g]
    if kind in ("recip", "scale"):
        return 100
    if kind == "rows":
        return 70 + 2 * T * c
    if kind in ("back_outer", "back_subtract"):
        return 120 + 2 * k * c
    r0, r1 = bands(T - 1 - k)[band]
    return 70 + 2 * (r1 - r0) * (T + c - k - 1 - r0)


DVE_STEPS = [pivot_steps() + (back_steps() if c else []) for c in DVE_COLS]
STEP_AT = [{step: n for n, step in enumerate(steps)} for steps in DVE_STEPS]
DVE_WORK = [[dve_work(g, *step) for step in steps] for g, steps in enumerate(DVE_STEPS)]
POOL_STEPS = [(k, kind, 0) for k in range(T - 1) for kind in ("outer", "subtract")] + back_steps()
POOL_WORK = [200 + (T if kind == "rows" else T - 1 - k if kind in ("outer", "subtract") else k) * 36
             for k, kind, _ in POOL_STEPS]


class Ring:

    def __init__(self, slots):
        self.slots, self.tasks, self.index = slots, [], {}

    def add(self, key, read):
        self.index[key] = len(self.tasks)
        self.tasks.append(read)

    def slot(self, key):
        return self.index[key] % self.slots

    def made(self, key):
        return self.index[key] + 1

    def before(self, key):
        n = self.index[key] - self.slots
        return self.tasks[n] if n >= 0 else None


def vit_tower(nc, patches, chan, wtok, w1, w2a, w2b, dw1, dw2, wkvrg, wo, wfc, bfc, wproj, bproj, alphas,
              lucid, ident, blocks, tri, scanmask, din, hout, out):
    h_dram = nc.dram_tensor("h_spill", (NC, HD, 2 * TC), F32, kind="Internal").ap()
    gate_dram = nc.dram_tensor("gate_spill", (NC, HD, 2 * TC), F32, kind="Internal").ap()
    at_dram = nc.dram_tensor("at_spill", (NC, 2, T, PP * HT), F32, kind="Internal").ap()

    ctx = ExitStack()
    with ctx:
        def sem(name):
            return ctx.enter_context(nc.semaphore(name))

        def sb(name, shape, dt=F32, where=ctx):
            return where.enter_context(nc.sbuf_tensor(name, shape, dt))


        chan_s = sb("chan_s", [HD, V_N])
        wtok_s = sb("wtok_s", [128, FK, D])
        w1_s = sb("w1_s", [128, 2, NMIX * MR])
        w2a_s = sb("w2a_s", [128, D])
        w2b_s = sb("w2b_s", [MR, D])
        dw1_s = sb("dw1_s", [128, 2, DDEC])
        dw2_s = sb("dw2_s", [DDEC, D])
        wproj4_s = sb("wproj4_s", [128, 4, 2, D])
        wo_s = sb("wo_s", [128, 2, D])
        ident_s = sb("ident_s", [128, 128])
        blocks_s = sb("blocks_s", [128, 2, HD])
        tri_s = sb("tri_s", [128, T], U32)
        scan_s = sb("scan_s", [HD, TC])
        lucid_s = sb("lucid_s", [NSYS, NG])
        temp = sb("temp", [NSYS, NG])
        tmp3 = sb("tmp3", [NSYS, 2, NG])
        eps_s = sb("eps_s", [128, 2])
        posb = sb("posb", [HD, 2, NPT])
        gram = sb("gram", [128, GR * T])
        vring = sb("vring", [128, GR * K])
        sysm = sb("sysm", [NSYS, 2, 2, T, W])
        nrm = sb("nrm", [NSYS, 2, T])
        rdiag = sb("rdiag", [NSYS, 2, 2, T])
        outer = sb("outer", [NSYS, 2880])
        outer_b = sb("outer_b", [NSYS, 2 * (T - 1) * K])

        gram_v = gram[:, :].rearrange("p (s t) -> p s t", t=T)
        v_v = vring[:, :].rearrange("p (s k) -> p s k", k=K)

        actx = ExitStack()

        def sa(name, shape, dt=F32):
            return sb(name, shape, dt, actx)
        pat = sa("pat", [128, FK, PC])
        hbuf_k = sa("hbuf", [128, 2, TC])
        xc = sa("xc", [HD, 2, TC])
        rstd = sa("rstd", [HD, TC])
        xpad = sa("xpad", [HD, 2, 2, NB, T + 2])
        dx = sa("dx", [HD, 2, 2, TC])
        xxx_k = sa("xxx", [128, 2, TC])
        sq_k = xxx_k
        m_a = sa("m_a", [128, TC])
        m_b = sa("m_b", [MR, TC])
        prod = sa("prod", [HD, 2, 2, TC])
        xs_k = sa("xs", [128, 2, 2, TC])
        xv_k = sa("xv", [128, 2, NB, TP])
        dect = sa("dect", [DDEC, TC])
        ew = sa("ew", [HD, 2, TC])
        cs = sa("cs", [HD, 2, TC])
        cb = sa("cb", [HD, 2, TC])
        ex = sa("ex", [HD, 2, 2, TC])
        kp = sa("kp", [HD, 2, TC + TP - T])
        kpar = sa("kpar", [HD, 2, 2, TC])
        rpar = sa("rpar", [HD, 2, 2, TC])
        ke = sa("ke", [HD, 2, 2, TC + TP - T])
        re = sa("re", [HD, 2, 2, 2, TC])
        th = sa("th", [HD, 2, TC])
        gate = th
        at = sa("at", [128, PP, HT])
        hbuf, xxx, sq, xs, xv = hbuf_k[0:HD], xxx_k[0:HD], sq_k[0:HD], xs_k[0:HD], xv_k[0:HD]
        actx.close()

        cctx = ExitStack()

        def sc(name, shape, dt=F32):
            return sb(name, shape, dt, cctx)
        wfc_s = sc("wfc_s", [128, 2, FH])
        wpr_s = sc("wpr_s", [128, FC, D])
        bfc_s = sc("bfc_s", [128, FC])
        bpr_s = sc("bpr_s", [1, D])
        alph_s = sc("alph_s", [NA, 2])
        aij = sc("aij", [NA, 1])
        din_s = sc("din_s", [NA, D])
        hout_s = sc("hout_s", [NA, FH])
        adin = sc("adin", [NA, D])
        ones_s = sc("ones_s", [1, 128])
        xpose = sc("xpose", [NSYS, K, 2, TP])
        pv = (sc("pv", [128, NSYS // 2, 3, K]),
              vring[:, 0:NSYS // 2 * 3 * K].rearrange("p (s u k) -> p s u k", u=3, k=K))
        atc = sc("atc", [128, PP, HT])
        yT_k = sc("yT", [128, 2, TC])
        yc = sc("yc", [HD, 2, TC])
        sqc_k = sc("sqc", [128, 2, TC])
        rsc = sc("rsc", [HD, 2, TC])
        gin = sc("gin", [HD, 2, TC])
        z_k = sc("z", [128, 2, 2, TC])
        hin = sc("hin", [HD, 2, TC])
        hc = sc("hc", [HD, 2, TC])
        sq2_k = sc("sq2", [128, 2, TC])
        rs2 = sc("rs2", [HD, TC])
        hact = gram[:, 0:FC * TC].rearrange("p (f t) -> p f t", f=FC)
        at_ = FC * TC
        osb = gram[:, at_:at_ + 3 * D].rearrange("p (n d) -> p n d", n=3)
        at_ += 3 * D
        h1_k = gram[:, at_:at_ + 4 * TC].rearrange("p (n a t) -> p n a t", n=2, a=2)
        at_ += 4 * TC
        hn_k = gram[:, at_:at_ + 4 * TC].rearrange("p (n a t) -> p n a t", n=2, a=2)
        yT, sqc, z, sq2, h1, hn = yT_k[0:HD], sqc_k[0:HD], z_k[0:HD], sq2_k[0:HD], h1_k[0:HD], hn_k[0:HD]
        cctx.close()

        bank = [ctx.enter_context(nc.psum_tensor(f"bank{i}", [128, 1024], F32)) for i in range(4)]
        def pair_of(i):
            return bank[i][:, :].rearrange("p (h c) -> p h c", h=2)

        chan_loaded, wtok_loaded, w_loaded = sem("chan_loaded"), sem("wtok_loaded"), sem("w_loaded")
        rows_zeroed = sem("rows_zeroed")
        memset_done, prep_done, temp_act, temp_ready = sem("memset_done"), sem("prep_done"), sem("temp_act"), sem("temp_ready")
        pat_loaded, h_ready, h_spilled = sem("pat_loaded"), sem("h_ready"), sem("h_spilled")
        xc_ready, sq_ready, rstd_log, rstd_ready = sem("xc_ready"), sem("sq_ready"), sem("rstd_log"), sem("rstd_ready")
        xn_ready, nbr_ready, dx_ready, xxx_ready = sem("xn_ready"), sem("nbr_ready"), sem("dx_ready"), sem("xxx_ready")
        m_ready, prod_ready, xs_ready = sem("m_ready"), sem("prod_ready"), sem("xs_ready")
        dect_ready, ew_ready, cs_ready = sem("dect_ready"), sem("ew_ready"), sem("cs_ready")
        cdiff_ready, clip_ready, e_ready = sem("cdiff_ready"), sem("clip_ready"), sem("e_ready")
        k_ready, r_ready, v_ready = sem("k_ready"), sem("r_ready"), sem("v_ready")
        th_ready, gate_ready, gate_spilled = sem("th_ready"), sem("gate_ready"), sem("gate_spilled")
        decayed_ready, f_ready = sem("decayed_ready"), sem("f_ready")
        at_ready, at_spilled = sem("at_ready"), sem("at_spilled")
        ring1_made, ring2_made, aux_made = sem("ring1_made"), sem("ring2_made"), sem("aux_made")
        sys_filled = sem("sys_filled")
        prep_dve, prep_act = sem("prep_dve"), sem("prep_act")
        dve_step = sem("dve_step")
        pool_step = sem("pool_step")
        xpose_ready, pv_ready = sem("xpose_ready"), sem("pv_ready")
        ffnw_loaded, c_memset, ffn_made, ffn_prep = sem("ffnw_loaded"), sem("c_memset"), sem("ffn_made"), sem("ffn_prep")
        at_loaded, gate_loaded, hin_loaded = sem("at_loaded"), sem("gate_loaded"), sem("hin_loaded")
        c1_made, c2_made = sem("c1_made"), sem("c2_made")
        yT_ready, yc_ready, sqc_ready, rsc_log, rsc_ready = (sem("yT_ready"), sem("yc_ready"),
                                                                      sem("sqc_ready"), sem("rsc_log"), sem("rsc_ready"))
        yn_ready, affine_ready, z_ready = sem("yn_ready"), sem("affine_ready"), sem("z_ready")
        h1_ready, hc_ready, sq2_ready, rs2_log, rs2_ready = (sem("h1_ready"), sem("hc_ready"), sem("sq2_ready"),
                                                             sem("rs2_log"), sem("rs2_ready"))
        hn_ready, hact_ready, osb_ready, out_stored = sem("hn_ready"), sem("hact_ready"), sem("osb_ready"), sem("out_stored")

        NTG, NTV = -(-T // 4), K // 4
        NFILL = NTG + NTV

        SLOTS, POOL_SLOTS = 21, 7
        DVE_SHARES = ((4,) + 6 * (4,) + 5 * (4,) + 6 * (4,) + (4, 4, 26),
                      (30, 30) + (SLOTS - 2) * (0,), SLOTS * (6,))
        BETWEEN, C_FIRST = NC + 2, NC + 3

        def stretch(iteration):
            return (iteration >= BETWEEN) + (iteration >= C_FIRST)

        DVE_PLACES = ((5 * SLOTS, 8 * SLOTS - 3), (8 * SLOTS, 12 * SLOTS), (12 * SLOTS, 16 * SLOTS - 6))
        POOL_PACE, POOL_LAG = (4500, 7000, 12000), 1

        def dve_plan():
            plan = {}
            for g, (first, end) in enumerate(DVE_PLACES):
                c = cuts([DVE_SHARES[stretch(place // SLOTS)][place % SLOTS] for place in range(first, end)], DVE_WORK[g])
                for n in range(end - first):
                    plan.setdefault(first + n, []).append((g, c[n], c[n + 1]))
            return plan

        def pool_plan(plan):
            given = {(g, n): place for place, parts in plan.items() for g, n0, n1 in parts for n in range(n0, n1)}
            todo = [(g, n) for g in range(NG) if DVE_COLS[g] < K for n in range(len(POOL_STEPS))]
            out, place = {}, 0
            while todo:
                work = 0
                while todo and work < POOL_PACE[stretch(place // POOL_SLOTS)]:
                    g, n = todo[0]
                    k, kind, _ = POOL_STEPS[n]
                    needed = {"outer": (k, "scale", 0), "rows": (T - 1, "recip", 0)}.get(kind)
                    if needed and given[g, STEP_AT[g][needed]] * POOL_SLOTS > (place - POOL_LAG) * SLOTS:
                        break
                    parts = out.setdefault(place, [])
                    if parts and parts[-1][0] == g:
                        parts[-1] = (g, parts[-1][1], n + 1)
                    else:
                        parts.append((g, n, n + 1))
                    work += POOL_WORK[n]
                    todo.pop(0)
                place += 1
            return out

        dve_parts = dve_plan()
        pool_parts = pool_plan(dve_parts)

        def c_iteration(j):
            return tuple(j - d if 0 <= j - d < NC else None for d in range(3))

        def group_needed(c):
            return next((g for g in range(NG) if NSYS * g // (H * PP) == c), None)

        def iteration(i):
            return (i if i < NC else None, i - 1 if 0 <= i - 1 < NC else None, i - 2 if 0 <= i - 2 < NC else None)

        def completed(c3):
            return next((g for g in range(NG) if group_chunk(g) == c3), None)

        def mix_count(c, n):
            return NMIX * c + n + 1

        def heads_count(c, p, q):
            return Q * (PP * c + p) + q + 1

        ring1, ring2, aux = Ring(1), Ring(2), Ring(2)
        for i in range(NC + 2):
            c1, c2, c3 = iteration(i)
            if c1 is not None:
                ring1.add(("embed", c1), (h_ready, 2 * c1 + 2))
                ring1.add(("mean", c1), (xc_ready, c1 + 1))
                ring1.add(("var", c1), (rstd_log, c1 + 1))
                ring1.add(("w1", c1), (m_ready, c1 + 1))
            if c2 is not None:
                reads = {"dec1": (dect_ready, c2 + 1), "dec2": (ew_ready, c2 + 1), "v": (v_ready, c2 + 1),
                         "g": (gate_ready, c2 + 1), "k": (k_ready, c2 + 1), "r": (r_ready, c2 + 1)}
                for what in ((0, 1, "dec1", 2, "v", 3, "dec2", "g", 4, "k", "r")):
                    if isinstance(what, int):
                        ring2.add(("mix", c2, what), (prod_ready, mix_count(c2, what)))
                    else:
                        ring2.add((what, c2), reads[what])
            if c3 is not None:
                for p in range(PP):
                    for q in range(Q):
                        aux.add(("heads", c3, p, q), (at_ready, heads_count(c3, p, q)))
                g = completed(c3)
                if g is not None:
                    for j in range(NFILL):
                        aux.add(("fill", g, j), (sys_filled, NFILL * g + j + 1))
        ringc1, ringc2 = Ring(1), Ring(3)
        for i in range(NC + 2):
                d1, d2, d3 = c_iteration(i)
                g = None if d1 is None else group_needed(d1)
                if g is not None:
                    for j in range(NTV // 2):
                        ringc1.add(("solution", g, j), (pv_ready, NTV // 2 * g + j + 1))
                if d1 is not None:
                    ringc1.add(("yT", d1), (yT_ready, d1 + 1))
                if d2 is not None:
                    ringc2.add(("wo", d2), (h1_ready, d2 + 1))
                if d3 is not None:
                    ringc2.add(("fc", d3, 0), (hact_ready, FC // 2 * d3 + 1))
                if d2 is not None:
                    ringc2.add(("lmean", d2), (hc_ready, d2 + 1))
                if d3 is not None:
                    ringc2.add(("fc", d3, 1), (hact_ready, FC // 2 * d3 + 2))
                if d1 is not None:
                    ringc1.add(("gmean", d1), (yc_ready, d1 + 1))
                if d2 is not None:
                    ringc2.add(("lvar", d2), (rs2_log, d2 + 1))
                if d3 is not None:
                    ringc2.add(("fc", d3, 2), (hact_ready, FC // 2 * d3 + 3))
                if d1 is not None:
                    ringc1.add(("gvar", d1), (rsc_log, d1 + 1))
                if d3 is not None:
                    ringc2.add(("proj", d3), (osb_ready, d3 + 1))

        dve_at = [sum(len(steps) for steps in DVE_STEPS[:g]) for g in range(NG + 1)]
        pool_at = [sum(len(POOL_STEPS) for c in DVE_COLS[:g] if c < K) for g in range(NG + 1)]

        def wait_free(eng, ring, key):
            read = ring.before(key)
            if read is not None:
                eng.wait_ge(*read)

        def wait_solved(eng, g):
            eng.wait_ge(dve_step, dve_at[g + 1])
            if DVE_COLS[g] < K:
                eng.wait_ge(pool_step, pool_at[g + 1])

        def phase_a_over(eng):
            eng.wait_ge(ring1_made, len(ring1.tasks))
            eng.wait_ge(ring2_made, len(ring2.tasks))
            eng.wait_ge(aux_made, aux.made(("heads", NC - 1, PP - 1, Q - 1)))
            eng.wait_ge(decayed_ready, 4 * NC)
            eng.wait_ge(at_ready, Q * PP * NC)
            eng.wait_ge(r_ready, NC)
            eng.wait_ge(e_ready, 4 * NC)
            eng.wait_ge(clip_ready, 2 * NC)
            eng.wait_ge(gate_ready, NC)
            eng.wait_ge(h_spilled, 16 * NC)
            eng.wait_ge(gate_spilled, 16 * NC)
            eng.wait_ge(at_spilled, 32 * NC)

        def need(c):
            return next(g for g in range(NG) if NSYS * (g + 1) >= H * PP * (c + 1))

        def tokens(c):
            return [(n, 128 * n, min(128, TC - 128 * n)) for n in range(-(-TC // 128))]

        block = ctx.enter_context(nc.Block())

        @block.sync
        def _(sp):
            sp.dma_start(chan_s[:, :], chan).then_inc(chan_loaded, 16)
            sp.dma_start(pat[:, :, :], patches[0]).then_inc(pat_loaded, 16)
            sp.dma_start(wtok_s[:, :, :], wtok).then_inc(wtok_loaded, 16)
            for dst, src in ((blocks_s[0:HD, :, :], blocks), (w1_s[0:HD, :, :], w1), (w2a_s[:, :], w2a), (w2b_s[:, :], w2b),
                             (dw1_s[0:HD, :, :], dw1), (dw2_s[:, :], dw2), (wproj4_s[0:HD, :, :, :], wkvrg),
                             (scan_s[:, :], scanmask), (tri_s[:, :], tri), (ident_s[:, :], ident),
                             (lucid_s[:, :], lucid), (wo_s[0:HD, :, :], wo)):
                sp.dma_start(dst, src).then_inc(w_loaded, 16)
            for i in range(NC + 2):
                c1, c2, c3 = iteration(i)
                if c1 is not None:
                    if c1 + 1 < NC:
                        sp.wait_ge(ring1_made, ring1.made(("embed", c1)))
                        sp.dma_start(pat[:, :, :], patches[c1 + 1]).then_inc(pat_loaded, 16)
                    sp.wait_ge(h_ready, 2 * c1 + 2)
                    sp.dma_start(h_dram[c1], hbuf[:, :, :].rearrange("p a t -> p (a t)")).then_inc(h_spilled, 16)
                if c2 is not None:
                    sp.wait_ge(gate_ready, c2 + 1)
                    sp.dma_start(gate_dram[c2], gate[:, :, :].rearrange("p a t -> p (a t)")).then_inc(gate_spilled, 16)
                if c3 is not None:
                    sp.wait_ge(at_ready, Q * PP * (c3 + 1))
                    for b2 in range(2):
                        sp.dma_start(at_dram[c3, b2], at[TP * b2:TP * b2 + T, :, :].rearrange("p a t -> p (a t)")
                                     ).then_inc(at_spilled, 16)
            phase_a_over(sp)
            for dst, src in ((wfc_s[0:HD, :, :], wfc), (wpr_s[:, :, :], wproj), (bfc_s[:, :], bfc), (bpr_s[:, :], bproj),
                             (alph_s[:, :], alphas), (din_s[:, :], din), (hout_s[:, :], hout)):
                sp.dma_start(dst, src).then_inc(ffnw_loaded, 16)

            def load_at(c):
                if c > 0:
                    sp.wait_ge(c1_made, ringc1.made(("yT", c - 1)))
                for b2 in range(2):
                    sp.dma_start(atc[TP * b2:TP * b2 + T, :, :],
                                 at_dram[c, b2].rearrange("p (a t) -> p a t", a=PP)).then_inc(at_loaded, 16)

            def load_gate(c):
                if c > 0:
                    sp.wait_ge(z_ready, c)
                sp.dma_start(gin[:, :, :].rearrange("p a t -> p (a t)"), gate_dram[c]).then_inc(gate_loaded, 16)

            load_at(0)
            load_gate(0)
            for i in range(NC + 2):
                d1, d2, d3 = c_iteration(i)
                if d1 is not None:
                    if d1 + 1 < NC:
                        load_at(d1 + 1)
                    if d1 > 0:
                        sp.wait_ge(h1_ready, d1)
                    sp.dma_start(hin[:, :, :].rearrange("p a t -> p (a t)"), h_dram[d1]).then_inc(hin_loaded, 16)
                if d3 is not None:
                    sp.wait_ge(osb_ready, d3 + 1)
                    for n, t0, nt in tokens(d3):
                        sp.dma_start(out[TC * d3 + t0:TC * d3 + t0 + nt, :], osb[0:nt, n, :]).then_inc(out_stored, 16)
                if d1 is not None and d1 + 1 < NC:
                    load_gate(d1 + 1)
            sp.wait_ge(out_stored, 16 * NC * len(tokens(0)))

        @block.tensor
        def _(pe):
            def mm(o, l, r, start=True, stop=True, at_tile=None):
                if at_tile is None:
                    return nc.tensor.matmul(o, l, r, start=start, stop=stop)
                return nc.tensor.matmul(o, l, r, start=start, stop=stop, tile_position=at_tile)

            r1 = pair_of(0)

            def two_halves(o, w, x):
                mm(o, w[:, 0], x[:, 0], True, False)
                return mm(o, w[:, 1], x[:, 1], False, True)

            def embed(c):
                pe.wait_ge(pat_loaded, 16 * (c + 1))
                wait_free(pe, ring1, ("embed", c))
                for half in range(2):
                    for f in range(FK):
                        last = mm(r1[0:HD, half, 0:PC], wtok_s[:, f, HD * half:HD * (half + 1)], pat[:, f, :],
                                  f == 0, f == FK - 1)
                last.then_inc(ring1_made, 1)

            def mean(c):
                pe.wait_ge(h_ready, 2 * c + 2)
                wait_free(pe, ring1, ("mean", c))
                mm(r1[0:HD, 0, 0:TC], blocks_s[:, 0, :], hbuf_k[:, 0, :], True, False)
                mm(r1[0:HD, 0, 0:TC], blocks_s[:, 0, :], hbuf_k[:, 1, :], False, True).then_inc(ring1_made, 1)

            def var(c):
                pe.wait_ge(sq_ready, c + 1)
                wait_free(pe, ring1, ("var", c))
                mm(r1[0:HD, 0, 0:TC], blocks_s[:, 0, :], sq_k[:, 0, :], True, False)
                mm(r1[0:HD, 0, 0:TC], blocks_s[:, 0, :], sq_k[:, 1, :], False, True).then_inc(ring1_made, 1)

            def lora_in(c):
                pe.wait_ge(xxx_ready, c + 1)
                wait_free(pe, ring1, ("w1", c))
                two_halves(r1[:, 0, 0:TC], w1_s[:, :, 0:128], xxx_k)
                two_halves(r1[0:MR, 1, 0:TC], w1_s[:, :, 128:128 + MR], xxx_k).then_inc(ring1_made, 1)

            def slot2(key):
                return pair_of(1 + ring2.slot(key))

            def mix(c, n):
                key, m = ("mix", c, n), MIXES[n]
                if n == 0:
                    pe.wait_ge(m_ready, c + 1)
                wait_free(pe, ring2, key)
                w2, mt, row = (w2a_s, m_a, MR * m) if m < 4 else (w2b_s, m_b, 0)
                for half in range(2):
                    last = mm(slot2(key)[0:HD, half, 0:TC], w2[row:row + MR, HD * half:HD * (half + 1)],
                              mt[row:row + MR, :], at_tile=(row, 0))
                last.then_inc(ring2_made, 1)

            def decay_in(c):
                pe.wait_ge(xs_ready, mix_count(c, 0))
                wait_free(pe, ring2, ("dec1", c))
                two_halves(slot2(("dec1", c))[0:DDEC, 0, 0:TC], dw1_s, xs_k[:, 0]).then_inc(ring2_made, 1)

            def decay_out(c):
                pe.wait_ge(dect_ready, c + 1)
                wait_free(pe, ring2, ("dec2", c))
                for half in range(2):
                    last = mm(slot2(("dec2", c))[0:HD, half, 0:TC], dw2_s[:, HD * half:HD * (half + 1)], dect[:, :])
                last.then_inc(ring2_made, 1)

            def project(c, what):
                n, w, x = {"k": (3, 0, 0), "r": (4, 2, 1), "g": (2, 3, 1)}[what]
                pe.wait_ge(xs_ready, mix_count(c, n))
                wait_free(pe, ring2, (what, c))
                for half in range(2):
                    last = two_halves(slot2((what, c))[0:HD, half, 0:TC],
                                      wproj4_s[:, w, :, HD * half:HD * (half + 1)], xs_k[:, x])
                last.then_inc(ring2_made, 1)

            def project_v(c):
                pe.wait_ge(xs_ready, mix_count(c, 1))
                wait_free(pe, ring2, ("v", c))
                for p in range(PP):
                    o = slot2(("v", c))[:, p // 2, D * (p % 2):D * (p % 2 + 1)]
                    for half in range(2):
                        last = mm(o, xv_k[:, half, 2 * p:2 * p + 2, :].rearrange("p b t -> p (b t)"),
                                  wproj4_s[:, 1, half, :], half == 0, half == 1)
                last.then_inc(ring2_made, 1)

            def aux_bank(key):
                s = aux.slot(key)
                return bank[3][:, 512 * s:512 * (s + 1)]

            def head_matrices(c, p):
                for q in range(Q):
                    key, row = ("heads", c, p, q), 32 * q
                    wait_free(pe, aux, key)
                    o = aux_bank(key)
                    for n, (left, right) in enumerate(((kp, kpar), (ke[:, 0], re[:, 0]), (ke[:, 1], re[:, 1]))):
                        if p == 0 and q == 0:
                            pe.wait_ge(*((decayed_ready, 4 * c + 2 * n) if n else (k_ready, c + 1)))
                        for half in range(2):
                            for b2 in range(2):
                                t0 = T * (2 * p + b2)
                                col = 2 * T * (2 * n + half)
                                last = mm(o[TP * b2:TP * (b2 + 1), col:col + 2 * T], left[row:row + 32, half, t0:t0 + TP],
                                          right[row:row + 32, :, half, t0:t0 + T], at_tile=(row, TP * b2))
                    last.then_inc(aux_made, 1)

            def fill(g):
                base = NSYS * (g % 2)
                for j in range(NFILL):
                    key = ("fill", g, j)
                    wait_free(pe, aux, key)
                    if j == 0:
                        pe.wait_ge(f_ready, Q * PP * (group_chunk(g) + 1))
                    if j == NTG:
                        pe.wait_ge(v_ready, group_chunk(g) + 1)
                    for n in range(4):
                        if j < NTG and 4 * j + n < T:
                            src = gram_v[:, base:base + NSYS, 4 * j + n]
                        elif j >= NTG:
                            src = v_v[:, base:base + NSYS, 4 * (j - NTG) + n]
                        else:
                            break
                        last = nc.tensor.transpose(aux_bank(key)[:, 128 * n:128 * (n + 1)], src, ident_s[:, :])
                    last.then_inc(aux_made, 1)

            pe.wait_ge(wtok_loaded, 16)
            pe.wait_ge(rows_zeroed, 1)
            for i in range(NC + 2):
                c1, c2, c3 = iteration(i)
                if c1 is not None:
                    embed(c1)
                    if c1 == 0:
                        pe.wait_ge(w_loaded, 16 * 12)
                if c2 is not None:
                    mix(c2, 0)
                    mix(c2, 1)
                if c3 is not None:
                    head_matrices(c3, 0)
                    head_matrices(c3, 1)
                if c1 is not None:
                    mean(c1)
                if c2 is not None:
                    decay_in(c2)
                    mix(c2, 2)
                if c1 is not None:
                    var(c1)
                if c2 is not None:
                    project_v(c2)
                    mix(c2, 3)
                    decay_out(c2)
                if c3 is not None:
                    head_matrices(c3, 2)
                    head_matrices(c3, 3)
                    if completed(c3) is not None:
                        fill(completed(c3))
                if c2 is not None:
                    project(c2, "g")
                    mix(c2, 4)
                if c1 is not None:
                    lora_in(c1)
                if c2 is not None:
                    project(c2, "k")
                    project(c2, "r")

            c1p, c2p = pair_of(1), (pair_of(0), pair_of(2), pair_of(3))
            phase_a_over(pe)
            pe.wait_ge(rows_zeroed, 2)

            def mixed_coefficients(part):
                if part == 0:
                    pe.wait_ge(ffn_prep, 1)
                    pe.wait_ge(ffnw_loaded, 16 * 7)
                    for half in range(2):
                        for n in range(2):
                            mm(c2p[half][0:HD, n, 0:FH // 2], adin[:, HD * half:HD * (half + 1)],
                               hout_s[:, FH // 2 * n:FH // 2 * (n + 1)])
                    for n in range(2):
                        last = mm(c2p[2][:, n, 0:D], hout_s[:, 128 * n:128 * (n + 1)], adin[:, :])
                    last.then_inc(ffn_made, 1)
                else:
                    pe.wait_ge(ffn_prep, 2)
                    for n in range(2, FC):
                        j = n - 2
                        mm(c2p[j // 2][:, j % 2, 0:D], hout_s[:, 128 * n:128 * (n + 1)], adin[:, :])
                    for n in range(FC):
                        mm(c2p[2][:, 0, n:n + 1], hout_s[:, 128 * n:128 * (n + 1)], aij[:, :])
                    mm(c2p[2][0:1, 1, 0:D], aij[:, :], din_s[:, :]).then_inc(ffn_made, 1)
                    pe.wait_ge(ffn_prep, 3)

            def c1slot(key):
                wait_free(pe, ringc1, key)
                return c1p

            def c2slot(key):
                wait_free(pe, ringc2, key)
                return c2p[ringc2.slot(key)]

            def solution(g):
                for j in range(NTV // 2):
                    o = c1slot(("solution", g, j))
                    if j == 0:
                        pe.wait_ge(xpose_ready, g + 1)
                    for n in range(8):
                        last = nc.tensor.transpose(o[:, n // 4, 128 * (n % 4):128 * (n % 4 + 1)],
                                                   xpose[:, 8 * j + n, :, :].rearrange("p b t -> p (b t)"), ident_s[:, :])
                    last.then_inc(c1_made, 1)

            def apply_a(c):
                o = c1slot(("yT", c))
                pe.wait_ge(at_loaded, 32 * (c + 1))
                pe.wait_ge(pv_ready, NTV // 2 * (need(c) + 1))
                for p in range(PP):
                    for h in range(H):
                        s = H * (PP * c + p) + h
                        half, q, odd = h // (H // 2), h % (H // 2) // 2, h % 2
                        for b2 in range(2):
                            rows, col = slice(TP * b2, TP * b2 + T), T * (PP * half + p)
                            last = mm(o[32 * q:32 * (q + 1), b2, col:col + T],
                                      pv[s // NSYS % 2][rows, s % NSYS // 2, odd:odd + 2, :].rearrange("p u k -> p (u k)"),
                                      atc[rows, p, T * h:T * (h + 1)], odd == 0, odd == 1, at_tile=(TP * b2, 32 * q))
                last.then_inc(c1_made, 1)

            def per_head(c, key, ready, x):
                pe.wait_ge(ready, c + 1)
                o = c1slot((key, c))
                for half in range(2):
                    last = mm(o[0:HD, half, 0:TC], blocks_s[:, 1, :], x[:, half, :])
                last.then_inc(c1_made, 1)

            def attention_out(c):
                pe.wait_ge(z_ready, c + 1)
                o = c2slot(("wo", c))
                for half in range(2):
                    last = two_halves(o[0:HD, half, 0:TC], wo_s[:, :, HD * half:HD * (half + 1)], z_k[:, c % 2])
                last.then_inc(c2_made, 1)

            def per_token(c, key, ready, x):
                pe.wait_ge(ready, c + 1)
                o = c2slot((key, c))
                mm(o[0:HD, 0, 0:TC], blocks_s[:, 0, :], x[:, 0, :], True, False)
                mm(o[0:HD, 0, 0:TC], blocks_s[:, 0, :], x[:, 1, :], False, True).then_inc(c2_made, 1)

            def ffn_in(c, j):
                if j == 0:
                    pe.wait_ge(hn_ready, c + 1)
                o = c2slot(("fc", c, j))
                for n in range(2):
                    f = 2 * j + n
                    last = two_halves(o[:, n, 0:TC], wfc_s[:, :, 128 * f:128 * (f + 1)], hn_k[:, c % 2])
                last.then_inc(c2_made, 1)

            def ffn_out(c):
                o = c2slot(("proj", c))
                pe.wait_ge(hact_ready, FC // 2 * (c + 1))
                for n, t0, nt in tokens(c):
                    dst = o[0:nt, n // 2, D * (n % 2):D * (n % 2 + 1)]
                    for f in range(FC):
                        mm(dst, hact[:, f, t0:t0 + nt], wpr_s[:, f, :], f == 0, False)
                    for half in range(2):
                        mm(dst[:, HD * half:HD * (half + 1)], h1_k[:, c % 2, half, t0:t0 + nt], ident_s[:, 0:HD], False, False)
                    last = mm(dst, ones_s[:, 0:nt], bpr_s[:, :], False, True)
                last.then_inc(c2_made, 1)

            for i in range(NC + 2):
                    d1, d2, d3 = c_iteration(i)
                    if d1 is not None:
                        if group_needed(d1) is not None:
                            solution(group_needed(d1))
                        apply_a(d1)
                        if d1 == 0:
                            mixed_coefficients(0)
                    if d2 is not None:
                        attention_out(d2)
                    if d3 is not None:
                        ffn_in(d3, 0)
                    if d2 is not None:
                        per_token(d2, "lmean", h1_ready, h1_k[:, d2 % 2])
                    if d3 is not None:
                        ffn_in(d3, 1)
                    if d1 is not None:
                        per_head(d1, "gmean", yT_ready, yT_k)
                    if d2 is not None:
                        per_token(d2, "lvar", sq2_ready, sq2_k)
                    if d3 is not None:
                        ffn_in(d3, 2)
                    if d1 is not None:
                        per_head(d1, "gvar", sqc_ready, sqc_k)
                        if d1 == 0:
                            mixed_coefficients(1)
                    if d3 is not None:
                        ffn_out(d3)

        @block.scalar
        def _(act):
            r1, a = pair_of(0), nc.scalar.activation

            def slot2(key):
                return pair_of(1 + ring2.slot(key))

            def aux_bank(key):
                s = aux.slot(key)
                return bank[3][:, 512 * s:512 * (s + 1)]

            act.wait_ge(w_loaded, 16 * 12)
            nc.scalar.preload_act_table_set("natural_log_exp_and_others")
            a(tmp3[:, 0, :], lucid_s[:, :], ACT.Abs).then_inc(temp_act, 1)
            act.wait_ge(temp_act, 1)
            a(tmp3[:, 1, :], tmp3[:, 0, :], ACT.Exp, scale=-1.0).then_inc(temp_act, 1)
            act.wait_ge(temp_act, 2)
            act.wait_ge(memset_done, 1)
            a(tmp3[:, 0, :], tmp3[:, 1, :], ACT.Ln, bias=1.0).then_inc(temp_act, 1)

            def square(c):
                act.wait_ge(xc_ready, c + 1)
                if c > 0:
                    act.wait_ge(ring1_made, ring1.made(("w1", c - 1)))
                a(sq[:, :, :], xc[:, :, :], ACT.Square).then_inc(sq_ready, 1)

            def inverse_std(c):
                nc.scalar.preload_act_table_set("natural_log_exp_and_others")
                act.wait_ge(ring1_made, ring1.made(("var", c)))
                if c > 0:
                    act.wait_ge(xn_ready, c)
                a(rstd[:, :], r1[0:HD, 0, 0:TC], ACT.Ln, bias=eps_s[0:HD, 0:1]).then_inc(rstd_log, 1)
                act.wait_ge(rstd_log, c + 1)
                a(rstd[:, :], rstd[:, :], ACT.Exp, scale=-0.5).then_inc(rstd_ready, 1)

            def lora_tanh(c):
                act.wait_ge(ring1_made, ring1.made(("w1", c)))
                if c > 0:
                    act.wait_ge(ring2_made, ring2.made(("mix", c - 1, 4)))
                a(m_a[:, :], r1[:, 0, 0:TC], ACT.Tanh)
                a(m_b[:, :], r1[0:MR, 1, 0:TC], ACT.Tanh).then_inc(m_ready, 1)

            def decay_tanh(c):
                act.wait_ge(ring2_made, ring2.made(("dec1", c)))
                if c > 0:
                    act.wait_ge(ring2_made, ring2.made(("dec2", c - 1)))
                a(dect[:, :], slot2(("dec1", c))[0:DDEC, 0, 0:TC], ACT.Tanh).then_inc(dect_ready, 1)

            def decay_exp(c):
                act.wait_ge(ring2_made, ring2.made(("dec2", c)))
                if c > 0:
                    act.wait_ge(e_ready, 4 * c)
                for half in range(2):
                    last = a(ew[:, half, :], slot2(("dec2", c))[0:HD, half, 0:TC], ACT.Exp,
                             bias=chan_s[:, V_TD + half:V_TD + half + 1])
                last.then_inc(ew_ready, 1)

            def copy_v(c):
                act.wait_ge(ring2_made, ring2.made(("v", c)))
                if H * PP * (c + 1) > GR:
                    act.wait_ge(aux_made, aux.made(("fill", 0, NFILL - 1)))
                for n in range(2):
                    for ro, so, m in pieces(H * (PP * c + 2 * n), 2 * H):
                        last = nc.scalar.copy(vring[:, K * ro:K * (ro + m)],
                                              slot2(("v", c))[:, n, K * so:K * (so + m)])
                last.then_inc(v_ready, 1)

            def gate_tanh(c):
                act.wait_ge(ring2_made, ring2.made(("g", c)))
                if c > 0:
                    act.wait_ge(gate_spilled, 16 * c)
                a(th[:, :, :], slot2(("g", c))[0:HD, :, 0:TC], ACT.Tanh, scale=0.5).then_inc(th_ready, 1)

            def decay_factors(c, e):
                act.wait_ge(clip_ready, 2 * c + 1 + e // 2)
                n = 4 * c + e
                if n >= 2:
                    act.wait_ge(decayed_ready, n - 1)
                src, scale = ((ew, 1.0), (ew, -1.0), (cs, -1.0), (cs, 1.0))[e]
                a(ex[:, e % 2], src[:, :, :], ACT.Exp, scale=scale).then_inc(e_ready, 1)

            def copy_k(c):
                act.wait_ge(ring2_made, ring2.made(("k", c)))
                if c > 0:
                    act.wait_ge(aux_made, aux.made(("heads", c - 1, PP - 1, Q - 1)))
                    act.wait_ge(decayed_ready, 4 * c)
                src = slot2(("k", c))[0:HD, :, 0:TC]
                nc.scalar.copy(kp[:, :, 0:TC], src)
                for par in range(2):
                    last = nc.scalar.activation(kpar[:, par], src, ACT.Copy, scale=chan_s[:, V_PAR + par:V_PAR + par + 1])
                last.then_inc(k_ready, 1)

            def copy_r(c):
                act.wait_ge(ring2_made, ring2.made(("r", c)))
                if c > 0:
                    act.wait_ge(decayed_ready, 4 * c)
                for par in range(2):
                    last = nc.scalar.activation(rpar[:, par], slot2(("r", c))[0:HD, :, 0:TC], ACT.Copy,
                                                scale=chan_s[:, V_PAR + par:V_PAR + par + 1])
                last.then_inc(r_ready, 1)

            def copy_matrices(c, p):
                first = H * (PP * c + p)
                if first + H > GR:
                    act.wait_ge(aux_made, aux.made(("fill", 0, NFILL - 1)))
                if c > 0 and p == 0:
                    act.wait_ge(at_spilled, 32 * c)
                for q in range(Q):
                    key = ("heads", c, p, q)
                    act.wait_ge(aux_made, aux.made(key))
                    src = aux_bank(key)[:, 0:4 * T].rearrange("p (a n) -> p a n", a=2)
                    s0, s1 = (first + 2 * q) % GR, (first + H // 2 + 2 * q) % GR
                    if s1 > s0:
                        a0 = min(s0, GR - H)
                        nc.scalar.copy(gram[:, T * a0:T * (a0 + H)].rearrange("p (a n) -> p a n", a=2)[
                            :, :, T * (s0 - a0):T * (s0 - a0 + 2)], src)
                    else:
                        nc.scalar.copy(gram[:, T * s0:T * (s0 + 2)], src[:, 0])
                        nc.scalar.copy(gram[:, T * s1:T * (s1 + 2)], src[:, 1])
                    nc.scalar.copy(at[:, p, :].rearrange("p (a n) -> p a n", a=2)[:, :, 2 * T * q:2 * T * (q + 1)],
                                   aux_bank(key)[:, 4 * T:8 * T].rearrange("p (a n) -> p a n", a=2)).then_inc(f_ready, 1)

            def fill(g):
                m = sysm[:, g % 2]
                for j in range(NFILL):
                    key = ("fill", g, j)
                    act.wait_ge(aux_made, aux.made(key))
                    if j == 0 and g == 2:
                        act.wait_ge(xpose_ready, 1)
                    src = aux_bank(key)[:, :].rearrange("p (n b t) -> p n b t", n=4, b=2)
                    if j < NTG:
                        n = min(4, T - 4 * j)
                        dst = m[:, :, 4 * j:4 * j + n, 0:T].rearrange("p b n t -> p n b t")
                    else:
                        n = 4
                        k0 = T + 4 * (j - NTG)
                        dst = m[:, :, :, k0:k0 + 4].rearrange("p b t n -> p n b t")
                    nc.scalar.copy(dst, src[:, 0:n, :, 0:T]).then_inc(sys_filled, 1)

            def inverse_norms(g):
                act.wait_ge(prep_dve, 5 * g + 1)
                a(nrm[:, :, :], nrm[:, :, :], ACT.Ln).then_inc(prep_act, 1)
                act.wait_ge(prep_act, 3 * g + 1)
                a(nrm[:, :, :], nrm[:, :, :], ACT.Exp, scale=-0.5).then_inc(prep_act, 1)

            def similarity_exp(g):
                act.wait_ge(prep_dve, 5 * g + 3)
                act.wait_ge(temp_ready, 1)
                a(sysm[:, g % 2, :, :, 0:T], sysm[:, g % 2, :, :, 0:T], ACT.Exp, scale=temp[:, g:g + 1]).then_inc(prep_act, 1)

            def solution_out(g):
                wait_solved(act, g)
                if g > 0:
                    act.wait_ge(c1_made, ringc1.made(("solution", g - 1, NTV // 2 - 1)))
                else:
                    act.wait_ge(c_memset, 1)
                for b2 in range(2):
                    last = nc.scalar.copy(xpose[:, :, b2, 0:T], sysm[:, g % 2, b2, :, T:W].rearrange("p t k -> p k t"))
                last.then_inc(xpose_ready, 1)

            def solution_in(g):
                for j in range(NTV // 2):
                    act.wait_ge(c1_made, ringc1.made(("solution", g, j)))
                    if j == 0:
                        act.wait_ge(c_memset, 2)
                        if g > 1:
                            act.wait_ge(c1_made, ringc1.made(("yT", (NSYS * (g - 1) - 1) // (H * PP))))
                    for n in range(2):
                        k0 = 8 * j + 4 * n
                        last = nc.scalar.copy(pv[g % 2][:, :, 0:3:2, k0:k0 + 4].rearrange("p s u k -> p k s u"),
                                              pair_of(1)[:, n, :].rearrange("p (k s u) -> p k s u", k=4, u=2))
                    last.then_inc(pv_ready, 1)

            for i in range(NC + 2):
                c1, c2, c3 = iteration(i)
                if c3 is not None:
                    copy_matrices(c3, 0)
                    copy_matrices(c3, 1)
                if c1 is not None:
                    square(c1)
                if c2 is not None:
                    decay_tanh(c2)
                if c1 is not None:
                    inverse_std(c1)
                if c2 is not None:
                    copy_v(c2)
                    decay_exp(c2)
                if c3 is not None:
                    copy_matrices(c3, 2)
                    copy_matrices(c3, 3)
                    if completed(c3) in (0, 1):
                        fill(completed(c3))
                if c2 is not None:
                    gate_tanh(c2)
                if c1 is not None:
                    lora_tanh(c1)
                if c3 is not None and completed(c3) in (0, 1):
                    inverse_norms(completed(c3))
                if c2 is not None:
                    decay_factors(c2, 0)
                    copy_k(c2)
                    copy_r(c2)
                    for e in range(1, 4):
                        decay_factors(c2, e)
                if c3 is not None and completed(c3) in (0, 1):
                    similarity_exp(completed(c3))
            phase_a_over(act)
            solution_out(0)
            fill(2)

            c1p, c2p = pair_of(1), (pair_of(0), pair_of(2), pair_of(3))

            def copy_yT(c):
                act.wait_ge(c1_made, ringc1.made(("yT", c)))
                if c > 0:
                    act.wait_ge(yc_ready, c)
                for b2 in range(2):
                    last = nc.scalar.copy(yT[:, :, :].rearrange("p a (n b t) -> p a n b t", n=PP, b=2)[:, :, :, b2, :],
                                          c1p[0:HD, b2, 0:TC].rearrange("p (a n t) -> p a n t", a=2, n=PP))
                last.then_inc(yT_ready, 1)

            def square_y(c):
                act.wait_ge(yc_ready, c + 1)
                if c > 0:
                    act.wait_ge(c1_made, ringc1.made(("gvar", c - 1)))
                a(sqc[:, :, :], yc[:, :, :], ACT.Square).then_inc(sqc_ready, 1)

            def inverse_std_y(c):
                nc.scalar.preload_act_table_set("natural_log_exp_and_others")
                act.wait_ge(c1_made, ringc1.made(("gvar", c)))
                if c > 0:
                    act.wait_ge(yn_ready, c)
                a(rsc[:, :, :], c1p[0:HD, :, 0:TC], ACT.Ln, bias=eps_s[0:HD, 1:2]).then_inc(rsc_log, 1)
                act.wait_ge(rsc_log, c + 1)
                a(rsc[:, :, :], rsc[:, :, :], ACT.Exp, scale=-0.5).then_inc(rsc_ready, 1)

            def affine(c):
                act.wait_ge(yn_ready, c + 1)
                for half in range(2):
                    last = a(yc[:, half, :], yc[:, half, :], ACT.Identity, scale=chan_s[:, V_LNW + half:V_LNW + half + 1],
                             bias=chan_s[:, V_LNB + half:V_LNB + half + 1])
                last.then_inc(affine_ready, 1)

            def square_h(c):
                act.wait_ge(hc_ready, c + 1)
                if c > 0:
                    act.wait_ge(c2_made, ringc2.made(("lvar", c - 1)))
                a(sq2[:, :, :], hc[:, :, :], ACT.Square).then_inc(sq2_ready, 1)

            def inverse_std_h(c):
                nc.scalar.preload_act_table_set("natural_log_exp_and_others")
                act.wait_ge(c2_made, ringc2.made(("lvar", c)))
                if c > 0:
                    act.wait_ge(hn_ready, c)
                a(rs2[:, :], c2p[ringc2.slot(("lvar", c))][0:HD, 0, 0:TC], ACT.Ln, bias=eps_s[0:HD, 0:1]
                  ).then_inc(rs2_log, 1)
                act.wait_ge(rs2_log, c + 1)
                a(rs2[:, :], rs2[:, :], ACT.Exp, scale=-0.5).then_inc(rs2_ready, 1)

            def gelu(c, j):
                act.wait_ge(c2_made, ringc2.made(("fc", c, j)))
                if c > 0 and j == 0:
                    act.wait_ge(c2_made, ringc2.made(("proj", c - 1)))
                if c == 0:
                    act.wait_ge(ffn_prep, 3)
                for n in range(2):
                    f = 2 * j + n
                    last = a(hact[:, f, :], c2p[ringc2.slot(("fc", c, j))][:, n, 0:TC], ACT.Gelu_apprx_tanh,
                             bias=bfc_s[:, f:f + 1])
                last.then_inc(hact_ready, 1)

            for i in range(NC + 2):
                    d1, d2, d3 = c_iteration(i)
                    if d1 is not None:
                        g = group_needed(d1)
                        if g is not None:
                            if g > 0:
                                solution_out(g)
                            solution_in(g)
                        copy_yT(d1)
                    if i == 0:
                        inverse_norms(NG - 1)
                    if d3 is not None:
                        gelu(d3, 0)
                    if d2 is not None:
                        square_h(d2)
                    if d3 is not None:
                        gelu(d3, 1)
                    if d1 is not None:
                        square_y(d1)
                    if d3 is not None:
                        gelu(d3, 2)
                    if d2 is not None:
                        inverse_std_h(d2)
                    if d1 is not None:
                        inverse_std_y(d1)
                        affine(d1)
                    if i == 0:
                        similarity_exp(NG - 1)

        @block.gpsimd
        def _(pool):
            tt = nc.gpsimd.tensor_tensor
            nc.gpsimd.memset(eps_s[:, 0:1], LN_EPS)
            nc.gpsimd.memset(eps_s[:, 1:2], GN_EPS)
            nc.gpsimd.memset(xpad[:, :, :, :, :], 0.0)
            nc.gpsimd.memset(xv[:, :, :, :], 0.0)
            nc.gpsimd.memset(kp[:, :, TC:TC + TP - T], 0.0)
            nc.gpsimd.memset(ke[:, :, :, TC:TC + TP - T], 0.0).then_inc(memset_done, 1)

            def token_view(x):
                return x.rearrange("p a (b t) -> p (a b) t", t=T)

            def neighbours(c):
                pool.wait_ge(xn_ready, c + 1)
                x = xpad[:, c % 2].rearrange("p a b t -> p (a b) t")
                tt(token_view(dx[:, c % 2]), x[:, :, 0:T], x[:, :, 2:T + 2], ALU.add).then_inc(nbr_ready, 1)

            def mixed(c, n):
                pool.wait_ge(prod_ready, mix_count(c, n))
                slot = (NMIX * c + n) % 2
                x = xpad[:, c % 2].rearrange("p a b t -> p (a b) t")[:, :, 1:T + 1]
                if n == 1:
                    if c > 0:
                        pool.wait_ge(ring2_made, ring2.made(("v", c - 1)))
                    dst = xv[:, :, :, :].rearrange("p a b t -> p (a b) t")[:, :, 0:T]
                else:
                    which = {0: 0, 2: 1, 3: 0, 4: 1}[n]
                    if n == 0 and c > 0:
                        pool.wait_ge(ring2_made, ring2.made(("k", c - 1)))
                    if n == 2 and c > 0:
                        pool.wait_ge(ring2_made, ring2.made(("r", c - 1)))
                    if n == 3:
                        pool.wait_ge(ring2_made, ring2.made(("dec1", c)))
                    if n == 4:
                        pool.wait_ge(ring2_made, ring2.made(("g", c)))
                    dst = token_view(xs[:, which])
                tt(dst, token_view(prod[:, slot]), x, ALU.add).then_inc(xs_ready, 1)

            def decay_sums(c):
                pool.wait_ge(cs_ready, c + 1)
                if c > 0:
                    pool.wait_ge(cdiff_ready, 3 * c)
                tt(cb[:, :, :], cs[:, :, :], ew[:, :, :], ALU.add).then_inc(cdiff_ready, 1)
                pool.wait_ge(cdiff_ready, 3 * c + 1)

                def centred(dst, src):
                    s = token_view(src)
                    mid = s[:, :, MID:MID + 1].broadcast_to([HD, 2 * NB, T])
                    return tt(token_view(dst), s, mid, ALU.subtract)
                centred(ew, cs).then_inc(cdiff_ready, 1)
                pool.wait_ge(cdiff_ready, 3 * c + 2)
                centred(cs, cb).then_inc(cdiff_ready, 1)

            def decayed(c, e):
                pool.wait_ge(e_ready, 4 * c + e + 1)
                if e == 0:
                    pool.wait_ge(k_ready, c + 1)
                    pool.wait_ge(r_ready, c + 1)
                    if c > 0:
                        pool.wait_ge(aux_made, aux.made(("heads", c - 1, PP - 1, Q - 1)))
                f = ex[:, e % 2]
                if e % 2 == 0:
                    f2 = f.unsqueeze(1).broadcast_to([HD, 2, 2, TC])
                    last = tt(re[:, e // 2], rpar[:, :, :, :], f2, ALU.mult)
                else:
                    last = tt(ke[:, e // 2, :, 0:TC], kp[:, :, 0:TC], f, ALU.mult)
                last.then_inc(decayed_ready, 1)

            def pool_solve(g, first, end):
                c = DVE_COLS[g]
                if c == K:
                    return
                m, n0 = sysm[:, g % 2], pool_at[g]
                for n in range(first, end):
                    k, kind, _ = POOL_STEPS[n]
                    if kind == "outer":
                        pool.wait_ge(dve_step, dve_at[g] + STEP_AT[g][k, "scale", 0] + 1)
                    if n0 + n > 0:
                        pool.wait_ge(pool_step, n0 + n)
                    v, rows = m[:, :, :, T + c:W], slice(k + 1, T) if kind in ("outer", "subtract") else slice(0, k)
                    if kind == "rows":
                        pool.wait_ge(dve_step, dve_at[g] + STEP_AT[g][T - 1, "recip", 0] + 1)
                        tt(v, v, rdiag[:, g % 2].unsqueeze(3).broadcast_to([NSYS, 2, T, K - c]), ALU.mult
                           ).then_inc(pool_step, 1)
                        continue
                    count = rows.stop - rows.start
                    o = outer_b[:, 0:2 * count * (K - c)].rearrange("p (b i c) -> p b i c", b=2, c=K - c)
                    if kind in ("outer", "back_outer"):
                        u = m[:, :, rows, k] if kind == "outer" else m[:, :, k, rows]
                        tt(o, u.unsqueeze(3).broadcast_to([NSYS, 2, count, K - c]),
                           v[:, :, k].unsqueeze(2).broadcast_to([NSYS, 2, count, K - c]), ALU.mult).then_inc(pool_step, 1)
                    else:
                        tt(v[:, :, rows], v[:, :, rows], o, ALU.subtract).then_inc(pool_step, 1)

            def solve(i, slot):
                for part in pool_parts.get(POOL_SLOTS * i + slot, ()):
                    pool_solve(*part)

            for i in range(NC + 2):
                c1, c2, c3 = iteration(i)
                if c2 is not None:
                    mixed(c2, 0)
                    mixed(c2, 1)
                solve(i, 0)
                solve(i, 1)
                if c2 is not None:
                    mixed(c2, 2)
                solve(i, 2)
                if c1 is not None:
                    neighbours(c1)
                if c2 is not None:
                    mixed(c2, 3)
                solve(i, 3)
                if c2 is not None:
                    decay_sums(c2)
                solve(i, 4)
                if c2 is not None:
                    mixed(c2, 4)
                solve(i, 5)
                if c2 is not None:
                    for e in range(4):
                        decayed(c2, e)
                solve(i, 6)
            phase_a_over(pool)
            nc.gpsimd.memset(xpose[:, :, :, :], 0.0)
            nc.gpsimd.memset(ones_s[:, :], 1.0).then_inc(c_memset, 1)
            nc.gpsimd.memset(pv[0][:, :, 1, :], 0.0)
            pool.wait_ge(aux_made, aux.made(("fill", NG - 1, NFILL - 1)))
            nc.gpsimd.memset(pv[1][:, :, 1, :], 0.0).then_inc(c_memset, 1)

            for slot in range(POOL_SLOTS):
                solve(BETWEEN, slot)

            def gated(c):
                pool.wait_ge(affine_ready, c + 1)
                pool.wait_ge(gate_loaded, 16 * (c + 1))
                if c > 1:
                    pool.wait_ge(c2_made, ringc2.made(("wo", c - 2)))
                tt(z[:, c % 2], yc[:, :, :], gin[:, :, :], ALU.mult).then_inc(z_ready, 1)

            for i in range(NC + 2):
                for slot in range(POOL_SLOTS // 2):
                    solve(C_FIRST + i, slot)
                if c_iteration(i)[0] is not None:
                    gated(i)
                for slot in range(POOL_SLOTS // 2, POOL_SLOTS):
                    solve(C_FIRST + i, slot)

        @block.vector
        def _(dve):
            tt, ts, stt = nc.vector.tensor_tensor, nc.vector.tensor_scalar, nc.vector.scalar_tensor_tensor
            r1 = pair_of(0)

            def slot2(key):
                return pair_of(1 + ring2.slot(key))

            def token_view(x):
                return x.rearrange("p a (b t) -> p (a b) t", t=T)

            for x in (hbuf_k, blocks_s, xxx_k, xs_k, xv_k, w1_s, dw1_s, wproj4_s, wo_s):
                last = nc.vector.memset(x[HD:128], 0.0)
            last.then_inc(rows_zeroed, 1)
            dve.wait_ge(chan_loaded, 16)
            for half in range(2):
                ts(posb[:, half, :], chan_s[:, V_POS + NPT * half:V_POS + NPT * (half + 1)],
                   chan_s[:, V_TOKB + half:V_TOKB + half + 1], None, ALU.add).then_inc(prep_done, 1)
            dve.wait_ge(prep_done, 2)

            def embedded(c):
                if c > 0:
                    dve.wait_ge(h_spilled, 16 * c)
                    dve.wait_ge(ring1_made, ring1.made(("mean", c - 1)))
                h4 = hbuf[:, :, :].rearrange("p a (b t) -> p a b t", b=NB)
                nc.vector.tensor_copy(h4[:, :, :, 0], chan_s[:, V_CLS:V_CLS + 2].unsqueeze(2).broadcast_to([HD, 2, NB])
                                      ).then_inc(h_ready, 1)
                dve.wait_ge(ring1_made, ring1.made(("embed", c)))
                for half in range(2):
                    src = r1[0:HD, half, 0:PC].rearrange("p (b t) -> p b t", b=NB)
                    last = tt(h4[:, half, :, 1:T], src, posb[:, half, :].unsqueeze(1).broadcast_to([HD, NB, NPT]), ALU.add)
                last.then_inc(h_ready, 1)

            def centre(c):
                dve.wait_ge(ring1_made, ring1.made(("mean", c)))
                dve.wait_ge(h_ready, 2 * c + 2)
                if c > 0:
                    dve.wait_ge(sq_ready, c)
                    dve.wait_ge(xn_ready, c)
                tt(xc[:, :, :], hbuf[:, :, :], r1[0:HD, 0:1, 0:TC].broadcast_to([HD, 2, TC]), ALU.subtract
                   ).then_inc(xc_ready, 1)

            def normalised(c):
                dve.wait_ge(rstd_ready, c + 1)
                dve.wait_ge(memset_done, 1)
                if c > 1:
                    dve.wait_ge(xs_ready, mix_count(c - 2, 4))
                dst = xpad[:, c % 2].rearrange("p a b t -> p (a b) t")[:, :, 1:T + 1]
                for half in range(2):
                    last = tt(dst[:, NB * half:NB * (half + 1)], xc[:, half, :].rearrange("p (b t) -> p b t", t=T),
                              rstd[:, :].rearrange("p (b t) -> p b t", t=T), ALU.mult)
                last.then_inc(xn_ready, 1)

            def difference(c):
                dve.wait_ge(nbr_ready, c + 1)
                x = xpad[:, c % 2].rearrange("p a b t -> p (a b) t")[:, :, 1:T + 1]
                d = token_view(dx[:, c % 2])
                stt(out=d, in0=d, scalar=0.5, in1=x, op0=ALU.mult, op1=ALU.subtract).then_inc(dx_ready, 1)
                dve.wait_ge(dx_ready, c + 1)
                if c > 0:
                    dve.wait_ge(ring1_made, ring1.made(("w1", c - 1)))
                for half in range(2):
                    b = slice(NB * half, NB * (half + 1))
                    last = stt(out=xxx[:, half, :].rearrange("p (b t) -> p b t", t=T), in0=d[:, b],
                               scalar=chan_s[:, V_MAA + half:V_MAA + half + 1], in1=x[:, b], op0=ALU.mult, op1=ALU.add)
                last.then_inc(xxx_ready, 1)

            def product(c, n):
                key, m = ("mix", c, n), MIXES[n]
                dve.wait_ge(ring2_made, ring2.made(key))
                count = mix_count(c, n)
                if count > 2:
                    dve.wait_ge(xs_ready, count - 2)
                for half in range(2):
                    col = V_MAA + 2 * (m + 1) + half
                    last = stt(out=prod[:, (count - 1) % 2, half, :], in0=slot2(key)[0:HD, half, 0:TC],
                               scalar=chan_s[:, col:col + 1], in1=dx[:, c % 2, half, :], op0=ALU.add, op1=ALU.mult)
                last.then_inc(prod_ready, 1)

            def scan(c):
                dve.wait_ge(ew_ready, c + 1)
                if c > 0:
                    dve.wait_ge(e_ready, 4 * c)
                for half in range(2):
                    last = nc.vector.tensor_tensor_scan(cs[:, half, :], scan_s[:, :], ew[:, half, :], 0.0, ALU.mult,
                                                        ALU.subtract)
                last.then_inc(cs_ready, 1)

            def clip(c):
                for n, x in enumerate((ew, cs)):
                    dve.wait_ge(cdiff_ready, 3 * c + 2 + n)
                    ts(x[:, :, :], x[:, :, :], -60.0, 60.0, ALU.max, ALU.min).then_inc(clip_ready, 1)

            def gated(c):
                dve.wait_ge(th_ready, c + 1)
                stt(out=gate[:, :, :], in0=th[:, :, :], scalar=1.0, in1=slot2(("g", c))[0:HD, :, 0:TC], op0=ALU.add,
                    op1=ALU.mult).then_inc(gate_ready, 1)

            def backward_half(i, c, p, slot):
                for q in range(Q):
                    if c is not None:
                        key = ("heads", c, p, q)
                        dve.wait_ge(f_ready, heads_count(c, p, q))
                        s = aux.slot(key)
                        nc.vector.copy_predicated(
                            at[:, p, :].rearrange("p (a h t) -> p a h t", a=2, t=T)[:, :, 2 * q:2 * q + 2, :],
                            tri_s[:, :].unsqueeze(1).unsqueeze(1).broadcast_to([128, 2, 2, T]),
                            bank[3][:, 512 * s + 8 * T:512 * s + 12 * T].rearrange("p (a h t) -> p a h t", a=2, t=T)
                            ).then_inc(at_ready, 1)
                    solve(i, slot + q)

            def diagonal(g):
                flat = sysm[:, g % 2].rearrange("p b i j -> p b (i j)")
                return flat[:, :, 0:(T - 1) * (W + 1) + 1:W + 1]

            def norm_squares(g):
                dve.wait_ge(sys_filled, NFILL * (g + 1))
                if g > 0:
                    dve.wait_ge(prep_dve, 5 * g)
                ts(nrm[:, :, :], diagonal(g), 1e-24, None, ALU.max).then_inc(prep_dve, 1)

            def similarities(g):
                m = sysm[:, g % 2, :, :, 0:T]
                dve.wait_ge(prep_act, 3 * g + 2)
                rows = nrm[:, :, :].unsqueeze(3).broadcast_to([NSYS, 2, T, T])
                cols = nrm[:, :, :].unsqueeze(2).broadcast_to([NSYS, 2, T, T])
                tt(m, m, rows, ALU.mult).then_inc(prep_dve, 1)
                dve.wait_ge(prep_dve, 5 * g + 2)
                tt(m, m, cols, ALU.mult).then_inc(prep_dve, 1)

            def bound(g):
                m = sysm[:, g % 2, :, :, 0:T]
                dve.wait_ge(prep_act, 3 * g + 3)
                ts(m, m, float(np.exp(-20.0)), float(np.exp(20.0)), ALU.max, ALU.min).then_inc(prep_dve, 1)
                dve.wait_ge(prep_dve, 5 * g + 4)
                ts(diagonal(g), diagonal(g), 1.0, None, ALU.add).then_inc(prep_dve, 1)
                dve.wait_ge(prep_dve, 5 * g + 5)

            def eliminate(g, first, end):
                m, rd, n0, c = sysm[:, g % 2], rdiag[:, g % 2], dve_at[g], DVE_COLS[g]
                at, v = STEP_AT[g], m[:, :, :, T:T + c]

                def after(k, kind, band=0):
                    dve.wait_ge(dve_step, n0 + at[k, kind, band] + 1)

                for k, kind, band in DVE_STEPS[g][first:end]:
                    rest = T - 1 - k
                    if kind == "recip":
                        if k > 0:
                            after(k - 1, "subtract")
                        nc.vector.reciprocal(rd[:, :, k:k + 1], m[:, :, k, k:k + 1]).then_inc(dve_step, 1)
                    elif kind == "scale":
                        after(k, "recip")
                        tt(m[:, :, k + 1:T, k], m[:, :, k, k + 1:T], rd[:, :, k:k + 1].broadcast_to([NSYS, 2, rest]),
                           ALU.mult).then_inc(dve_step, 1)
                    elif kind == "rows":
                        after(T - 1, "recip")
                        tt(v, v, rd.unsqueeze(3).broadcast_to([NSYS, 2, T, c]), ALU.mult).then_inc(dve_step, 1)
                    elif kind in ("back_outer", "back_subtract"):
                        o = outer[:, 0:2 * k * c].rearrange("p (b i c) -> p b i c", b=2, c=c)
                        if kind == "back_outer":
                            after(*((k + 1, "back_subtract") if k < T - 1 else (T, "rows")))
                            tt(o, m[:, :, k, 0:k].unsqueeze(3).broadcast_to([NSYS, 2, k, c]),
                               v[:, :, k].unsqueeze(2).broadcast_to([NSYS, 2, k, c]), ALU.mult).then_inc(dve_step, 1)
                        else:
                            after(k, "back_outer")
                            tt(v[:, :, 0:k], v[:, :, 0:k], o, ALU.subtract).then_inc(dve_step, 1)
                    else:
                        end_ = T + c
                        used = sum(2 * (b1 - b0) * (end_ - k - 1 - b0) for b0, b1 in bands(rest)[:band])
                        r0, r1_ = bands(rest)[band]
                        rows, cols = r1_ - r0, end_ - (k + 1 + r0)
                        o = outer[:, used:used + 2 * rows * cols].rearrange("p (b i j) -> p b i j", b=2, j=cols)
                        if kind == "outer":
                            after(k, "scale")
                            tt(o, m[:, :, k + 1 + r0:k + 1 + r1_, k].unsqueeze(3).broadcast_to([NSYS, 2, rows, cols]),
                               m[:, :, k, k + 1 + r0:end_].unsqueeze(2).broadcast_to([NSYS, 2, rows, cols]), ALU.mult
                               ).then_inc(dve_step, 1)
                        else:
                            after(k, "outer", band)
                            a_ = m[:, :, k + 1 + r0:k + 1 + r1_, k + 1 + r0:end_]
                            tt(a_, a_, o, ALU.subtract).then_inc(dve_step, 1)

            def solve(i, slot):
                for g, first, end in dve_parts.get(SLOTS * i + slot, ()):
                    if first == 0:
                        bound(g)
                    eliminate(g, first, end)

            for i in range(NC + 2):
                c1, c2, c3 = iteration(i)
                if c1 is not None:
                    embedded(c1)
                    if c1 == 0:
                        dve.wait_ge(w_loaded, 16 * 12)
                        ts(wo_s[0:HD], wo_s[0:HD], 0.5, None, ALU.mult).then_inc(prep_done, 1)
                        dve.wait_ge(temp_act, 3)
                        ts(lucid_s[:, :], lucid_s[:, :], 0.0, None, ALU.max).then_inc(prep_done, 1)
                        dve.wait_ge(prep_done, 4)
                        tt(temp[:, :], lucid_s[:, :], tmp3[:, 0, :], ALU.add).then_inc(temp_ready, 1)
                if c2 is not None:
                    product(c2, 0)
                    product(c2, 1)
                solve(i, 0)
                backward_half(i, c3, 0, 1)
                backward_half(i, c3, 1, 4)
                if c1 is not None:
                    centre(c1)
                solve(i, 7)
                if c2 is not None:
                    product(c2, 2)
                solve(i, 8)
                if c1 is not None:
                    normalised(c1)
                solve(i, 9)
                if c2 is not None:
                    product(c2, 3)
                solve(i, 10)
                if c1 is not None:
                    difference(c1)
                solve(i, 11)
                if c2 is not None:
                    scan(c2)
                backward_half(i, c3, 2, 12)
                backward_half(i, c3, 3, 15)
                if c2 is not None:
                    gated(c2)
                    product(c2, 4)
                solve(i, 18)
                g = None if c3 is None else completed(c3)
                if g in (0, 1):
                    norm_squares(g)
                if c2 is not None:
                    clip(c2)
                solve(i, 19)
                if g in (0, 1):
                    similarities(g)
                solve(i, 20)

            c1p, c2p = pair_of(1), (pair_of(0), pair_of(2), pair_of(3))
            solve(BETWEEN, 0)
            phase_a_over(dve)
            dve.wait_ge(aux_made, aux.made(("fill", NG - 1, NFILL - 1)))
            for x in (yT_k, sqc_k, z_k, sq2_k, wfc_s, h1_k, hn_k):
                last = nc.vector.memset(x[HD:128], 0.0)
            last.then_inc(rows_zeroed, 1)
            dve.wait_ge(ffnw_loaded, 16 * 7)
            tt(aij[:, :], alph_s[:, 0:1], alph_s[:, 1:2], ALU.mult).then_inc(prep_done, 1)
            dve.wait_ge(prep_done, 5)
            ts(adin[:, :], din_s[:, :], aij[:, 0:1], None, ALU.mult).then_inc(ffn_prep, 1)
            for slot in range(1, SLOTS):
                solve(BETWEEN, slot)

            def mix_coefficients(part):
                dve.wait_ge(ffn_made, part + 1)
                if part == 0:
                    for half in range(2):
                        w = wfc_s[0:HD, half, :].rearrange("p (n f) -> p n f", n=2)
                        tt(w, w, c2p[half][0:HD, :, 0:FH // 2], ALU.mult)
                    tt(wpr_s[:, 0:2, :], wpr_s[:, 0:2, :], c2p[2][:, :, 0:D], ALU.mult).then_inc(ffn_prep, 1)
                else:
                    for j in range(2):
                        w = wpr_s[:, 2 + 2 * j:4 + 2 * j, :]
                        tt(w, w, c2p[j][:, :, 0:D], ALU.mult)
                    tt(bfc_s[:, :], bfc_s[:, :], c2p[2][:, 0, 0:FC], ALU.mult)
                    tt(bpr_s[:, :], bpr_s[:, :], c2p[2][0:1, 1, 0:D], ALU.mult).then_inc(ffn_prep, 1)

            def centre_y(c):
                dve.wait_ge(c1_made, ringc1.made(("gmean", c)))
                if c > 0:
                    dve.wait_ge(z_ready, c)
                dve.wait_ge(yT_ready, c + 1)
                tt(yc[:, :, :], yT[:, :, :], c1p[0:HD, :, 0:TC], ALU.subtract).then_inc(yc_ready, 1)

            def normalise_y(c):
                dve.wait_ge(rsc_ready, c + 1)
                tt(yc[:, :, :], yc[:, :, :], rsc[:, :, :], ALU.mult).then_inc(yn_ready, 1)

            def residual(c):
                dve.wait_ge(c2_made, ringc2.made(("wo", c)))
                dve.wait_ge(hin_loaded, 16 * (c + 1))
                if c > 1:
                    dve.wait_ge(c2_made, ringc2.made(("proj", c - 2)))
                tt(h1[:, c % 2], hin[:, :, :], c2p[ringc2.slot(("wo", c))][0:HD, :, 0:TC], ALU.add).then_inc(h1_ready, 1)

            def centre_h(c):
                dve.wait_ge(c2_made, ringc2.made(("lmean", c)))
                if c > 0:
                    dve.wait_ge(sq2_ready, c)
                dve.wait_ge(h1_ready, c + 1)
                tt(hc[:, :, :], h1[:, c % 2], c2p[ringc2.slot(("lmean", c))][0:HD, 0:1, 0:TC].broadcast_to([HD, 2, TC]),
                   ALU.subtract).then_inc(hc_ready, 1)

            def normalise_h(c):
                dve.wait_ge(rs2_ready, c + 1)
                if c > 1:
                    dve.wait_ge(c2_made, ringc2.made(("fc", c - 2, FC // 2 - 1)))
                tt(hn[:, c % 2], hc[:, :, :], rs2[:, :].unsqueeze(1).broadcast_to([HD, 2, TC]), ALU.mult
                   ).then_inc(hn_ready, 1)

            def copy_out(c):
                dve.wait_ge(c2_made, ringc2.made(("proj", c)))
                if c > 0:
                    dve.wait_ge(out_stored, 16 * 3 * c)
                src = c2p[ringc2.slot(("proj", c))]
                for n, _, nt in tokens(c):
                    last = nc.vector.tensor_copy(osb[0:nt, n, :], src[0:nt, n // 2, D * (n % 2):D * (n % 2 + 1)])
                last.then_inc(osb_ready, 1)

            for i in range(NC + 2):
                d1, d2, d3 = c_iteration(i)

                def steps(slot):
                    for n in range(SLOTS * slot // 6, SLOTS * (slot + 1) // 6):
                        solve(C_FIRST + i, n)
                if i == 0:
                    norm_squares(NG - 1)
                steps(0)
                if d2 is not None:
                    residual(d2)
                steps(1)
                if d2 is not None:
                    centre_h(d2)
                steps(2)
                if d1 is not None:
                    centre_y(d1)
                if d1 == 0:
                    similarities(NG - 1)
                    mix_coefficients(0)
                steps(3)
                if d2 is not None:
                    normalise_h(d2)
                steps(4)
                if d1 is not None:
                    normalise_y(d1)
                if d1 == 0:
                    mix_coefficients(1)
                steps(5)
                if d3 is not None:
                    copy_out(d3)


def kernel(**inputs):
    import concourse.bacc as bacc
    from concourse.bass_utils import run_bass_kernel_spmd as run

    a = {k: np.asarray(v) for k, v in inputs.items()}

    def halves(v):
        v = v.reshape(v.shape[:-1] + (2, HD))
        return np.moveaxis(v, -1, 0)

    def rows(w):
        return w.reshape(2, HD, -1).transpose(1, 0, 2)

    x = a["x"].reshape(B, CH, HP, PATCH, HP, PATCH).transpose(0, 2, 4, 1, 3, 5)
    maa = np.stack([a["L0_attn_time_maa_" + n].reshape(D) for n in "xwkvrg"])
    par = (np.arange(HD)[:, None] // K % 2 == np.arange(2)[None, :]).astype(np.float32)
    chan = np.concatenate([
        halves(a["L0_tok_b"]), halves(a["cls_tok"].reshape(D)), halves(maa).reshape(HD, 12),
        halves(a["L0_attn_time_decay"].reshape(D)), halves(a["L0_attn_ln_w"]), halves(a["L0_attn_ln_b"]), par,
        halves(a["L0_tok_pos"].reshape(NPT, D)).transpose(0, 2, 1).reshape(HD, 2 * NPT)], axis=1)
    heads = np.arange(HD) // K
    p = np.arange(128)
    w2 = a["L0_attn_maa_w2"]
    token = np.arange(TC) % T
    arrays = {
        "patches": x.reshape(NC, PC, FK, 128).transpose(0, 3, 2, 1),
        "chan": chan,
        "wtok": a["L0_tok_W"].T.reshape(FK, 128, D).transpose(1, 0, 2),
        "w1": rows(a["L0_attn_maa_w1"]),
        "w2a": w2[0:4].reshape(128, D), "w2b": w2[4],
        "dw1": rows(a["L0_attn_decay_w1"]), "dw2": a["L0_attn_decay_w2"],
        "wkvrg": np.stack([rows(a["L0_attn_W" + n]) for n in "kvrg"], axis=1),
        "wo": rows(a["L0_attn_Wo"]),
        "wfc": rows(a["L0_ffn_w_fc"].T), "bfc": a["L0_ffn_b_fc"].reshape(FC, 128).T,
        "wproj": a["L0_ffn_w_proj"].T.reshape(FC, 128, D).transpose(1, 0, 2), "bproj": a["L0_ffn_b_proj"].reshape(1, D),
        "alphas": np.stack([np.repeat(a["L0_ffn_alpha_e"], len(RATIOS)), np.tile(a["L0_ffn_alpha_r"], len(EMBEDS))], axis=1),
        "lucid": np.tile(a["L0_attn_lucid_temp"].reshape(H), B // 2).reshape(NG, NSYS).T,
        "ident": np.eye(128, dtype=np.float32),
        "blocks": np.stack([np.full((HD, HD), 1.0 / D), (heads[:, None] == heads[None, :]) / K], axis=1).astype(np.float32),
        "tri": (np.arange(T)[None, :] < p[:, None] % TP).astype(np.uint32),
        "scanmask": np.broadcast_to((token > 0).astype(np.float32), (HD, TC)),
        "din": np.array([[d < e for d in range(D)] for e in EMBEDS for _ in RATIOS], np.float32),
        "hout": np.array([[f < r * e for f in range(FH)] for e in EMBEDS for r in RATIOS], np.float32),
    }
    arrays = {k: np.ascontiguousarray(v) for k, v in arrays.items()}
    nc = bacc.Bacc("TRN2", target_bir_lowering=False, num_devices=1)
    aps = {k: nc.dram_tensor(f"in_{k}", v.shape, mybir.dt.from_np(v.dtype), kind="ExternalInput").ap()
           for k, v in arrays.items()}
    o = nc.dram_tensor("out_0", (B, T, D), F32, kind="ExternalOutput").ap()
    vit_tower(nc, **aps, out=o.rearrange("b t d -> (b t) d"))
    r = run(nc, [{f"in_{k}": v for k, v in arrays.items()}], core_ids=[0])
    return r.results[0]["out_0"]
```
